# Optimizing a Trainium2 kernel written in Bass

```python
import numpy as np
import jax
import jax.numpy as jnp

def _softmax(x, axis=-1):
    return jax.nn.softmax(x, axis=axis)

def _gelu(x):
    return jax.nn.gelu(x, approximate=True)

def _silu(x):
    return jax.nn.silu(x)

def _sigmoid(x):
    return jax.nn.sigmoid(x)

def _layernorm(x, axis=-1, eps=1e-05):
    m = jnp.mean(x, axis=axis, keepdims=True)
    v = jnp.var(x, axis=axis, keepdims=True)
    return (x - m) / jnp.sqrt(v + eps)

def _scatter_add(tgt, idx, src, axis=0):
    return tgt.at[idx].add(src)

def _segment_sum(src, seg, n):
    return jax.ops.segment_sum(src, seg, n)
kernel_name = 'mk_macaron_d1_jaxref_r8_490620'

def setup_inputs(seed: int=0):
    np.random.seed(seed)
    _w = jnp.asarray

    def _L0_attn_setup():
        import jax, jax.numpy as jnp
        import numpy as np
        EPS_RMS = 1e-06
        EPS_LN = 1e-05
        ETA_MIN = 1e-06
        B, T, D, F = (8, 64, 128, 64)

        def _rmsnorm(x, w):
            return x * jax.lax.rsqrt(jnp.mean(x * x, axis=-1, keepdims=True) + EPS_RMS) * w

        def _phi(x):
            return jax.nn.elu(x) + 1.0

        def _ln2(M):
            mu = jnp.mean(M, axis=(-2, -1), keepdims=True)
            var = jnp.mean((M - mu) ** 2, axis=(-2, -1), keepdims=True)
            return (M - mu) * jax.lax.rsqrt(var + EPS_LN)

        def _reference_tuple_inner(x, norm_weight, Wk, Wv, Wq, eta, Wout):
            b, t, d = x.shape
            f = Wk.shape[0]
            x_norm = _rmsnorm(x, norm_weight)
            k = _phi(jnp.einsum('btd,fd->btf', x_norm, Wk))
            v = jnp.einsum('btd,ed->bte', x_norm, Wv)
            eta_c = jnp.maximum(jnp.abs(eta), ETA_MIN)

            def step(M, kv):
                k_t, v_t = kv
                v_pred = jnp.einsum('bf,bfd->bd', k_t, M)
                surprise = jnp.linalg.norm(v_t - v_pred, axis=-1, keepdims=True)
                delta = k_t[:, :, None] * v_t[:, None, :]
                M = M + eta_c[None, :, None] * surprise[:, :, None] * delta
                return (_ln2(M), None)
            M0 = jnp.zeros((b, f, d), dtype=x.dtype)
            kT = jnp.transpose(k, (1, 0, 2))
            vT = jnp.transpose(v, (1, 0, 2))
            M, _ = jax.lax.scan(step, M0, (kT, vT))
            q = _phi(jnp.einsum('btd,fd->btf', x_norm, Wq))
            mem_out = jnp.einsum('btf,bfd->btd', q, M)
            out = jnp.einsum('btd,ed->bte', mem_out, Wout)
            output = x + out
            return (output, M)
        key = jax.random.key(seed)
        ks = jax.random.split(key, 5)
        x = jax.random.normal(ks[0], (B, T, D), dtype=jnp.float32)
        norm_weight = jnp.ones((D,), dtype=jnp.float32)
        Wk = jax.random.normal(ks[1], (F, D), dtype=jnp.float32) * 0.02
        Wv = jax.random.normal(ks[2], (D, D), dtype=jnp.float32) * 0.02
        Wq = jax.random.normal(ks[3], (F, D), dtype=jnp.float32) * 0.02
        Wout = jax.random.normal(ks[4], (D, D), dtype=jnp.float32) * 0.02
        eta = jnp.ones((F,), dtype=jnp.float32) * 0.01
        return {'x': x, 'norm_weight': norm_weight, 'Wk': Wk, 'Wv': Wv, 'Wq': Wq, 'eta': eta, 'Wout': Wout}
    _L0_attn_in = _L0_attn_setup()

    def _L0_ffn_setup():
        import jax, jax.numpy as jnp
        import numpy as np
        DIM = 128
        DEPTH = 6
        HEADS = 16
        DIM_HEAD = 64
        WINDOW = 32
        INNER = HEADS * DIM_HEAD
        DIM_INNER = int(DIM * 4 * 2 / 3)
        QK_SCALE = 8.0

        def shift_tokens(t):
            a, s = jnp.split(t, 2, -1)
            s = jnp.pad(s, ((0, 0), (1, 0), (0, 0)))[:, :-1]
            return jnp.concatenate([a, s], -1)

        def l2norm(t):
            return t / jnp.maximum(jnp.linalg.norm(t, axis=-1, keepdims=True), 1e-12)

        def rotate_half(x):
            x1, x2 = jnp.split(x, 2, -1)
            return jnp.concatenate([-x2, x1], -1)

        def rotary_tables(n):
            half = jnp.arange(0, DIM_HEAD, 2, dtype=jnp.float32)
            inv_freq = 1.0 / 10000.0 ** (half / DIM_HEAD)
            t = jnp.arange(n, dtype=jnp.float32)
            freqs = t[:, None] * inv_freq[None, :]
            freqs = jnp.concatenate([freqs, freqs], -1)
            base_scale = (half + 0.4 * DIM_HEAD) / (1.4 * DIM_HEAD)
            power = (t - n // 2) / (WINDOW // 2)
            scale = base_scale[None, :] ** power[:, None]
            scale = jnp.concatenate([scale, scale], -1)
            return (freqs, scale)

        def local_attention(q, k, v):
            b, h, n, d = q.shape
            w = WINDOW
            nw = n // w
            bq = q.reshape(b, h, nw, w, d)
            bk = k.reshape(b, h, nw, w, d)
            bv = v.reshape(b, h, nw, w, d)

            def look(t):
                p = jnp.pad(t, ((0, 0), (0, 0), (1, 0), (0, 0), (0, 0)))
                return jnp.concatenate([p[:, :, :nw], p[:, :, 1:]], axis=3)
            bk2, bv2 = (look(bk), look(bv))
            seq = jnp.arange(n).reshape(nw, w)
            seq_p = jnp.pad(seq, ((1, 0), (0, 0)), constant_values=-1)
            jt = jnp.concatenate([seq_p[:nw], seq_p[1:]], axis=1)
            it = seq[:, :, None]
            jb = jt[:, None, :]
            mask = (it < jb) | (it > jb + w) | (jb == -1)
            sim = jnp.einsum('bhwie,bhwje->bhwij', bq, bk2) * QK_SCALE
            sim = jnp.where(mask, -jnp.finfo(sim.dtype).max, sim)
            attn = jax.nn.softmax(sim, -1)
            out = jnp.einsum('bhwij,bhwje->bhwie', attn, bv2)
            return out.reshape(b, h, n, d)

        def attn_layer(x, Wqkv, qs, ksc, Wo):
            b, n, _ = x.shape
            qkv = x @ Wqkv
            q, k, v = jnp.split(qkv, 3, -1)
            sh = lambda t: t.reshape(b, n, HEADS, DIM_HEAD).transpose(0, 2, 1, 3)
            q, k, v = (sh(q), sh(k), sh(v))
            q = l2norm(q) * qs
            k = l2norm(k) * ksc
            freqs, scale = rotary_tables(n)
            cos, sin = (jnp.cos(freqs), jnp.sin(freqs))
            q = q * cos * scale + rotate_half(q) * sin * scale
            inv = 1.0 / scale
            k = k * cos * inv + rotate_half(k) * sin * inv
            out = local_attention(q, k, v)
            out = out.transpose(0, 2, 1, 3).reshape(b, n, INNER)
            return out @ Wo

        def ffn_layer(x, g, bln, W1, b1, W2, b2):
            mu = x.mean(-1, keepdims=True)
            var = ((x - mu) ** 2).mean(-1, keepdims=True)
            xn = (x - mu) / jnp.sqrt(var + 1e-05) * g + bln
            hg = xn @ W1 + b1
            a, gate = jnp.split(hg, 2, -1)
            return a * jax.nn.gelu(gate, approximate=False) @ W2 + b2
        key = jax.random.key(seed)
        ks = jax.random.split(key, 8)
        B, N = (2, 256)
        init = lambda k, shape: jax.random.normal(k, shape, jnp.float32) * 0.02
        return {'x': jax.random.normal(ks[0], (B, N, DIM), jnp.float32), 'Wqkv': init(ks[1], (DEPTH, DIM, 3 * INNER)), 'q_scale': jnp.ones((DEPTH, DIM_HEAD), jnp.float32), 'k_scale': jnp.ones((DEPTH, DIM_HEAD), jnp.float32), 'Wo': init(ks[2], (DEPTH, INNER, DIM)), 'ln_g': jnp.ones((DEPTH, DIM), jnp.float32), 'ln_b': jnp.zeros((DEPTH, DIM), jnp.float32), 'W1': init(ks[3], (DEPTH, DIM, 2 * DIM_INNER)), 'b1': jnp.zeros((DEPTH, 2 * DIM_INNER), jnp.float32), 'W2': init(ks[4], (DEPTH, DIM_INNER, DIM)), 'b2': jnp.zeros((DEPTH, DIM), jnp.float32)}
    _L0_ffn_in = _L0_ffn_setup()
    _d = {'L0_attn_x': _L0_attn_in['x'], 'L0_attn_norm_weight': _L0_attn_in['norm_weight'], 'L0_attn_Wk': _L0_attn_in['Wk'], 'L0_attn_Wv': _L0_attn_in['Wv'], 'L0_attn_Wq': _L0_attn_in['Wq'], 'L0_attn_eta': _L0_attn_in['eta'], 'L0_attn_Wout': _L0_attn_in['Wout'], 'L0_ffn_Wqkv': _L0_ffn_in['Wqkv'], 'L0_ffn_q_scale': _L0_ffn_in['q_scale'], 'L0_ffn_k_scale': _L0_ffn_in['k_scale'], 'L0_ffn_Wo': _L0_ffn_in['Wo'], 'L0_ffn_ln_g': _L0_ffn_in['ln_g'], 'L0_ffn_ln_b': _L0_ffn_in['ln_b'], 'L0_ffn_W1': _L0_ffn_in['W1'], 'L0_ffn_b1': _L0_ffn_in['b1'], 'L0_ffn_W2': _L0_ffn_in['W2'], 'L0_ffn_b2': _L0_ffn_in['b2']}
    _x0 = _d['L0_attn_x']
    _d['L0_attn_x'] = jax.random.normal(jax.random.fold_in(jax.random.key(seed), 1), (8, 256, 128), dtype=_x0.dtype)
    del _x0
    return _d

def reference(L0_attn_x, L0_attn_norm_weight, L0_attn_Wk, L0_attn_Wv, L0_attn_Wq, L0_attn_eta, L0_attn_Wout, L0_ffn_Wqkv, L0_ffn_q_scale, L0_ffn_k_scale, L0_ffn_Wo, L0_ffn_ln_g, L0_ffn_ln_b, L0_ffn_W1, L0_ffn_b1, L0_ffn_W2, L0_ffn_b2):

    def _L0_attn_ref(x, norm_weight, Wk, Wv, Wq, eta, Wout):
        import jax, jax.numpy as jnp
        import numpy as np
        EPS_RMS = 1e-06
        EPS_LN = 1e-05
        ETA_MIN = 1e-06
        B, T, D, F = (8, 64, 128, 64)

        def _rmsnorm(x, w):
            return x * jax.lax.rsqrt(jnp.mean(x * x, axis=-1, keepdims=True) + EPS_RMS) * w

        def _phi(x):
            return jax.nn.elu(x) + 1.0

        def _ln2(M):
            mu = jnp.mean(M, axis=(-2, -1), keepdims=True)
            var = jnp.mean((M - mu) ** 2, axis=(-2, -1), keepdims=True)
            return (M - mu) * jax.lax.rsqrt(var + EPS_LN)

        def _reference_tuple_inner(x, norm_weight, Wk, Wv, Wq, eta, Wout):
            b, t, d = x.shape
            f = Wk.shape[0]
            x_norm = _rmsnorm(x, norm_weight)
            k = _phi(jnp.einsum('btd,fd->btf', x_norm, Wk))
            v = jnp.einsum('btd,ed->bte', x_norm, Wv)
            eta_c = jnp.maximum(jnp.abs(eta), ETA_MIN)

            def step(M, kv):
                k_t, v_t = kv
                v_pred = jnp.einsum('bf,bfd->bd', k_t, M)
                surprise = jnp.linalg.norm(v_t - v_pred, axis=-1, keepdims=True)
                delta = k_t[:, :, None] * v_t[:, None, :]
                M = M + eta_c[None, :, None] * surprise[:, :, None] * delta
                return (_ln2(M), None)
            M0 = jnp.zeros((b, f, d), dtype=x.dtype)
            kT = jnp.transpose(k, (1, 0, 2))
            vT = jnp.transpose(v, (1, 0, 2))
            M, _ = jax.lax.scan(step, M0, (kT, vT))
            q = _phi(jnp.einsum('btd,fd->btf', x_norm, Wq))
            mem_out = jnp.einsum('btf,bfd->btd', q, M)
            out = jnp.einsum('btd,ed->bte', mem_out, Wout)
            output = x + out
            return (output, M)
        return _reference_tuple_inner(x, norm_weight, Wk, Wv, Wq, eta, Wout)[0]

    def _L0_ffn_ref(x, Wqkv, q_scale, k_scale, Wo, ln_g, ln_b, W1, b1, W2, b2):
        import jax, jax.numpy as jnp
        import numpy as np
        DIM = 128
        DEPTH = 6
        HEADS = 16
        DIM_HEAD = 64
        WINDOW = 32
        INNER = HEADS * DIM_HEAD
        DIM_INNER = int(DIM * 4 * 2 / 3)
        QK_SCALE = 8.0

        def shift_tokens(t):
            a, s = jnp.split(t, 2, -1)
            s = jnp.pad(s, ((0, 0), (1, 0), (0, 0)))[:, :-1]
            return jnp.concatenate([a, s], -1)

        def l2norm(t):
            return t / jnp.maximum(jnp.linalg.norm(t, axis=-1, keepdims=True), 1e-12)

        def rotate_half(x):
            x1, x2 = jnp.split(x, 2, -1)
            return jnp.concatenate([-x2, x1], -1)

        def rotary_tables(n):
            half = jnp.arange(0, DIM_HEAD, 2, dtype=jnp.float32)
            inv_freq = 1.0 / 10000.0 ** (half / DIM_HEAD)
            t = jnp.arange(n, dtype=jnp.float32)
            freqs = t[:, None] * inv_freq[None, :]
            freqs = jnp.concatenate([freqs, freqs], -1)
            base_scale = (half + 0.4 * DIM_HEAD) / (1.4 * DIM_HEAD)
            power = (t - n // 2) / (WINDOW // 2)
            scale = base_scale[None, :] ** power[:, None]
            scale = jnp.concatenate([scale, scale], -1)
            return (freqs, scale)

        def local_attention(q, k, v):
            b, h, n, d = q.shape
            w = WINDOW
            nw = n // w
            bq = q.reshape(b, h, nw, w, d)
            bk = k.reshape(b, h, nw, w, d)
            bv = v.reshape(b, h, nw, w, d)

            def look(t):
                p = jnp.pad(t, ((0, 0), (0, 0), (1, 0), (0, 0), (0, 0)))
                return jnp.concatenate([p[:, :, :nw], p[:, :, 1:]], axis=3)
            bk2, bv2 = (look(bk), look(bv))
            seq = jnp.arange(n).reshape(nw, w)
            seq_p = jnp.pad(seq, ((1, 0), (0, 0)), constant_values=-1)
            jt = jnp.concatenate([seq_p[:nw], seq_p[1:]], axis=1)
            it = seq[:, :, None]
            jb = jt[:, None, :]
            mask = (it < jb) | (it > jb + w) | (jb == -1)
            sim = jnp.einsum('bhwie,bhwje->bhwij', bq, bk2) * QK_SCALE
            sim = jnp.where(mask, -jnp.finfo(sim.dtype).max, sim)
            attn = jax.nn.softmax(sim, -1)
            out = jnp.einsum('bhwij,bhwje->bhwie', attn, bv2)
            return out.reshape(b, h, n, d)

        def attn_layer(x, Wqkv, qs, ksc, Wo):
            b, n, _ = x.shape
            qkv = x @ Wqkv
            q, k, v = jnp.split(qkv, 3, -1)
            sh = lambda t: t.reshape(b, n, HEADS, DIM_HEAD).transpose(0, 2, 1, 3)
            q, k, v = (sh(q), sh(k), sh(v))
            q = l2norm(q) * qs
            k = l2norm(k) * ksc
            freqs, scale = rotary_tables(n)
            cos, sin = (jnp.cos(freqs), jnp.sin(freqs))
            q = q * cos * scale + rotate_half(q) * sin * scale
            inv = 1.0 / scale
            k = k * cos * inv + rotate_half(k) * sin * inv
            out = local_attention(q, k, v)
            out = out.transpose(0, 2, 1, 3).reshape(b, n, INNER)
            return out @ Wo

        def ffn_layer(x, g, bln, W1, b1, W2, b2):
            mu = x.mean(-1, keepdims=True)
            var = ((x - mu) ** 2).mean(-1, keepdims=True)
            xn = (x - mu) / jnp.sqrt(var + 1e-05) * g + bln
            hg = xn @ W1 + b1
            a, gate = jnp.split(hg, 2, -1)
            return a * jax.nn.gelu(gate, approximate=False) @ W2 + b2
        for i in range(DEPTH):
            x = attn_layer(shift_tokens(x), Wqkv[i], q_scale[i], k_scale[i], Wo[i]) + x
            x = ffn_layer(shift_tokens(x), ln_g[i], ln_b[i], W1[i], b1[i], W2[i], b2[i]) + x
        return x
    x = L0_attn_x
    x = x + 0.5 * _L0_ffn_ref(_layernorm(x, axis=-1), L0_ffn_Wqkv, L0_ffn_q_scale, L0_ffn_k_scale, L0_ffn_Wo, L0_ffn_ln_g, L0_ffn_ln_b, L0_ffn_W1, L0_ffn_b1, L0_ffn_W2, L0_ffn_b2)
    x = x + _L0_attn_ref(_layernorm(x, axis=-1), L0_attn_norm_weight, L0_attn_Wk, L0_attn_Wv, L0_attn_Wq, L0_attn_eta, L0_attn_Wout)
    x = x + 0.5 * _L0_ffn_ref(_layernorm(x, axis=-1), L0_ffn_Wqkv, L0_ffn_q_scale, L0_ffn_k_scale, L0_ffn_Wo, L0_ffn_ln_g, L0_ffn_ln_b, L0_ffn_W1, L0_ffn_b1, L0_ffn_W2, L0_ffn_b2)
    return x

_drawn_inputs = setup_inputs


def setup_inputs(seed=0):
    import zlib

    import numpy as np

    out = dict(_drawn_inputs(seed))
    spreads = {'L0_attn_norm_weight': (1.0, 0.2),
     'L0_attn_eta': (0.009999999776482582, 0.6),
     'L0_ffn_q_scale': (1.0, 0.6),
     'L0_ffn_k_scale': (1.0, 0.6),
     'L0_ffn_ln_g': (1.0, 0.6),
     'L0_ffn_ln_b': (0.0, 0.8),
     'L0_ffn_b1': (0.0, 0.8),
     'L0_ffn_b2': (0.0, 0.1)}
    factors = {'L0_ffn_W1': 5.413, 'L0_ffn_W2': 4.898, 'L0_attn_Wq': 2.931}
    for name, (base, spread) in spreads.items():
        noise = np.random.default_rng([zlib.crc32(name.encode()), seed]).standard_normal(out[name].shape)
        drawn = base * np.exp(spread * noise) if base else spread * noise
        out[name] = jnp.asarray(drawn.astype(out[name].dtype))
    for name, factor in factors.items():
        out[name] = (out[name] * factor).astype(out[name].dtype)
    return out
```

```python
from contextlib import ExitStack

import numpy as np

import concourse.bass as bass
from concourse import mybir
from concourse.alu_op_type import AluOpType as ALU

ACT = mybir.ActivationFunctionType
AX = mybir.AxisListType
F32 = mybir.dt.float32
F32R = mybir.dt.float32r
BF16 = mybir.dt.bfloat16

BATCH, SEQ, DIM = 8, 256, 128
LAYERS, HEADS, HEAD_DIM, WINDOW = 6, 16, 64, 32
INNER = HEADS * HEAD_DIM
PAIRS = HEADS // 2
UNITS = PAIRS // 2
FFN = int(DIM * 4 * 2 / 3)
CHUNKS = [(0, 128), (128, 128), (256, FFN - 256)]
TOKENS = BATCH * SEQ
WINDOWS = SEQ // WINDOW
PAD = WINDOW
VW = HEAD_DIM + 1
MASKED = -1e30
NORM_FLOOR = 1e-24
LN_SHIFT = 2.0 ** 20
SMALLS = 13
EPS = 1e-5


def tables():
    half = np.arange(0, HEAD_DIM, 2, dtype=np.float32)
    inv_freq = (1.0 / 10000.0 ** (half / HEAD_DIM)).astype(np.float32)
    t = np.arange(SEQ, dtype=np.float32)
    freqs = t[:, None] * inv_freq[None, :]
    freqs = np.concatenate([freqs, freqs], -1)
    base = (half + 0.4 * HEAD_DIM) / (1.4 * HEAD_DIM)
    power = (t - SEQ // 2) / (WINDOW // 2)
    scale = base[None, :] ** power[:, None]
    scale = np.concatenate([scale, scale], -1)
    sign = np.where(np.arange(HEAD_DIM) < HEAD_DIM // 2, -1.0, 1.0)
    cos, sin = np.cos(freqs), np.sin(freqs) * sign
    rot = np.stack([cos * scale, sin * scale, cos / scale, sin / scale], 0)
    rot = np.concatenate([rot, rot], 2).transpose(2, 0, 1)
    mask = np.zeros((2, 128, 2 * WINDOW), np.float32)
    for first in range(2):
        for q in range(128):
            g, i = divmod(q, WINDOW)
            for j in range(WINDOW):
                if j < i or (first == 0 and g == 0):
                    mask[first, q, j] = MASKED
                if j > i:
                    mask[first, q, WINDOW + j] = MASKED
    mask = np.tile(mask.transpose(1, 0, 2)[:, :, None, :], (1, 1, 4, 1))
    ident = np.eye(128, dtype=np.float32)
    heads = np.zeros((128, 2, 32), np.float32)
    for a in range(2):
        for e in range(2):
            heads[64 * e:64 * e + 64, a, 2 * a + e] = 1.0
    spread = np.zeros((128, 2, 128), np.float32)
    for a in range(2):
        for e in range(2):
            spread[32 + 2 * a + e, a, 64 * e:64 * e + 64] = 1.0
    bias = np.zeros((128, 4), np.float32)
    bias[0:32, 0] = np.log(8.0 * LN_SHIFT ** 0.5)
    bias[32:64, 0] = np.log(LN_SHIFT ** 0.5)
    bias[:, 1] = EPS
    bias[:, 2] = EPS_RMS
    bias[:, 3] = 1.0
    mean = np.full((128, 128), 1.0 / DIM, np.float32)
    f = np.concatenate([rot.reshape(128, -1), ident, heads.reshape(128, -1), spread.reshape(128, -1), bias, mean], 1)
    return np.ascontiguousarray(f.astype(np.float32)), np.ascontiguousarray(mask.reshape(128, -1))


MEM = 64
STEPS = 16
STEPS1 = STEPS + 1
MEM_SIZE = MEM * DIM
EPS_RMS, ETA_MIN = 1e-6, 1e-6
MEM_COLS = 2 * MEM + 2 * DIM + 2
GRAM = 2 * STEPS1 + STEPS

ROT0, IDENT0 = 0, 4 * SEQ
HEADS0 = IDENT0 + 128
SPREAD0 = HEADS0 + 64
BIAS0 = SPREAD0 + 256
MEAN0 = BIAS0 + 4
CONST_COLS = MEAN0 + 128


class Count:

    def __init__(self, layer, stack):
        self.layer, self.stack = layer, stack

    def __call__(self, per, b, k):
        return self.layer * (per * BATCH) + (per * (BATCH * LAYERS * self.stack + b + 2) + k + 1)

    def x(self, b):
        return self.layer * BATCH + (BATCH * (LAYERS + 1) * self.stack + b + 1)


def build(nc, xT, w_qk, w_v, w_o, w_1, w_2, smalls, mem_w, consts, maskc, out, stacks=2, layers=LAYERS):
    x2 = nc.dram_tensor("x2", (DIM, TOKENS), F32, kind="Internal").ap()
    ctx = ExitStack()
    with ctx:
        def sb(name, shape, dt=F32):
            return ctx.enter_context(nc.sbuf_tensor(name, shape, dt))

        def ps(name, cols):
            return ctx.enter_context(nc.psum_tensor(name, [128, cols], F32))

        def sem(name):
            return ctx.enter_context(nc.semaphore(name))

        const = sb("const", [128, CONST_COLS])
        maskf = sb("maskf", [128, 512])
        mask = sb("mask", [128, 2, 256], BF16)
        identb = sb("identb", [128, 128], BF16)
        rot = const[:, ROT0:IDENT0].rearrange("p (k t) -> p k t", k=4)
        ident = const[:, IDENT0:HEADS0]
        head_sum = const[:, HEADS0:SPREAD0].rearrange("p (a m) -> p a m", a=2)
        spread = const[:, SPREAD0:BIAS0].rearrange("p (a m) -> p a m", a=2)
        norm_bias = const[0:64, BIAS0:BIAS0 + 1]
        eps = const[:, BIAS0 + 1:BIAS0 + 2]
        eps_rms = const[:, BIAS0 + 2:BIAS0 + 3]
        ones_col = const[:, BIAS0 + 3:BIAS0 + 4]
        mean_w = const[:, MEAN0:MEAN0 + 128]

        x = sb("x", [128, TOKENS])
        xo = sb("xo", [128, 512])
        memw = sb("memw", [128, MEM_COLS])
        wk_T, wq_T = memw[:, 0:MEM], memw[:, MEM:2 * MEM]
        wv_T, wout_T = memw[:, 2 * MEM:2 * MEM + DIM], memw[:, 2 * MEM + DIM:2 * MEM + 2 * DIM]
        norm_w, eta_in = memw[:, MEM_COLS - 2:MEM_COLS - 1], memw[0:MEM, MEM_COLS - 1:MEM_COLS]
        ctx2 = ExitStack()

        def sb(name, shape, dt=F32):
            return ctx2.enter_context(nc.sbuf_tensor(name, shape, dt))

        xs = sb("xs", [128, 2, PAD + SEQ])
        xh = sb("xh", [128, 2, SEQ], F32R)
        xl = sb("xl", [128, 2, SEQ], F32R)
        raw = sb("raw", [128, 2, INNER])
        wh = sb("wh", [128, 4 * INNER], F32R)
        wl = sb("wl", [128, 4 * INNER], F32R)
        wv = sb("wv", [128, INNER])
        wo = sb("wo", [128, PAIRS, DIM])
        w1 = sb("w1", [128, 2 * FFN])
        w2 = sb("w2", [128, 3, DIM])
        small = sb("small", [128, SMALLS])
        rots = sb("rots", [128, 4, SEQ])
        q = sb("q", [128, 2, PAIRS, SEQ])
        k = sb("k", [128, 2, PAIRS, SEQ])
        v = sb("v", [128, 2, WINDOWS, PAIRS, VW])
        prod = sb("prod", [128, 4, 2, SEQ])
        sq = sb("sq", [128, 2, 2, SEQ])
        nsum = sb("nsum", [64, SEQ])
        nlog = sb("nlog", [64, SEQ])
        rnorm = sb("rnorm", [64, SEQ])
        rq = sb("rq", [128, 2, 2, HEADS])
        smax = sb("smax", [128, 2, PAIRS])
        diff = sb("diff", [128, 2, 512])
        prob = sb("prob", [128, 2, 512])
        probT = sb("probT", [128, 2, 512])
        rsum = sb("rsum", [128, 8])
        o = sb("o", [128, 2, 512])
        oT = sb("oT", [128, PAIRS, SEQ])
        fs = sb("fs", [128, SEQ])
        fc = sb("fc", [128, SEQ])
        fq = sb("fq", [128, SEQ])
        fl = sb("fl", [128, SEQ])
        fr = sb("fr", [128, SEQ])
        fn = sb("fn", [128, SEQ])
        gl = sb("gl", [128, SEQ])
        hid = sb("hid", [128, 3, SEQ])

        bank_c = ps("bank_c", 512)
        bank_r = ps("bank_r", 512)
        bank_m = ps("bank_m", 512)
        bank_t = ps("bank_t", 512)
        bank_s = ps("bank_s", 1024)
        bank_o = ps("bank_o", 1024)

        c_full, r_full = sem("c_full"), sem("r_full")
        nsum_full = sem("nsum_full")
        rqt_full, spread_full = sem("rqt_full"), sem("spread_full")
        v_full, f_full = sem("v_full"), sem("f_full")
        s_full, pt_full, o_full, ot_full = sem("s_full"), sem("pt_full"), sem("o_full"), sem("ot_full")
        sq_done = sem("sq_done")
        log_done, rnorm_done = sem("log_done"), sem("rnorm_done")
        v_done, prob_done, pt_done, ot_done = sem("v_done"), sem("prob_done"), sem("pt_done"), sem("ot_done")
        xh_done = sem("xh_done")
        fq_done, fl_done, fr_done, gelu_done = sem("fq_done"), sem("fl_done"), sem("fr_done"), sem("gelu_done")
        wh_done = sem("wh_done")
        xs_done = sem("xs_done")
        prod_done = sem("prod_done")
        clamp_done, rq_done, kn_done = sem("clamp_done"), sem("rq_done"), sem("kn_done")
        max_done, diff_done, rsum_done, o_done = sem("max_done"), sem("diff_done"), sem("rsum_done"), sem("o_done")
        xl_done = sem("xl_done")
        x1_done, fs_done, fc_done, fm_done, fn_done, hid_done = (
            sem("x1_done"), sem("fs_done"), sem("fc_done"), sem("fm_done"), sem("fn_done"), sem("hid_done"))
        x_ready = sem("x_ready")
        wl_done, rots_done = sem("wl_done"), sem("rots_done")
        scaled_done, qadd_done, kadd_done = sem("scaled_done"), sem("qadd_done"), sem("kadd_done")
        raw_in = [sem("raw_in0"), sem("raw_in1")]
        wv_in, wo_in, w1_in, small_in = sem("wv_in"), sem("wo_in"), sem("w1_in"), sem("small_in")
        const_in, x_in, setup, out_done = sem("const_in"), sem("x_in"), sem("setup"), sem("out_done")
        pro_pe, pro_act, pro_dve = sem("pro_pe"), sem("pro_act"), sem("pro_dve")

        ctx2.close()

        def chunk_buffers():
            alloc = ExitStack()

            def sb(name, shape):
                return alloc.enter_context(nc.sbuf_tensor(name, shape, F32))

            return dict(
                x1=sb("x1", [128, TOKENS]), yn=sb("yn", [128, TOKENS]), msq=sb("msq", [128, 512]), mlog=sb("mlog", [128, 512]),
                mrs=sb("mrs", [128, 512]), neg=sb("neg", [64, 2, 512]),
                kT=sb("kT", [64, BATCH, SEQ + STEPS]), qT=sb("qT", [64, BATCH, SEQ]), vT=sb("vT", [128, BATCH, SEQ + STEPS]),
                eta=sb("eta", [64, 1]), ke=sb("ke", [64, 2, BATCH, 2 * STEPS + 1]), vc=sb("vc", [128, 2, BATCH, STEPS1]),
                ek_rows=sb("ek_rows", [STEPS1, 2, BATCH, MEM]), v_rows=sb("v_rows", [STEPS1, 2, BATCH, DIM]),
                gram_s=sb("gram_s", [STEPS1, BATCH * GRAM]), gram_b=sb("gram_b", [BATCH, 2, STEPS1, GRAM]),
                coef=sb("coef", [BATCH, 2, STEPS, STEPS1, STEPS1]), ab=sb("ab", [BATCH, STEPS, STEPS1]),
                lin=sb("lin", [BATCH, 2, STEPS, STEPS1]), sqr=sb("sqr", [BATCH, 2, STEPS, STEPS1]),
                kap2=sb("kap2", [BATCH, 2, STEPS]), sigh=sb("sigh", [BATCH, 2, STEPS]), cvec=sb("cvec", [BATCH, STEPS1]),
                m=sb("m", [64, BATCH, DIM]), yt=sb("yt", [128, BATCH, 2 * STEPS]), ysq=sb("ysq", [128, 2, BATCH, STEPS]),
                gp_s=sb("gp_s", [STEPS1, BATCH * STEPS]), hp_s=sb("hp_s", [1, 2 * BATCH * STEPS]),
                gram_m=sb("gram_m", [BATCH, STEPS1, STEPS1]), quad=sb("quad", [BATCH, STEPS1]), e_raw=sb("e_raw", [BATCH, STEPS]),
                u2=sb("u2", [BATCH, 1]), pn=sb("pn", [BATCH, 1]), s1=sb("s1", [BATCH, 1]), s2=sb("s2", [BATCH, 1]),
                s3=sb("s3", [BATCH, 1]), w2_=sb("w2_", [BATCH, 1]), w2c=sb("w2c", [BATCH, 1]), nd=sb("nd", [BATCH, 1]),
                tau=sb("tau", [BATCH, 1]), rt2=sb("rt2", [BATCH, 1]), lv=sb("lv", [BATCH, STEPS1]), lw=sb("lw", [BATCH, STEPS1]),
                w=sb("w", [BATCH, STEPS]), rho=sb("rho", [BATCH, 1]), itau=sb("itau", [BATCH, 1]), nrho=sb("nrho", [BATCH, 1]),
                cf=sb("cf", [BATCH, STEPS1]), diag=sb("diag", [BATCH, BATCH]), cf_s=sb("cf_s", [STEPS1, BATCH]),
                scaled=sb("scaled", [STEPS1, BATCH, MEM]), mem_T=sb("mem_T", [128, 512]), ones8=sb("ones8", [BATCH, MEM]),
                half=sb("half", [BATCH, 1]),
            ), alloc

        A, alloc = chunk_buffers()
        alloc.close()
        g = type("Buffers", (), A)
        NCH = SEQ // STEPS
        mp, ma, mv, mq = sem("mp"), sem("ma"), sem("mv"), sem("mq")
        x1_in, memw_in, x2_out, xo_in = sem("x1_in"), sem("memw_in"), sem("x2_out"), sem("xo_in")
        end_dve = sem("end_dve")
        prep_in, rows_full, gram_full, y_full, gp_full, hp_full, cf_full, n_full = (
            sem("prep_in"), sem("rows_full"), sem("gram_full"), sem("y_full"), sem("gp_full"), sem("hp_full"),
            sem("cf_full"), sem("n_full"))
        rows_done, gram_done, gp_done, root_done = sem("rows_done"), sem("gram_done"), sem("gp_done"), sem("root_done")
        coef_step, coef_done, gram_in, start_in = sem("coef_step"), sem("coef_done"), sem("gram_in"), sem("start_in")
        dve_step, want_root, yt_done, ysq_done, cf_done, scaled_done2, m_done = (
            sem("dve_step"), sem("want_root"), sem("yt_done"), sem("ysq_done"), sem("cf_done"), sem("scaled2"), sem("m_done"))
        fin_pe, fin_act, fin_dve = sem("fin_pe"), sem("fin_act"), sem("fin_dve")
        ROOTS = 2 * STEPS
        ALL_X = BATCH * (layers + 1)

        class Chunk:

            def __init__(self, it, p):
                self.it, self.p = it, p

            def __call__(self, per, k, ahead=0):
                return self.it * (2 * per) + (per * (self.p + ahead + 2) + k + 1)

        def mid_sp(sp):
            sp.wait_ge(x_ready, ALL_X)
            for c in range(4):
                sp.dma_start(g.x1[:, 512 * c:512 * c + 512], xT[:, 512 * c:512 * c + 512]).then_inc(x1_in, 16)
            sp.wait_ge(mq, 1)

            def gram(done):
                sp.wait_ge(gram_done, done(1, 0))
                for b in range(BATCH):
                    sp.dma_start(g.gram_b[b:b + 1, done.p, :, :], g.gram_s[:, GRAM * b:GRAM * b + GRAM]).then_inc(gram_in, 16)

            def start(done):
                sp.wait_ge(gp_done, done(2, 1))
                for b in range(BATCH):
                    sp.dma_start(g.gram_m[b:b + 1, :, 0:STEPS], g.gp_s[:, STEPS * b:STEPS * b + STEPS]).then_inc(start_in, 16)
                sp.dma_start(g.quad[:, 0:STEPS], g.hp_s[:, 0:BATCH * STEPS]).then_inc(start_in, 16)
                sp.dma_start(g.e_raw[:, :], g.hp_s[:, BATCH * STEPS:]).then_inc(start_in, 16)

            gram(Chunk(0, 0))
            sp.sem_inc(start_in, 1)
            with sp.Fori(0, NCH // 2) as it:
                for p in range(2):
                    start(Chunk(it, p))
                    d = Chunk(it, p)
                    sp.wait_ge(gram_done, d(1, 0, 1))
                    for b in range(BATCH):
                        sp.dma_start(g.gram_b[b:b + 1, 1 - p, :, :], g.gram_s[:, GRAM * b:GRAM * b + GRAM]).then_inc(gram_in, 16)
            sp.wait_ge(fin_dve, 8)
            sp.dma_start(x2, x[:, :]).then_inc(x2_out, 16)
            sp.wait_ge(x2_out, 16)

        def mid_pe(pe):
            for s, per in ((rows_full, 2), (gram_full, 1), (y_full, 1), (gp_full, 1), (hp_full, 1), (cf_full, 1), (n_full, 1)):
                pe.sem_inc(s, 2 * per)
            pe.wait_ge(memw_in, 16)
            for c in range(4):
                cols = slice(512 * c, 512 * c + 512)
                pe.wait_ge(mv, 8 * c + 1)
                pe.matmul(bank_c[:, :], mean_w, g.x1[:, cols], start=True, stop=True).then_inc(mp, 1)
                for k_ in (1, 4):
                    pe.wait_ge(ma, 9 * c + k_)
                    pe.matmul(bank_c[:, :], mean_w, g.msq[:, :], start=True, stop=True).then_inc(mp, 1)
                pe.wait_ge(mv, 8 * c + 4)
                pe.matmul(bank_r[0:64, :], wk_T, g.yn[:, cols], start=True, stop=True).then_inc(mp, 1)
                pe.matmul(bank_t[0:64, :], wq_T, g.yn[:, cols], start=True, stop=True).then_inc(mp, 1)
                pe.matmul(bank_m[:, :], wv_T, g.yn[:, cols], start=True, stop=True).then_inc(mp, 1)

            def prep(done, ahead):
                p = (done.p + ahead) % 2
                pe.wait_ge(prep_in, done(3, 2, ahead))
                pe.wait_ge(rows_done, done(2, 1, ahead - 1))
                for b in range(BATCH):
                    last = pe.transpose(bank_o[0:STEPS, DIM * b:DIM * b + DIM], g.vc[:, p, b, 0:STEPS], ident)
                last.then_inc(rows_full, 1)
                for b in range(BATCH):
                    last = pe.transpose(bank_t[0:STEPS, MEM * b:MEM * b + MEM], g.ke[:, p, b, STEPS:2 * STEPS], ident[0:64, 0:64])
                last.then_inc(rows_full, 1)
                pe.wait_ge(gram_done, done(1, 0, ahead - 1))
                for b in range(BATCH):
                    pe.matmul(bank_m[0:STEPS1, GRAM * b + 2 * STEPS + 1:GRAM * b + GRAM], g.vc[:, p, b, :], g.vc[:, p, b, :],
                              start=True, stop=True)
                    last = pe.matmul(bank_m[0:STEPS1, GRAM * b:GRAM * b + 2 * STEPS + 1], g.ke[:, p, b, STEPS:], g.ke[:, p, b, :],
                                     start=True, stop=True)
                last.then_inc(gram_full, 1)

            pe.wait_ge(mv, 32 + 16)
            prep(Chunk(0, 0), 0)
            with pe.Fori(0, NCH // 2) as it:
                for p in range(2):
                    done = Chunk(it, p)
                    pe.wait_ge(m_done, done(1, 0, -1))
                    for b in range(BATCH):
                        last = pe.matmul(bank_c[:, 2 * STEPS * b:2 * STEPS * (b + 1)], g.m[:, b, :], g.ke[:, p, b, 0:2 * STEPS],
                                         start=True, stop=True)
                    last.then_inc(y_full, 1)
                    pe.wait_ge(yt_done, done(1, 0))
                    pe.wait_ge(gp_done, done(2, 1, -1))
                    for b in range(BATCH):
                        last = pe.matmul(bank_r[0:STEPS1, STEPS * b:STEPS * (b + 1)], g.vc[:, p, b, :], g.yt[:, b, 0:STEPS],
                                         start=True, stop=True)
                    last.then_inc(gp_full, 1)
                    pe.wait_ge(ysq_done, done(2, 1))
                    pe.wait_ge(rows_done, done(2, 1))
                    pe.matmul(bank_t[0:1, 0:2 * BATCH * STEPS], ones_col, g.ysq[:, :, :, :].rearrange("p a b j -> p (a b j)"),
                              start=True, stop=True).then_inc(hp_full, 1)
                    pe.wait_ge(gp_done, done(2, 1))
                    prep(done, 1)
                    pe.wait_ge(cf_done, done(2, 1))
                    pe.matmul(bank_c[0:64, 272:272 + BATCH], g.ones8[:, :], g.diag[:, :], start=True, stop=True)
                    pe.transpose(bank_c[0:STEPS1, 256:256 + BATCH], g.cf[:, :], ident[0:BATCH, 0:BATCH]).then_inc(cf_full, 1)
                    pe.wait_ge(scaled_done2, done(1, 0))
                    pe.wait_ge(rows_done, done(2, 1))
                    for b in range(BATCH):
                        last = pe.matmul(bank_s[0:64, DIM * b:DIM * (b + 1)], g.scaled[:, b, :], g.v_rows[:, p, b, :],
                                         start=True, stop=True)
                    last.then_inc(n_full, 1)
            done = Chunk(NCH // 2, 0)
            pe.wait_ge(m_done, done(1, 0, -1))
            for c in range(4):
                if c:
                    pe.wait_ge(fin_act, c)
                for b in range(2):
                    last = pe.matmul(bank_c[:, SEQ * b:SEQ * (b + 1)], g.m[:, 2 * c + b, :], g.qT[:, 2 * c + b, :],
                                     start=True, stop=True)
                last.then_inc(fin_pe, 1)
                pe.wait_ge(fin_act, c + 1)
                if c:
                    pe.wait_ge(fin_dve, 2 * c)
                pe.matmul(bank_r[:, :], wout_T, g.mem_T[:, :], start=True, stop=True).then_inc(fin_pe, 1)

        def mid_act(act):
            for s, per in ((rows_done, 2), (gram_done, 1), (gp_done, 2), (root_done, ROOTS)):
                act.sem_inc(s, 2 * per)
            act.preload_act_table_set("natural_log_exp_and_others")
            for c in range(4):
                cols = slice(512 * c, 512 * c + 512)
                for r in range(2):
                    act.wait_ge(mv, 8 * c + 2 + r)
                    act.activation(g.msq[:, :], x[:, cols], ACT.Square).then_inc(ma, 1)
                    act.wait_ge(mp, 6 * c + 2 + r)
                    act.activation(g.mlog[:, :], bank_c[:, :], ACT.Ln, bias=(eps, eps_rms)[r]).then_inc(ma, 1)
                    act.wait_ge(ma, 9 * c + 3 * r + 2)
                    if r:
                        act.wait_ge(mv, 8 * c + 3)
                    act.activation(g.mrs[:, :], g.mlog[:, :], ACT.Exp, scale=-0.5).then_inc(ma, 1)
                for r in range(2):
                    act.wait_ge(mv, 8 * c + 5 + r)
                    act.activation(g.neg[:, r, :], g.neg[:, r, :], ACT.Exp).then_inc(ma, 1)
                act.wait_ge(mp, 6 * c + 6)
                act.activation(g.vT[:, 2 * c:2 * c + 2, 0:SEQ], bank_m[:, :].rearrange("p (b t) -> p b t", b=2), ACT.Copy)\
                    .then_inc(ma, 1)
            act.preload_act_table_set("sqrt_and_others")

            def prep_out(done, ahead, first=False):
                p = (done.p + ahead) % 2
                act.wait_ge(rows_full, done(2, 0, ahead))
                act.activation(g.v_rows[0:STEPS, p, :, :], bank_o[0:STEPS, :].rearrange("p (b f) -> p b f", b=BATCH), ACT.Copy)\
                    .then_inc(rows_done, 1)
                act.wait_ge(rows_full, done(2, 1, ahead))
                act.activation(g.ek_rows[0:STEPS, p, :, :], bank_t[0:STEPS, :].rearrange("p (b f) -> p b f", b=BATCH), ACT.Copy)\
                    .then_inc(rows_done, 1)
                act.wait_ge(gram_full, done(1, 0, ahead))
                if not first:
                    act.wait_ge(gram_in, 16 * BATCH * 1 + done.it * (2 * 16 * BATCH) + (16 * BATCH * (done.p + ahead - 1)))
                act.activation(g.gram_s[:, :], bank_m[0:STEPS1, 0:BATCH * GRAM], ACT.Copy).then_inc(gram_done, 1)

            act.wait_ge(mv, 32 + 16)
            prep_out(Chunk(0, 0), 0, True)

            with act.Fori(0, NCH // 2) as it:
                for p in range(2):
                    done = Chunk(it, p)
                    act.wait_ge(gp_full, done(1, 0))
                    act.wait_ge(start_in, it * (2 * 160) + 160 * p + 1)
                    act.activation(g.gp_s[:, :], bank_r[0:STEPS1, 0:BATCH * STEPS], ACT.Copy).then_inc(gp_done, 1)
                    act.wait_ge(hp_full, done(1, 0))
                    act.activation(g.hp_s[:, :], bank_t[0:1, 0:2 * BATCH * STEPS], ACT.Copy).then_inc(gp_done, 1)
                    for i in range(STEPS):
                        act.wait_ge(want_root, done(ROOTS, 2 * i))
                        act.activation(g.w[:, i:i + 1], g.w2c[:, :], ACT.Sqrt).then_inc(root_done, 1)
                        act.wait_ge(want_root, done(ROOTS, 2 * i + 1))
                        act.activation(g.rt2[:, :], g.tau[:, :], ACT.Sqrt, scale=4.0).then_inc(root_done, 1)
                        if i == 4:
                            prep_out(done, 1)
            for c in range(4):
                act.wait_ge(fin_pe, 2 * c + 1)
                if c:
                    act.wait_ge(fin_pe, 2 * c)
                act.activation(g.mem_T[:, :], bank_c[:, :], ACT.Copy).then_inc(fin_act, 1)

        def mid_pool(pool):
            for s, per in ((prep_in, 3), (coef_done, 1)):
                pool.sem_inc(s, 2 * per)
            pool.wait_ge(mv, 32 + 16)
            pool.sem_inc(mq, 1)

            PER = 12

            def prep(done, ahead, at, base):
                p = (done.p + ahead) % 2
                n = [0]

                def step(ins):
                    ins.then_inc(coef_step, 1)
                    n[0] += 1
                    pool.wait_ge(coef_step, base + n[0])

                pool.wait_ge(m_done, done(1, 0, ahead - 2))
                kc = g.kT[:, :, bass.ds(at, STEPS)]
                pool.tensor_copy(g.ke[:, p, :, 0:STEPS], kc).then_inc(prep_in, 1)
                pool.tensor_tensor(g.ke[:, p, :, STEPS:2 * STEPS], kc, g.eta[:, 0:1].unsqueeze(2).to_broadcast([MEM, BATCH, STEPS]),
                                   ALU.mult).then_inc(prep_in, 1)
                pool.wait_ge(prep_in, done(3, 1, ahead))
                pool.tensor_copy(g.vc[:, p, :, 0:STEPS], g.vT[:, :, bass.ds(at, STEPS)]).then_inc(prep_in, 1)
                pool.wait_ge(prep_in, done(3, 2, ahead))
                pool.wait_ge(gram_in, 16 * BATCH + done.it * (2 * 16 * BATCH) + 16 * BATCH * (done.p + ahead))
                gb = g.gram_b[:, p, :, :]
                kk, ee, vv = gb[:, 0:STEPS, 0:STEPS], gb[:, 0:STEPS, STEPS:2 * STEPS + 1], gb[:, 0:STEPS, 2 * STEPS + 1:]
                vdiag = gb.rearrange("b i m -> b (i m)")[:, 2 * STEPS + 1:2 * STEPS + 1 + (STEPS - 1) * (GRAM + 1) + 1:GRAM + 1]
                co = g.coef[:, p, :, :, :]
                full = [BATCH, STEPS, STEPS1, STEPS]
                step(pool.tensor_tensor(co[:, :, :, 0:STEPS], kk.unsqueeze(2).to_broadcast(full),
                                        vv.unsqueeze(3).to_broadcast(full), ALU.mult))
                step(pool.tensor_tensor(g.ab[:, :, :], ee, vv, ALU.mult))
                step(pool.tensor_tensor(co[:, :, :, STEPS], g.ab[:, :, :], g.cvec[:, :].unsqueeze(1).to_broadcast([BATCH, STEPS, STEPS1]),
                                        ALU.mult))
                step(pool.tensor_tensor(g.lin[:, p, :, 0:STEPS], kk, kk, ALU.add))
                step(pool.tensor_tensor(g.sqr[:, p, :, 0:STEPS], kk, kk, ALU.mult))
                step(pool.tensor_tensor(g.sqr[:, p, :, 0:STEPS], g.sqr[:, p, :, 0:STEPS],
                                        vdiag.unsqueeze(2).to_broadcast([BATCH, STEPS, STEPS]), ALU.mult))
                abdiag = g.ab[:, :, :].rearrange("b i l -> b (i l)")[:, 0:(STEPS - 1) * (STEPS1 + 1) + 1:STEPS1 + 1]
                step(pool.tensor_tensor(g.sqr[:, p, :, STEPS], abdiag, g.cvec[:, STEPS:].to_broadcast([BATCH, STEPS]), ALU.mult))
                step(pool.tensor_tensor(g.kap2[:, p, :], gb[:, STEPS, 0:STEPS], gb[:, STEPS, 0:STEPS], ALU.add))
                pool.tensor_tensor(g.sigh[:, p, :], gb[:, 0:STEPS, GRAM - 1], g.half[:, :].to_broadcast([BATCH, STEPS]), ALU.mult).then_inc(coef_done, 1)
                pool.wait_ge(coef_done, done(1, 0, ahead))
                return n[0]

            per = prep(Chunk(0, 0), 0, 0, 0)
            with pool.Fori(0, NCH // 2) as it:
                for p in range(2):
                    prep(Chunk(it, p), 1, it * (2 * STEPS) + STEPS * (p + 1), it * (2 * per) + per * (p + 1))

        def mid_dve(dve):
            for s, per in ((want_root, ROOTS), (yt_done, 1), (ysq_done, 2), (cf_done, 2), (scaled_done2, 1), (m_done, 1)):
                dve.sem_inc(s, 2 * per)
            for c in range(4):
                cols = slice(512 * c, 512 * c + 512)
                dve.wait_ge(x_ready, ALL_X)
                dve.wait_ge(x1_in, 64)
                dve.scalar_tensor_tensor(out=g.x1[:, cols], in0=x[:, cols], scalar=0.5, in1=g.x1[:, cols], op0=ALU.mult, op1=ALU.add)\
                    .then_inc(mv, 1)
                dve.wait_ge(mp, 6 * c + 1)
                dve.wait_ge(mv, 8 * c + 1)
                dve.tensor_tensor(x[:, cols], g.x1[:, cols], bank_c[:, :], ALU.subtract).then_inc(mv, 1)
                dve.wait_ge(ma, 9 * c + 3)
                dve.wait_ge(mv, 8 * c + 2)
                dve.tensor_tensor(x[:, cols], x[:, cols], g.mrs[:, :], ALU.mult).then_inc(mv, 1)
                dve.wait_ge(ma, 9 * c + 6)
                dve.wait_ge(mv, 8 * c + 3)
                dve.scalar_tensor_tensor(out=g.yn[:, cols], in0=x[:, cols], scalar=norm_w, in1=g.mrs[:, :], op0=ALU.mult, op1=ALU.mult)\
                    .then_inc(mv, 1)
                for r, bank in ((0, bank_r), (1, bank_t)):
                    dve.wait_ge(mp, 6 * c + 4 + r)
                    dve.tensor_scalar(g.neg[:, r, :], bank[0:64, :], 0.0, None, ALU.min).then_inc(mv, 1)
                for r, (bank, dst) in enumerate(((bank_r, g.kT), (bank_t, g.qT))):
                    dve.wait_ge(ma, 9 * c + 7 + r)
                    dve.scalar_tensor_tensor(out=dst[:, 2 * c:2 * c + 2, 0:SEQ], in0=bank[0:64, :].rearrange("p (b t) -> p b t", b=2),
                                             scalar=0.0, in1=g.neg[:, r, :].rearrange("p (b t) -> p b t", b=2),
                                             op0=ALU.max, op1=ALU.add).then_inc(mv, 1)
            dve.wait_ge(ma, 36)
            dve.scalar_tensor_tensor(out=g.eta[:, :], in0=eta_in, scalar=-1.0, in1=eta_in, op0=ALU.mult, op1=ALU.max).then_inc(mv, 1)
            dve.wait_ge(mv, 32 + 1)
            dve.tensor_scalar(g.eta[:, :], g.eta[:, :], ETA_MIN, None, ALU.max).then_inc(mv, 1)
            dve.memset(g.kT[:, :, SEQ:], 0.0).then_inc(mv, 1)
            dve.memset(g.vT[:, :, SEQ:], 0.0).then_inc(mv, 1)
            dve.memset(g.ke[:, :, :, 2 * STEPS:], 1.0).then_inc(mv, 1)
            dve.memset(g.vc[:, :, :, STEPS:], 1.0).then_inc(mv, 1)
            dve.memset(g.ek_rows[:, :, :, :], 1.0).then_inc(mv, 1)
            dve.memset(g.v_rows[:, :, :, :], 1.0).then_inc(mv, 1)
            dve.memset(g.lin[:, :, :, STEPS:], 1.0).then_inc(mv, 1)
            dve.memset(g.cvec[:, 0:STEPS], 2.0 / MEM_SIZE).then_inc(mv, 1)
            dve.memset(g.cvec[:, STEPS:], 1.0 / MEM_SIZE).then_inc(mv, 1)
            dve.memset(g.m[:, :, :], 0.0).then_inc(mv, 1)
            dve.memset(g.itau[:, :], 0.0).then_inc(mv, 1)
            dve.memset(g.nd[:, :], 0.0).then_inc(mv, 1)
            dve.memset(g.ones8[:, :], 1.0).then_inc(mv, 1)
            dve.memset(g.half[:, :], 0.5).then_inc(mv, 1)
            dve.wait_ge(mv, 32 + 16)

            def chunk(done, base):
                p, n = done.p, [0]

                def step(ins, wait=True):
                    ins.then_inc(dve_step, 1)
                    n[0] += 1
                    if wait:
                        dve.wait_ge(dve_step, base + n[0])

                def stt(out, in0, scalar, in1, op0, op1):
                    return dve.scalar_tensor_tensor(out=out, in0=in0, scalar=scalar, in1=in1, op0=op0, op1=op1)

                dve.wait_ge(y_full, done(1, 0))
                dve.tensor_copy(g.yt[:, :, :], bank_c[:, 0:2 * STEPS * BATCH].rearrange("p (b j) -> p b j", b=BATCH)).then_inc(yt_done, 1)
                dve.wait_ge(yt_done, done(1, 0))
                dve.tensor_tensor(g.ysq[:, 0, :, :], g.yt[:, :, 0:STEPS], g.yt[:, :, 0:STEPS], ALU.mult).then_inc(ysq_done, 1)
                dve.tensor_tensor(g.ysq[:, 1, :, :], g.yt[:, :, STEPS:], g.vc[:, p, :, 0:STEPS], ALU.mult).then_inc(ysq_done, 1)
                step(stt(g.quad[:, STEPS:], g.nd[:, :], -1.0, g.itau[:, :], ALU.mult, ALU.mult))
                step(dve.memset(g.gram_m[:, STEPS, STEPS:], 0.0), False)
                step(dve.memset(g.tau[:, :], 1.0), False)
                step(dve.memset(g.rt2[:, :], 2.0), False)
                dve.wait_ge(start_in, done.it * (2 * 160) + 160 * (p + 1) + 1)
                step(dve.tensor_scalar(g.gram_m[:, 0:STEPS, STEPS], g.e_raw[:, :], 2.0 / MEM_SIZE, None, ALU.mult))
                dve.wait_ge(coef_done, done(1, 0))
                mean = g.gram_m[:, STEPS, STEPS:]
                for i in range(STEPS):
                    now, nxt_ = slice(i, i + 1), slice(i + 1, STEPS1)
                    step(dve.tensor_tensor(g.lv[:, :], g.lin[:, p, i, :], g.gram_m[:, i, :], ALU.mult), False)
                    step(dve.tensor_tensor(g.u2[:, :], mean, g.kap2[:, p, now], ALU.mult))
                    step(stt(g.pn[:, :], g.sigh[:, p, now], g.u2[:, :], g.gram_m[:, i, now], ALU.mult, ALU.subtract), False)
                    step(stt(g.s1[:, :], g.u2[:, :], float(DIM // 4), g.gram_m[:, STEPS, now], ALU.mult, ALU.subtract))
                    step(stt(g.s2[:, :], g.s1[:, :], g.u2[:, :], g.quad[:, now], ALU.mult, ALU.add))
                    vii = g.gram_b[:, p, i, 2 * STEPS + 1 + i:2 * STEPS + 2 + i]
                    step(stt(g.s3[:, :], g.tau[:, :], vii, g.s2[:, :], ALU.mult, ALU.add))
                    dve.wait_ge(root_done, done(ROOTS, 2 * i - 1))
                    step(stt(g.w2_[:, :], g.pn[:, :], g.rt2[:, :], g.s3[:, :], ALU.mult, ALU.add))
                    dve.tensor_scalar(g.w2c[:, :], g.w2_[:, :], 0.0, None, ALU.max).then_inc(want_root, 1)
                    dve.wait_ge(root_done, done(ROOTS, 2 * i))
                    w = g.w[:, now]
                    step(stt(g.lw[:, :], g.sqr[:, p, i, :], w, g.lv[:, :], ALU.mult, ALU.add))
                    step(stt(g.quad[:, :], g.lw[:, :], w, g.quad[:, :], ALU.mult, ALU.add), False)
                    step(stt(g.gram_m[:, nxt_, :], g.coef[:, p, i, nxt_, :], w, g.gram_m[:, nxt_, :], ALU.mult, ALU.add))
                    step(stt(g.nd[:, :], mean, mean, g.quad[:, STEPS:], ALU.mult, ALU.subtract))
                    stt(g.tau[:, :], g.tau[:, :], EPS, g.nd[:, :], ALU.mult, ALU.subtract).then_inc(want_root, 1)
                    dve.wait_ge(want_root, done(ROOTS, 2 * i + 1))
                dve.wait_ge(root_done, done(ROOTS, ROOTS - 1))
                step(dve.reciprocal(g.rho[:, :], g.rt2[:, :]))
                step(dve.reciprocal(g.itau[:, :], g.tau[:, :]), False)
                step(dve.tensor_scalar(g.nrho[:, :], g.rho[:, :], 2.0, None, ALU.mult))
                dve.tensor_scalar(g.cf[:, 0:STEPS], g.w[:, :], g.nrho[:, :], None, ALU.mult).then_inc(cf_done, 1)
                step(stt(g.cf[:, STEPS:], mean, -1.0, g.nrho[:, :], ALU.mult, ALU.mult))
                dve.tensor_scalar(g.diag[:, :], ident[0:BATCH, 0:BATCH], g.nrho[:, :], None, ALU.mult).then_inc(cf_done, 1)
                dve.wait_ge(cf_full, done(1, 0))
                step(dve.tensor_copy(g.cf_s[:, :], bank_c[0:STEPS1, 256:256 + BATCH]))
                dve.wait_ge(rows_done, done(2, 1))
                dve.tensor_tensor(g.scaled[:, :, :], g.ek_rows[:, p, :, :], g.cf_s[:, :].unsqueeze(2).to_broadcast([STEPS1, BATCH, MEM]),
                                  ALU.mult).then_inc(scaled_done2, 1)
                step(dve.tensor_tensor(g.m[:, :, :], g.m[:, :, :], bank_c[0:64, 272:272 + BATCH].unsqueeze(2).to_broadcast([64, BATCH, DIM]),
                                       ALU.mult))
                dve.wait_ge(n_full, done(1, 0))
                dve.tensor_tensor(g.m[:, :, :], g.m[:, :, :], bank_s[0:64, :].rearrange("p (b d) -> p b d", b=BATCH), ALU.add)\
                    .then_inc(m_done, 1)
                return n[0]

            per = 5 + 11 * STEPS + 6
            with dve.Fori(0, NCH // 2) as it:
                for p in range(2):
                    used = chunk(Chunk(it, p), it * (2 * per) + per * p)
                    assert used == per, used
            for c in range(4):
                cols = slice(512 * c, 512 * c + 512)
                dve.wait_ge(fin_pe, 2 * c + 2)
                dve.tensor_tensor(x[:, cols], x[:, cols], bank_r[:, :], ALU.add).then_inc(fin_dve, 1)
                dve.wait_ge(fin_dve, 2 * c + 1)
                dve.tensor_tensor(x[:, cols], x[:, cols], g.x1[:, cols], ALU.add).then_inc(fin_dve, 1)

        NCONV = 4
        block = ctx.enter_context(nc.Block())

        def layer_of(layer, stack):
            return layer + LAYERS * stack

        @block.sync
        def _(sp):
            sp.dma_start(x[:, :], xT).then_inc(x_in, 16)
            sp.dma_start(memw[:, :], mem_w).then_inc(memw_in, 16)
            sp.dma_start(const[:, :], consts).then_inc(const_in, 16)
            sp.dma_start(maskf[:, :], maskc).then_inc(const_in, 16)
            for stack in range(stacks):
                if stack:
                    mid_sp(sp)
                with sp.Fori(0, layers) as layer:
                    done = Count(layer, stack)
                    nth = layer_of(layer, stack)
                    for c in range(NCONV):
                        sp.wait_ge(wl_done, nth * NCONV + max(0, c - 1) + 1)
                        sp.dma_start(raw[:, c % 2, :], w_qk[layer, :, c * INNER:(c + 1) * INNER]).then_inc(raw_in[c % 2], 16)
                        if c == 1:
                            sp.wait_ge(v_full, done(8, -1, 7))
                            sp.dma_start(wv[:, :], w_v[layer]).then_inc(wv_in, 16)
                            sp.wait_ge(x_ready, done.x(7))
                            sp.dma_start(small[:, :], smalls[layer]).then_inc(small_in, 16)
                    sp.dma_start(wo[:, :, :], w_o[layer].rearrange("(c p) n -> p c n", p=128)).then_inc(wo_in, 16)
                    sp.dma_start(w1[:, :], w_1[layer]).then_inc(w1_in, 16)
                    sp.dma_start(w2[:, 0:2, :], w_2[layer, 0:256, :].rearrange("(c p) n -> p c n", p=128)).then_inc(w1_in, 16)
                    sp.dma_start(w2[0:FFN - 256, 2, :], w_2[layer, 256:FFN, :]).then_inc(w1_in, 16)
            for c in range(4):
                cols = slice(512 * c, 512 * c + 512)
                if c:
                    sp.wait_ge(end_dve, c)
                sp.dma_start(xo[:, :], (x2 if stacks > 1 else xT)[:, cols]).then_inc(xo_in, 16)
            for c in range(4):
                cols = slice(512 * c, 512 * c + 512)
                sp.wait_ge(end_dve, c + 1)
                sp.dma_start(out[:, cols], x[:, cols]).then_inc(out_done, 16)
            sp.wait_ge(out_done, 64)

        @block.tensor
        def _(pe):
            for s, per in ((c_full, 8), (r_full, 8), (nsum_full, 4), (rqt_full, 4), (spread_full, 4), (v_full, 8),
                           (f_full, 7), (s_full, 4), (pt_full, 4), (o_full, 4), (ot_full, 4)):
                pe.sem_inc(s, 2 * per)
            pe.wait_ge(const_in, 32)
            pe.wait_ge(setup, 5)

            def project(done, b, u, kind, which, bank, full):
                p = b % 2
                n = 2 * u + kind
                if kind == 0:
                    if which == 0:
                        pe.wait_ge(rq_done, done(4, b, u - 1))
                    else:
                        pe.wait_ge(kn_done, done(4, b, u - 1))
                else:
                    pe.wait_ge(prod_done, done(16, b, 4 * u + which))
                    if which == 0:
                        pe.wait_ge(sq_done, done(8, b, 2 * u))
                sec = 2 * kind + which
                for a in range(2):
                    w = slice(sec * INNER + (2 * u + a) * 128, sec * INNER + (2 * u + a + 1) * 128)
                    dst = bank[:, a * SEQ:(a + 1) * SEQ]
                    pe.matmul(dst, wh[:, w], xh[:, p, :], start=True, stop=False)
                    pe.matmul(dst, wl[:, w], xh[:, p, :], start=False, stop=False)
                    last = pe.matmul(dst, wh[:, w], xl[:, p, :], start=False, stop=True)
                last.then_inc(full, 1)

            def values(done, b, w, before):
                p = b % 2
                before()
                for e in range(2):
                    last = pe.matmul(bank_m[64 * e:64 * e + 64, :], xs[:, p, w * WINDOW:w * WINDOW + 64],
                                     wv[:, :].rearrange("p (c e d) -> p e c d", e=2, d=HEAD_DIM)[:, e, :, :],
                                     start=True, stop=True)
                last.then_inc(v_full, 1)

            def norms(done, b, u):
                pe.wait_ge(sq_done, done(8, b, 2 * u + 1))
                pe.wait_ge(prod_done, done(16, b, 4 * u + 2))
                for a in range(2):
                    for kind in range(2):
                        last = pe.matmul(bank_c[32 * kind:32 * kind + 32, 0:SEQ], head_sum[:, a, :], sq[:, kind, a, :],
                                         start=(a == 0), stop=(a == 1))
                last.then_inc(nsum_full, 1)

            def spread_norms(done, b, u):
                pe.wait_ge(rnorm_done, done(4, b, u))
                pe.wait_ge(prod_done, done(16, b, 4 * u + 3))
                for a in range(2):
                    last = pe.matmul(bank_r[:, a * SEQ:(a + 1) * SEQ], spread[32:64, a, :], rnorm[32:64, :],
                                     start=True, stop=True)
                last.then_inc(spread_full, 1)
                for j in range(2):
                    last = pe.transpose(bank_c[:, SEQ + 32 * j:SEQ + 32 * j + 32], rnorm[0:32, 128 * j:128 * j + 128],
                                        ident[0:32, 0:32])
                last.then_inc(rqt_full, 1)

            def scores(done, b, i):
                p, j, oct_ = b % 2, i // 2, i % 2
                half = 256 * (i % 2)
                pe.wait_ge(kn_done, done(4, b, 2 * oct_ + 1))
                pe.wait_ge(qadd_done, done(4, b, 2 * oct_ + 1))
                pe.wait_ge(diff_done, done(4, b, i - 2))
                for e in range(2):
                    pe.matmul(bank_s[:, 512 * e + half:512 * e + half + 256], identb[:, :], mask[:, j, :],
                              start=True, stop=False, skip_group_check=True)
                for c in range(4):
                    for g in range(4):
                        t = 128 * j + WINDOW * g
                        lo = 0 if t == 0 else WINDOW
                        n = WINDOW + lo
                        for e in range(2):
                            rows = slice(64 * e, 64 * e + 64)
                            s0 = 512 * e + half + 64 * c + WINDOW - lo
                            last = pe.matmul(bank_s[32 * g:32 * g + 32, s0:s0 + n],
                                             q[rows, p, 4 * oct_ + c, t:t + WINDOW], k[rows, p, 4 * oct_ + c, t - lo:t + WINDOW],
                                             start=False, stop=True, skip_group_check=True)
                last.then_inc(s_full, 1)

            def probs_T(done, b, i):
                pe.wait_ge(prob_done, done(4, b, i))
                pe.wait_ge(ot_done, done(4, b, i - 1))
                for c in range(4):
                    last = pe.transpose(bank_t[:, 128 * c:128 * c + 128], prob[:, i % 2, 128 * c:128 * c + 128], ident)
                last.then_inc(pt_full, 1)

            def attend(done, b, i):
                p, j, oct_ = b % 2, i // 2, i % 2
                pe.wait_ge(setup, 5)
                pe.wait_ge(pt_done, done(4, b, i))
                pe.wait_ge(v_done, done(8, b, 4 * j + 3))
                pe.wait_ge(o_done, done(4, b, i - 1))
                for c in range(4):
                    for g in range(4):
                        for e in range(2):
                            rows = slice(64 * e, 64 * e + 64)
                            last = pe.matmul(bank_o[32 * g:32 * g + 32, 512 * e + VW * c:512 * e + VW * c + VW],
                                             probT[rows, i % 2, 128 * c + 32 * g:128 * c + 32 * g + 32],
                                             v[rows, p, 4 * j + g, 4 * oct_ + c, :], start=True, stop=True)
                last.then_inc(o_full, 1)

            def out_T(done, b, i):
                pe.wait_ge(o_done, done(4, b, i))
                pe.wait_ge(pt_done, done(4, b, i))
                for c in range(4):
                    last = pe.transpose(bank_t[:, 128 * c:128 * c + 128], o[:, i % 2, 128 * c:128 * c + 128], ident)
                last.then_inc(ot_full, 1)

            def ffn(done, b, step, before):
                before()
                if step == 0:
                    pe.wait_ge(ot_done, done(4, b, 3))
                    for c in range(PAIRS):
                        last = pe.matmul(bank_m[:, 0:SEQ], wo[:, c, :], oT[:, c, :], start=(c == 0), stop=(c == PAIRS - 1))
                elif step in (1, 2):
                    if step == 1:
                        pe.wait_ge(fs_done, done(2, b, 1))
                    else:
                        pe.wait_ge(fq_done, done(1, b, 0))
                    last = pe.matmul(bank_m[:, 0:SEQ], mean_w, (fs if step == 1 else fq)[:, :], start=True, stop=True)
                elif step < 6:
                    c0, n = CHUNKS[step - 3]
                    if step == 3:
                        pe.wait_ge(fn_done, done(1, b, 0))
                    pe.matmul(bank_m[0:n, 0:SEQ], w1[:, c0:c0 + n], fn[:, :], start=True, stop=True)
                    last = pe.matmul(bank_m[0:n, SEQ:2 * SEQ], w1[:, FFN + c0:FFN + c0 + n], fn[:, :], start=True, stop=True)
                else:
                    pe.wait_ge(hid_done, done(3, b, 2))
                    for c, (_, n) in enumerate(CHUNKS):
                        last = pe.matmul(bank_m[:, 0:SEQ], w2[0:n, c, :], hid[0:n, c, :], start=(c == 0), stop=(c == 2))
                last.then_inc(f_full, 1)

            for stack in range(stacks):
                if stack:
                    mid_pe(pe)
                for c in range(TOKENS // 512):
                    for h in range(2):
                        if h == 0:
                            if c:
                                pe.wait_ge(pro_dve, (stack * 4 + c) * 2)
                            elif stack:
                                pe.wait_ge(fin_dve, 8)
                            else:
                                pe.wait_ge(x_in, 16)
                            src = x[:, c * 512:c * 512 + 512]
                        else:
                            pe.wait_ge(pro_act, (stack * 4 + c) * 3 + 1)
                            src = sq[:, 0, :, :].rearrange("p a t -> p (a t)")
                        pe.matmul(bank_c[:, :], mean_w, src, start=True, stop=True).then_inc(pro_pe, 1)
                pe.wait_ge(pro_dve, (stack * 4 + 4) * 2)
                pe.wait_ge(setup, 5 + 3 * stack)
                with pe.Fori(0, layers) as layer:
                    done = Count(layer, stack)
                    nth = layer_of(layer, stack)
                    used = {"m": None}

                    def m_free():
                        if used["m"] is None:
                            pe.wait_ge(x_ready, done.x(7))
                        else:
                            pe.wait_ge(*used["m"])

                    def V(b, w):
                        values(done, b, w, m_free)
                        used["m"] = (v_done, done(8, b, w))

                    def F(b, step):
                        ffn(done, b, step, m_free)
                        used["m"] = [(x1_done, done(1, b, 0)), (fc_done, done(1, b, 0)), (fl_done, done(1, b, 0)),
                                     (hid_done, done(3, b, 0)), (hid_done, done(3, b, 1)), (hid_done, done(3, b, 2)),
                                     (x_ready, done.x(b + BATCH))][step]

                    for b in range(-1, BATCH + 1):
                        nxt = b + 1 if b + 1 < BATCH else None
                        att = 0 <= b < BATCH
                        prev = b - 1 if b >= 1 else None
                        for i in range(4):
                            if att:
                                scores(done, b, i)
                            if prev is not None and i > 0:
                                F(prev, [None, 1, 3, 5][i])
                            if att and i:
                                out_T(done, b, i - 1)
                            elif i == 0 and prev is not None:
                                out_T(done, prev, 3)
                            if nxt is not None:
                                if i == 0:
                                    pe.wait_ge(xl_done, done(1, nxt, 0))
                                    if nxt == 0:
                                        pe.wait_ge(wv_in, nth * 16 + 16)
                                if nxt == 0:
                                    pe.wait_ge(wl_done, nth * NCONV + (2 if i == 0 else 4) + 1)
                                project(done, nxt, i, 0, 0, bank_c, c_full)
                                project(done, nxt, i, 0, 1, bank_r, r_full)
                                V(nxt, 2 * i)
                                if nxt == 0:
                                    pe.wait_ge(wl_done, nth * NCONV + 4 + 1)
                                project(done, nxt, i, 1, 0, bank_c, c_full)
                                project(done, nxt, i, 1, 1, bank_r, r_full)
                                V(nxt, 2 * i + 1)
                                norms(done, nxt, i)
                            if att:
                                probs_T(done, b, i)
                            if prev is not None:
                                if i == 0:
                                    if prev == 0:
                                        pe.wait_ge(wo_in, nth * 16 + 16)
                                        pe.wait_ge(w1_in, nth * 48 + 48)
                                F(prev, [0, 2, 4, 6][i])
                            if nxt is not None:
                                spread_norms(done, nxt, i)
                            if att:
                                attend(done, b, i)

        @block.scalar
        def _(act):
            for s, per in ((sq_done, 8), (log_done, 4), (rnorm_done, 4), (v_done, 8), (prob_done, 4), (pt_done, 4),
                           (ot_done, 4), (xh_done, 1), (fq_done, 1), (fl_done, 1), (fr_done, 1), (gelu_done, 3)):
                act.sem_inc(s, 2 * per)
            act.wait_ge(const_in, 32)
            act.preload_act_table_set("natural_log_exp_and_others")
            for stack in range(stacks):
                if stack:
                    mid_act(act)
                for c in range(TOKENS // 512):
                    at = stack * 4 + c
                    flat = sq[:, 0, :, :].rearrange("p a t -> p (a t)")
                    act.wait_ge(pro_dve, at * 2 + 1)
                    act.activation(flat, x[:, c * 512:c * 512 + 512], ACT.Square).then_inc(pro_act, 1)
                    act.wait_ge(pro_pe, at * 2 + 2)
                    act.activation(diff[:, 0, :], bank_c[:, :], ACT.Ln, bias=eps).then_inc(pro_act, 1)
                    act.wait_ge(pro_act, at * 3 + 2)
                    act.activation(diff[:, 1, :], diff[:, 0, :], ACT.Exp, scale=-0.5).then_inc(pro_act, 1)

                with act.Fori(0, layers) as layer:
                    done = Count(layer, stack)
                    nth = layer_of(layer, stack)

                    def to_xh(b):
                        act.wait_ge(xs_done, done(2, b, 1))
                        act.wait_ge(r_full, done(8, b - 2, 7))
                        act.activation(xh[:, b % 2, :], xs[:, b % 2, PAD:], ACT.Copy).then_inc(xh_done, 1)

                    def square(b, u, kind):
                        act.wait_ge(c_full, done(8, b, 2 * u + kind))
                        if kind == 0:
                            act.wait_ge(nsum_full, done(4, b, u - 1))
                        act.activation(sq[:, kind, :, :], bank_c[:, :].rearrange("p (a t) -> p a t", a=2), ACT.Square)\
                            .then_inc(sq_done, 1)

                    def values_out(b, w):
                        act.wait_ge(v_full, done(8, b, w))
                        act.wait_ge(o_full, done(4, b - 2, 3))
                        act.activation(v[:, b % 2, w, :, 0:HEAD_DIM], bank_m[:, :].rearrange("p (c d) -> p c d", d=HEAD_DIM),
                                       ACT.Copy).then_inc(v_done, 1)

                    def rnorms(b, u):
                        act.wait_ge(clamp_done, done(4, b, u))
                        act.activation(nlog[:, :], nsum[:, :], ACT.Ln).then_inc(log_done, 1)
                        act.wait_ge(log_done, done(4, b, u))
                        act.wait_ge(rqt_full, done(4, b, u - 1))
                        act.activation(rnorm[:, :], nlog[:, :], ACT.Exp, bias=norm_bias, scale=-0.5).then_inc(rnorm_done, 1)

                    def exps(b, i):
                        act.wait_ge(scaled_done, done(4, b, i))
                        act.wait_ge(pt_full, done(4, b, i - 2))
                        act.activation(prob[:, i % 2, :], diff[:, i % 2, :], ACT.Exp).then_inc(prob_done, 1)

                    def probs_out(b, i):
                        act.wait_ge(pt_full, done(4, b, i))
                        act.wait_ge(o_full, done(4, b, i - 2))
                        act.activation(probT[:, i % 2, :], bank_t[:, :], ACT.Copy).then_inc(pt_done, 1)

                    def out_out(b, i):
                        act.wait_ge(ot_full, done(4, b, i))
                        act.wait_ge(f_full, done(7, b - 1, 0))
                        j, oct_ = i // 2, i % 2
                        act.activation(oT[:, 4 * oct_:4 * oct_ + 4, 128 * j:128 * j + 128],
                                       bank_t[:, :].rearrange("p (c t) -> p c t", c=4), ACT.Copy).then_inc(ot_done, 1)

                    def gelu(b, c):
                        n = CHUNKS[c][1]
                        act.wait_ge(f_full, done(7, b, 3 + c))
                        act.wait_ge(hid_done, done(3, b, c - 1))
                        act.activation(gl[0:n, :], bank_m[0:n, SEQ:2 * SEQ], ACT.Gelu, bias=small[0:n, 10 + c:11 + c])\
                            .then_inc(gelu_done, 1)

                    def fvar(b):
                        act.wait_ge(f_full, done(7, b, 2))
                        act.activation(fl[:, :], bank_m[:, 0:SEQ], ACT.Ln, bias=eps).then_inc(fl_done, 1)
                        act.wait_ge(fl_done, done(1, b, 0))
                        act.wait_ge(fm_done, done(1, b - 1, 0))
                        act.activation(fr[:, :], fl[:, :], ACT.Exp, scale=-0.5).then_inc(fr_done, 1)

                    act.preload_act_table_set("natural_log_exp_and_others")
                    act.wait_ge(r_full, done(8, -1, 7))
                    for c in range(NCONV):
                        act.wait_ge(raw_in[c % 2], nth * 32 + 16 * (c // 2 + 1))
                        act.activation(wh[:, c * INNER:(c + 1) * INNER], raw[:, c % 2, :], ACT.Copy).then_inc(wh_done, 1)
                        if c == 0:
                            to_xh(0)
                    for b in range(-1, BATCH + 1):
                        nxt = b + 1 if b + 1 < BATCH else None
                        att = 0 <= b < BATCH
                        prev = b - 1 if b >= 1 else None
                        for i in range(4):
                            if prev is not None and i == 2:
                                gelu(prev, 0)
                            if prev is not None and i == 1:
                                act.wait_ge(fc_done, done(1, prev, 0))
                                act.wait_ge(f_full, done(7, prev - 1, 2))
                                act.activation(fq[:, :], fc[:, :], ACT.Square).then_inc(fq_done, 1)
                            if att and i:
                                out_out(b, i - 1)
                            elif i == 0 and prev is not None:
                                out_out(prev, 3)
                            if nxt is not None:
                                square(nxt, i, 0)
                                values_out(nxt, 2 * i)
                                square(nxt, i, 1)
                                values_out(nxt, 2 * i + 1)
                            if att:
                                exps(b, i)
                            if nxt is not None:
                                rnorms(nxt, i)
                            if att:
                                probs_out(b, i)
                            if prev is not None:
                                if i == 1:
                                    fvar(prev)
                                if i == 2:
                                    gelu(prev, 1)
                                    gelu(prev, 2)
                                    act.preload_act_table_set("natural_log_exp_and_others")
                            if i == 1 and b + 2 < BATCH:
                                to_xh(b + 2)

        @block.vector
        def _(dve):
            for s, per in ((prod_done, 16), (clamp_done, 4), (rq_done, 4), (kn_done, 4), (max_done, 4), (diff_done, 4),
                           (rsum_done, 4), (o_done, 4), (xl_done, 1), (x1_done, 1), (fs_done, 2), (fc_done, 1),
                           (fm_done, 1), (fn_done, 1), (hid_done, 3), (xs_done, 2)):
                dve.sem_inc(s, 2 * per)
            dve.sem_inc(wl_done, 1)
            dve.wait_ge(const_in, 32)
            dve.tensor_copy(identb[:, :], ident).then_inc(setup, 1)
            dve.tensor_copy(mask[:, :, :], maskf[:, :].rearrange("p (f n) -> p f n", f=2)).then_inc(setup, 1)
            dve.wait_ge(setup, 2)
            for stack in range(stacks):
                if stack:
                    mid_dve(dve)
                    dve.wait_ge(coef_done, NCH + 3)
                    dve.wait_ge(rows_done, 2 * (NCH + 3))
                    dve.wait_ge(gram_done, NCH + 3)
                    dve.wait_ge(gram_in, 16 * BATCH * (NCH + 1))
                    dve.wait_ge(fin_act, 4)
                dve.memset(xs[:, :, 0:PAD + 1], 0.0).then_inc(setup, 1)
                dve.memset(fs[:, 0:1], 0.0).then_inc(setup, 1)
                dve.memset(v[:, :, :, :, HEAD_DIM:VW], 1.0).then_inc(setup, 1)
                dve.wait_ge(setup, 5 + 3 * stack)
                for c in range(TOKENS // 512):
                    at = stack * 4 + c
                    xc = x[:, c * 512:c * 512 + 512]
                    dve.wait_ge(pro_pe, at * 2 + 1)
                    if c == 0:
                        dve.wait_ge(*((x2_out, 16) if stack else (x_in, 16)))
                    dve.tensor_tensor(xc, xc, bank_c[:, :], ALU.subtract).then_inc(pro_dve, 1)
                    dve.wait_ge(pro_act, at * 3 + 3)
                    dve.wait_ge(pro_dve, at * 2 + 1)
                    dve.tensor_tensor(xc, xc, diff[:, 1, :], ALU.mult).then_inc(pro_dve, 1)
                dve.wait_ge(pro_dve, (stack * 4 + 4) * 2)
                dve.sem_inc(x_ready, BATCH)

                with dve.Fori(0, layers) as layer:
                    done = Count(layer, stack)
                    nth = layer_of(layer, stack)

                    def shift_tokens(b):
                        dve.wait_ge(x_ready, done.x(b))
                        dve.wait_ge(v_full, done(8, b - 2, 7))
                        dve.wait_ge(xl_done, done(1, b - 2, 0))
                        p = b % 2
                        dve.tensor_copy(xs[0:64, p, PAD:], x[0:64, SEQ * b:SEQ * b + SEQ]).then_inc(xs_done, 1)
                        dve.tensor_copy(xs[64:128, p, PAD + 1:], x[64:128, SEQ * b:SEQ * b + SEQ - 1]).then_inc(xs_done, 1)

                    def to_xl(b):
                        dve.wait_ge(xh_done, done(1, b, 0))
                        dve.tensor_tensor(xl[:, b % 2, :], xs[:, b % 2, PAD:], xh[:, b % 2, :].bitcast(F32), ALU.subtract)\
                            .then_inc(xl_done, 1)

                    def product(b, u, kind, which):
                        bank, full = ((bank_c, c_full), (bank_r, r_full))[which]
                        dve.wait_ge(full, done(8, b, 2 * u + kind))
                        if which == 0:
                            dve.wait_ge(sq_done, done(8, b, 2 * u + kind))
                            dve.wait_ge((qadd_done, kadd_done)[kind], done(4, b, u - 1))
                        table = rots[:, 2 * kind + which, :].unsqueeze(1).to_broadcast([128, 2, SEQ])
                        dve.tensor_tensor(prod[:, 2 * kind + which, :, :], bank[:, :].rearrange("p (a t) -> p a t", a=2),
                                          table, ALU.mult).then_inc(prod_done, 1)

                    def clamp(b, u):
                        dve.wait_ge(nsum_full, done(4, b, u))
                        dve.wait_ge(log_done, done(4, b, u - 1))
                        dve.tensor_scalar(nsum[:, :], bank_c[0:64, 0:SEQ], NORM_FLOOR, LN_SHIFT, ALU.max, ALU.mult)\
                            .then_inc(clamp_done, 1)

                    def norms_out(b, u):
                        dve.wait_ge(spread_full, done(4, b, u))
                        dve.wait_ge(kadd_done, done(4, b, u))
                        ku = k[:, b % 2, 2 * u:2 * u + 2, :]
                        dve.tensor_tensor(ku, ku, bank_r[:, :].rearrange("p (a t) -> p a t", a=2), ALU.mult)\
                            .then_inc(kn_done, 1)
                        dve.wait_ge(rqt_full, done(4, b, u))
                        if u == 0:
                            dve.wait_ge(scaled_done, done(4, b - 2, 3))
                        dve.tensor_copy(rq[:, b % 2, :, 4 * u:4 * u + 4],
                                        bank_c[:, SEQ:SEQ + 64].rearrange("p (j h) -> p j h", j=2)[:, :, 0:4])\
                            .then_inc(rq_done, 1)

                    def shift_scores(b, i):
                        half = 256 * (i % 2)
                        s4 = bank_s[:, :].rearrange("p (e n) -> p e n", e=2)[:, :, half:half + 256]\
                            .rearrange("p e (c k) -> p e c k", c=4)
                        m = smax[:, i % 2, :].rearrange("p (e c) -> p e c", e=2)
                        dve.wait_ge(s_full, done(4, b, i))
                        dve.tensor_reduce(m, s4, AX.X, ALU.max).then_inc(max_done, 1)
                        dve.wait_ge(max_done, done(4, b, i))
                        dve.wait_ge(prob_done, done(4, b, i - 2))
                        d = diff[:, i % 2, :].rearrange("p (c e k) -> p e c k", c=4, e=2)
                        for e in range(2):
                            last = dve.tensor_tensor(d[:, e, :, :], s4[:, e, :, :],
                                                     m[:, e, :].unsqueeze(2).to_broadcast([128, 4, 64]), ALU.subtract)
                        last.then_inc(diff_done, 1)

                    def out_norm(b, i):
                        dve.wait_ge(o_full, done(4, b, i))
                        o4 = bank_o[:, :].rearrange("p (e n) -> p e n", e=2)[:, :, 0:4 * VW]\
                            .rearrange("p e (c d) -> p e c d", c=4)
                        r = rsum[:, :].rearrange("p (e c) -> p e c", e=2)
                        dve.wait_ge(o_done, done(4, b, i - 1))
                        dve.reciprocal(r, o4[:, :, :, HEAD_DIM]).then_inc(rsum_done, 1)
                        dve.wait_ge(rsum_done, done(4, b, i))
                        dve.wait_ge(ot_full, done(4, b, i - 2))
                        dst = o[:, i % 2, :].rearrange("p (c e d) -> p e c d", c=4, e=2)
                        for e in range(2):
                            last = dve.tensor_tensor(dst[:, e, :, :], o4[:, e, :, 0:HEAD_DIM],
                                                     r[:, e, :].unsqueeze(2).to_broadcast([128, 4, HEAD_DIM]), ALU.mult)
                        last.then_inc(o_done, 1)

                    def ffn(b, step):
                        xb = x[:, SEQ * b:SEQ * b + SEQ]
                        dve.wait_ge(f_full, done(7, b, step))
                        if step == 0:
                            dve.tensor_tensor(xb, xb, bank_m[:, 0:SEQ], ALU.add).then_inc(x1_done, 1)
                            dve.wait_ge(x1_done, done(1, b, 0))
                            dve.tensor_copy(fs[0:64, :], xb[0:64, :]).then_inc(fs_done, 1)
                            dve.tensor_copy(fs[64:128, 1:], xb[64:128, 0:SEQ - 1]).then_inc(fs_done, 1)
                        elif step == 1:
                            dve.wait_ge(fs_done, done(2, b, 1))
                            dve.tensor_tensor(fc[:, :], fs[:, :], bank_m[:, 0:SEQ], ALU.subtract).then_inc(fc_done, 1)
                        elif step == 2:
                            dve.wait_ge(fr_done, done(1, b, 0))
                            dve.tensor_tensor(fc[:, :], fc[:, :], fr[:, :], ALU.mult).then_inc(fm_done, 1)
                            dve.wait_ge(fm_done, done(1, b, 0))
                            dve.tensor_scalar(fn[:, :], fc[:, :], small[:, 4:5], small[:, 5:6], ALU.mult, ALU.add)\
                                .then_inc(fn_done, 1)
                        elif step < 6:
                            c, n = step - 3, CHUNKS[step - 3][1]
                            dve.wait_ge(gelu_done, done(3, b, c))
                            dve.scalar_tensor_tensor(out=hid[0:n, c, :], in0=bank_m[0:n, 0:SEQ], scalar=small[0:n, 7 + c:8 + c],
                                                     in1=gl[0:n, :], op0=ALU.add, op1=ALU.mult).then_inc(hid_done, 1)
                        else:
                            dve.scalar_tensor_tensor(out=xb, in0=bank_m[:, 0:SEQ], scalar=small[:, 6:7], in1=xb,
                                                     op0=ALU.add, op1=ALU.add).then_inc(x_ready, 1)

                    shift_tokens(0)
                    dve.wait_ge(small_in, nth * 16 + 16)
                    for t in range(4):
                        dve.tensor_scalar(rots[:, t, :], rot[:, t, :], small[:, t:t + 1], None, ALU.mult).then_inc(rots_done, 1)
                    for c in range(NCONV):
                        dve.wait_ge(wh_done, nth * NCONV + c + 1)
                        sec = slice(c * INNER, (c + 1) * INNER)
                        dve.tensor_tensor(wl[:, sec], raw[:, c % 2, :], wh[:, sec].bitcast(F32), ALU.subtract)\
                            .then_inc(wl_done, 1)
                        if c == 0:
                            to_xl(0)
                    dve.wait_ge(rots_done, nth * 4 + 4)
                    for b in range(-1, BATCH + 1):
                        nxt = b + 1 if b + 1 < BATCH else None
                        att = 0 <= b < BATCH
                        prev = b - 1 if b >= 1 else None
                        for i in range(4):
                            if i == 0 and b + 2 < BATCH:
                                shift_tokens(b + 2)
                            if att:
                                shift_scores(b, i)
                            if prev is not None and i > 0:
                                ffn(prev, [None, 1, 3, 5][i])
                            if nxt is not None:
                                for kind in range(2):
                                    for which in range(2):
                                        product(nxt, i, kind, which)
                                clamp(nxt, i)
                            if prev is not None:
                                ffn(prev, [0, 2, 4, 6][i])
                            if nxt is not None:
                                norms_out(nxt, i)
                            if att:
                                out_norm(b, i)
                            if i == 1 and b + 2 < BATCH:
                                to_xl(b + 2)

            dve.wait_ge(x_ready, BATCH * (LAYERS + 1) * (stacks - 1) + BATCH * (layers + 1))
            for c in range(4):
                cols = slice(512 * c, 512 * c + 512)
                dve.wait_ge(xo_in, 16 * c + 16)
                dve.scalar_tensor_tensor(out=x[:, cols], in0=x[:, cols], scalar=0.5, in1=xo[:, :], op0=ALU.mult, op1=ALU.add)\
                    .then_inc(end_dve, 1)

        @block.gpsimd
        def _(pool):
            for s, per in ((scaled_done, 4), (qadd_done, 4), (kadd_done, 4)):
                pool.sem_inc(s, 2 * per)
            pool.wait_ge(setup, 5)
            for stack in range(stacks):
                if stack:
                    mid_pool(pool)
                with pool.Fori(0, layers) as layer:
                    done = Count(layer, stack)

                    def scale_scores(b, i):
                        pool.wait_ge(diff_done, done(4, b, i))
                        if i < 2:
                            pool.wait_ge(rq_done, done(4, b, 3))
                        d = diff[:, i % 2, :].rearrange("p (h k) -> p h k", k=64)
                        r = rq[:, b % 2, i // 2, 8 * (i % 2):8 * (i % 2) + 8].unsqueeze(2).to_broadcast([128, 8, 64])
                        pool.tensor_tensor(d, d, r, ALU.mult).then_inc(scaled_done, 1)

                    def rotate(b, u, kind):
                        pool.wait_ge(prod_done, done(16, b, 4 * u + 2 * kind + 1))
                        pool.wait_ge(s_full, done(4, b - 2, 3))
                        dst = (q, k)[kind][:, b % 2, 2 * u:2 * u + 2, :]
                        pool.tensor_tensor(dst, prod[:, 2 * kind, :, :], prod[:, 2 * kind + 1, :, :], ALU.add)\
                            .then_inc((qadd_done, kadd_done)[kind], 1)

                    for b in range(-1, BATCH + 1):
                        for i in range(4):
                            if 0 <= b < BATCH:
                                scale_scores(b, i)
                            if b + 1 < BATCH:
                                rotate(b + 1, i, 0)
                                rotate(b + 1, i, 1)
    return nc


def layout(inputs):
    a = {n: np.asarray(v) for n, v in inputs.items()}
    half = HEAD_DIM // 2
    wqkv = a["L0_ffn_Wqkv"]

    def swapped(w, axis):
        parts = np.split(w, w.shape[axis] // half, axis)
        return np.concatenate([parts[i ^ 1] for i in range(len(parts))], axis)

    wq, wk, wv = np.split(wqkv, 3, -1)
    w_qk = np.concatenate([wq, swapped(wq, 2), wk, swapped(wk, 2)], -1)
    qs, ks = a["L0_ffn_q_scale"], a["L0_ffn_k_scale"]
    cols = [np.concatenate([c, c], 1) for c in (qs, swapped(qs, 1), ks, swapped(ks, 1))]
    cols += [a["L0_ffn_ln_g"], a["L0_ffn_ln_b"], a["L0_ffn_b2"]]
    b1 = a["L0_ffn_b1"]
    for base in (0, FFN):
        for c0, n in CHUNKS:
            part = np.zeros((LAYERS, 128), np.float32)
            part[:, :n] = b1[:, base + c0:base + c0 + n]
            cols.append(part)
    smalls = np.stack(cols, -1)
    consts, mask = tables()
    return {
        "xT": a["L0_attn_x"].transpose(2, 0, 1).reshape(DIM, TOKENS), "w_qk": w_qk, "w_v": wv,
        "w_o": a["L0_ffn_Wo"], "w_1": a["L0_ffn_W1"], "w_2": a["L0_ffn_W2"], "smalls": smalls,
        "mem_w": np.concatenate([a["L0_attn_Wk"].T, a["L0_attn_Wq"].T, a["L0_attn_Wv"].T, a["L0_attn_Wout"].T,
                                 a["L0_attn_norm_weight"][:, None], np.pad(a["L0_attn_eta"], (0, DIM - MEM))[:, None]], 1),
        "consts": consts, "maskc": mask,
    }


def kernel(**inputs):
    import concourse.bacc as bacc
    from concourse.bass_utils import run_bass_kernel_spmd

    nc = bacc.Bacc("TRN2", target_bir_lowering=False, num_devices=1)
    arrays, args = {}, []
    for name, a in layout(inputs).items():
        a = np.ascontiguousarray(a)
        arrays[f"in_{name}"] = a
        args.append(nc.dram_tensor(f"in_{name}", a.shape, mybir.dt.from_np(a.dtype), kind="ExternalInput").ap())
    args.append(nc.dram_tensor("out", (DIM, TOKENS), F32, kind="ExternalOutput").ap())
    build(nc, *args)
    r = run_bass_kernel_spmd(nc, [arrays], core_ids=[0])
    return r.results[0]["out"].reshape(DIM, BATCH, SEQ).transpose(1, 2, 0)
```

```python
from contextlib import ExitStack

import numpy as np

import concourse.bass as bass
from concourse import mybir
from concourse.alu_op_type import AluOpType as ALU

ACT = mybir.ActivationFunctionType
AX = mybir.AxisListType
F32 = mybir.dt.float32
F32R = mybir.dt.float32r
BF16 = mybir.dt.bfloat16

BATCH, SEQ, DIM = 8, 256, 128
LAYERS, HEADS, HEAD_DIM, WINDOW = 6, 16, 64, 32
INNER = HEADS * HEAD_DIM
PAIRS = HEADS // 2
UNITS = PAIRS // 2
FFN = int(DIM * 4 * 2 / 3)
CHUNKS = [(0, 128), (128, 128), (256, FFN - 256)]
TOKENS = BATCH * SEQ
WINDOWS = SEQ // WINDOW
PAD = WINDOW
VW = HEAD_DIM + 1
MASKED = -1e30
NORM_FLOOR = 1e-24
LN_SHIFT = 2.0 ** 20
SMALLS = 13
EPS = 1e-5


def tables():
    half = np.arange(0, HEAD_DIM, 2, dtype=np.float32)
    inv_freq = (1.0 / 10000.0 ** (half / HEAD_DIM)).astype(np.float32)
    t = np.arange(SEQ, dtype=np.float32)
    freqs = t[:, None] * inv_freq[None, :]
    freqs = np.concatenate([freqs, freqs], -1)
    base = (half + 0.4 * HEAD_DIM) / (1.4 * HEAD_DIM)
    power = (t - SEQ // 2) / (WINDOW // 2)
    scale = base[None, :] ** power[:, None]
    scale = np.concatenate([scale, scale], -1)
    sign = np.where(np.arange(HEAD_DIM) < HEAD_DIM // 2, -1.0, 1.0)
    cos, sin = np.cos(freqs), np.sin(freqs) * sign
    rot = np.stack([cos * scale, sin * scale, cos / scale, sin / scale], 0)
    rot = np.concatenate([rot, rot], 2).transpose(2, 0, 1)
    mask = np.zeros((2, 128, 2 * WINDOW), np.float32)
    for first in range(2):
        for q in range(128):
            g, i = divmod(q, WINDOW)
            for j in range(WINDOW):
                if j < i or (first == 0 and g == 0):
                    mask[first, q, j] = MASKED
                if j > i:
                    mask[first, q, WINDOW + j] = MASKED
    mask = np.tile(mask.transpose(1, 0, 2)[:, :, None, :], (1, 1, 4, 1))
    ident = np.eye(128, dtype=np.float32)
    heads = np.zeros((128, 2, 32), np.float32)
    for a in range(2):
        for e in range(2):
            heads[64 * e:64 * e + 64, a, 2 * a + e] = 1.0
    spread = np.zeros((128, 2, 128), np.float32)
    for a in range(2):
        for e in range(2):
            spread[32 + 2 * a + e, a, 64 * e:64 * e + 64] = 1.0
    bias = np.zeros((128, 4), np.float32)
    bias[0:32, 0] = np.log(8.0 * LN_SHIFT ** 0.5)
    bias[32:64, 0] = np.log(LN_SHIFT ** 0.5)
    bias[:, 1] = EPS
    bias[:, 2] = EPS_RMS
    bias[:, 3] = 1.0
    mean = np.full((128, 128), 1.0 / DIM, np.float32)
    at = np.arange(128)
    picks = np.concatenate([at[:, None] % STEPS == np.arange(STEPS), at[:, None] // STEPS == np.arange(BATCH)], 1)
    f = np.concatenate([rot.reshape(128, -1), ident, heads.reshape(128, -1), spread.reshape(128, -1), bias, mean, picks.astype(np.float32)], 1)
    return np.ascontiguousarray(f.astype(np.float32)), np.ascontiguousarray(mask.reshape(128, -1))


MEM = 64
STEPS = 16
STEPS1 = STEPS + 1
MEM_SIZE = MEM * DIM
EPS_RMS, ETA_MIN = 1e-6, 1e-6
MEM_COLS = 2 * MEM + 2 * DIM + 2
GRAM = 2 * STEPS1 + STEPS

ROT0, IDENT0 = 0, 4 * SEQ
HEADS0 = IDENT0 + 128
SPREAD0 = HEADS0 + 64
BIAS0 = SPREAD0 + 256
MEAN0 = BIAS0 + 4
STEP0 = MEAN0 + 128
SEQUENCE0 = STEP0 + STEPS
CONST_COLS = SEQUENCE0 + BATCH


class Count:

    def __init__(self, layer, stack):
        self.layer, self.stack = layer, stack

    def __call__(self, per, b, k):
        return self.layer * (per * BATCH) + (per * (BATCH * LAYERS * self.stack + b + 2) + k + 1)

    def x(self, b):
        return self.layer * BATCH + (BATCH * (LAYERS + 1) * self.stack + b + 1)


def build(nc, xT, w_qk, w_v, w_o, w_1, w_2, smalls, mem_w, consts, maskc, out, stacks=2, layers=LAYERS):
    x2 = nc.dram_tensor("x2", (DIM, TOKENS), F32, kind="Internal").ap()
    ctx = ExitStack()
    with ctx:
        def sb(name, shape, dt=F32):
            return ctx.enter_context(nc.sbuf_tensor(name, shape, dt))

        def ps(name, cols):
            return ctx.enter_context(nc.psum_tensor(name, [128, cols], F32))

        def sem(name):
            return ctx.enter_context(nc.semaphore(name))

        const = sb("const", [128, CONST_COLS])
        maskf = sb("maskf", [128, 512])
        mask = sb("mask", [128, 2, 256], BF16)
        identb = sb("identb", [128, 128], BF16)
        rot = const[:, ROT0:IDENT0].rearrange("p (k t) -> p k t", k=4)
        ident = const[:, IDENT0:HEADS0]
        head_sum = const[:, HEADS0:SPREAD0].rearrange("p (a m) -> p a m", a=2)
        spread = const[:, SPREAD0:BIAS0].rearrange("p (a m) -> p a m", a=2)
        norm_bias = const[0:64, BIAS0:BIAS0 + 1]
        eps = const[:, BIAS0 + 1:BIAS0 + 2]
        eps_rms = const[:, BIAS0 + 2:BIAS0 + 3]
        ones_col = const[:, BIAS0 + 3:BIAS0 + 4]
        mean_w = const[:, MEAN0:STEP0]
        step_mask = const[:, STEP0:SEQUENCE0]
        sequence_mask = const[:, SEQUENCE0:CONST_COLS]

        x = sb("x", [128, TOKENS])
        xo = sb("xo", [128, 512])
        memw = sb("memw", [128, MEM_COLS])
        wk_T, wq_T = memw[:, 0:MEM], memw[:, MEM:2 * MEM]
        wv_T, wout_T = memw[:, 2 * MEM:2 * MEM + DIM], memw[:, 2 * MEM + DIM:2 * MEM + 2 * DIM]
        norm_w, eta_in = memw[:, MEM_COLS - 2:MEM_COLS - 1], memw[0:MEM, MEM_COLS - 1:MEM_COLS]
        ctx2 = ExitStack()

        def sb(name, shape, dt=F32):
            return ctx2.enter_context(nc.sbuf_tensor(name, shape, dt))

        xs = sb("xs", [128, 2, PAD + SEQ])
        xh = sb("xh", [128, 2, SEQ], F32R)
        xl = sb("xl", [128, 2, SEQ], F32R)
        raw = sb("raw", [128, 2, INNER])
        wh = sb("wh", [128, 4 * INNER], F32R)
        wl = sb("wl", [128, 4 * INNER], F32R)
        wv = sb("wv", [128, INNER])
        wv_next = sb("wv_next", [128, INNER])
        wo = sb("wo", [128, PAIRS, DIM])
        w1 = sb("w1", [128, 2 * FFN])
        w2 = sb("w2", [128, 3, DIM])
        small = sb("small", [128, SMALLS - 4])
        qk_scales = sb("qk_scales", [128, 4])
        rots = sb("rots", [128, 4, SEQ])
        q = sb("q", [128, 2, PAIRS, SEQ])
        k = sb("k", [128, 2, PAIRS, SEQ])
        v = sb("v", [128, 2, WINDOWS, PAIRS, VW])
        prod = sb("prod", [128, 4, 2, SEQ])
        sq = sb("sq", [128, 2, 2, SEQ])
        nsum = sb("nsum", [64, SEQ])
        nlog = sb("nlog", [64, SEQ])
        rnorm = sb("rnorm", [64, SEQ])
        rq = sb("rq", [128, 2, 2, HEADS])
        smax = sb("smax", [128, 2, PAIRS])
        diff = sb("diff", [128, 2, 512])
        prob = sb("prob", [128, 2, 512])
        probT = sb("probT", [128, 2, 512])
        rsum = sb("rsum", [128, 8])
        o = sb("o", [128, 2, 512])
        oT = sb("oT", [128, PAIRS, SEQ])
        fs = sb("fs", [128, SEQ])
        fc = sb("fc", [128, SEQ])
        fq = sb("fq", [128, SEQ])
        fl = sb("fl", [128, SEQ])
        fr = sb("fr", [128, SEQ])
        fn = sb("fn", [128, SEQ])
        gl = sb("gl", [128, SEQ])
        hid = sb("hid", [128, 3, SEQ])

        bank_c = ps("bank_c", 512)
        bank_r = ps("bank_r", 512)
        bank_m = ps("bank_m", 512)
        bank_t = ps("bank_t", 512)
        bank_s = ps("bank_s", 1024)
        bank_o = ps("bank_o", 1024)

        c_full, r_full = sem("c_full"), sem("r_full")
        nsum_full = sem("nsum_full")
        rqt_full, spread_full = sem("rqt_full"), sem("spread_full")
        v_full, f_full = sem("v_full"), sem("f_full")
        s_full, pt_full, o_full, ot_full = sem("s_full"), sem("pt_full"), sem("o_full"), sem("ot_full")
        sq_done = sem("sq_done")
        log_done, rnorm_done = sem("log_done"), sem("rnorm_done")
        v_done, prob_done, pt_done, ot_done = sem("v_done"), sem("prob_done"), sem("pt_done"), sem("ot_done")
        xh_done = sem("xh_done")
        fq_done, fl_done, fr_done, gelu_done = sem("fq_done"), sem("fl_done"), sem("fr_done"), sem("gelu_done")
        wh_done, wv_done = sem("wh_done"), sem("wv_done")
        attend_on = sem("attend_on")
        xs_done = sem("xs_done")
        prod_done = sem("prod_done")
        clamp_done, rq_done, kn_done = sem("clamp_done"), sem("rq_done"), sem("kn_done")
        max_done, diff_done, rsum_done, o_done = sem("max_done"), sem("diff_done"), sem("rsum_done"), sem("o_done")
        xl_done = sem("xl_done")
        x1_done, fs_done, fc_done, fm_done, fn_done, hid_done = (
            sem("x1_done"), sem("fs_done"), sem("fc_done"), sem("fm_done"), sem("fn_done"), sem("hid_done"))
        x_ready = sem("x_ready")
        wl_done, rots_done = sem("wl_done"), sem("rots_done")
        scaled_done, qadd_done, kadd_done = sem("scaled_done"), sem("qadd_done"), sem("kadd_done")
        raw_in = [sem("raw_in0"), sem("raw_in1")]
        wv_in, wo_in, w1_in, w2_in = sem("wv_in"), sem("wo_in"), sem("w1_in"), sem("w2_in")
        small_in, scales_in = sem("small_in"), sem("scales_in")
        const_in, x_in, setup, out_done = sem("const_in"), sem("x_in"), sem("setup"), sem("out_done")
        pro_pe, pro_act, pro_dve = sem("pro_pe"), sem("pro_act"), sem("pro_dve")

        ctx2.close()

        def chunk_buffers():
            alloc = ExitStack()

            def sb(name, shape):
                return alloc.enter_context(nc.sbuf_tensor(name, shape, F32))

            return dict(
                x1=sb("x1", [128, TOKENS]), yn=sb("yn", [128, TOKENS]), msq=sb("msq", [128, 512]), mlog=sb("mlog", [128, 512]),
                mrs=sb("mrs", [128, 512]), neg=sb("neg", [64, 2, 512]),
                kT=sb("kT", [64, BATCH, SEQ + STEPS]), qT=sb("qT", [64, BATCH, SEQ]), vT=sb("vT", [128, BATCH, SEQ + STEPS]),
                eta=sb("eta", [64, 1]), ke=sb("ke", [64, 2, BATCH, 2 * STEPS + 1]), vc=sb("vc", [128, 2, BATCH, STEPS1]),
                ek_rows=sb("ek_rows", [STEPS1, 2, BATCH, MEM]), v_rows=sb("v_rows", [STEPS1, 2, BATCH, DIM]),
                gram_s=sb("gram_s", [STEPS1, BATCH * GRAM]), gram_b=sb("gram_b", [BATCH, 2, STEPS1, GRAM]),
                coef=sb("coef", [BATCH, 2, STEPS, STEPS1, STEPS1]), ab=sb("ab", [BATCH, STEPS, STEPS1]),
                lin=sb("lin", [BATCH, 2, STEPS, STEPS1]), sqr=sb("sqr", [BATCH, 2, STEPS, STEPS1]),
                kap2=sb("kap2", [BATCH, 2, STEPS]), sigh=sb("sigh", [BATCH, 2, STEPS]), cvec=sb("cvec", [BATCH, STEPS1]),
                m=sb("m", [64, BATCH, DIM]), yt=sb("yt", [128, BATCH, 2 * STEPS]), ysq=sb("ysq", [128, 2, BATCH, STEPS]),
                gp_s=sb("gp_s", [STEPS1, BATCH * STEPS]), by_step=sb("by_step", [128, 2, STEPS]),
                gram_m=sb("gram_m", [BATCH, STEPS1, STEPS1]), quad=sb("quad", [BATCH, STEPS1]), 
                u2=sb("u2", [BATCH, 1]), pn=sb("pn", [BATCH, 1]), s1=sb("s1", [BATCH, 1]), s2=sb("s2", [BATCH, 1]),
                s3=sb("s3", [BATCH, 1]), cross=sb("cross", [BATCH, 1]), nd=sb("nd", [BATCH, 1]),
                tau=sb("tau", [BATCH, 1]), rt2=sb("rt2", [BATCH, 1]), lv=sb("lv", [BATCH, STEPS1]), lw=sb("lw", [BATCH, STEPS1]),
                w=sb("w", [BATCH, STEPS]), rho=sb("rho", [BATCH, 1]), itau=sb("itau", [BATCH, 1]), nrho=sb("nrho", [BATCH, 1]),
                cf=sb("cf", [BATCH, STEPS1]), diag=sb("diag", [BATCH, BATCH]), cf_s=sb("cf_s", [STEPS1, BATCH]),
                scaled=sb("scaled", [STEPS1, BATCH, MEM]), mem_T=sb("mem_T", [128, 512]), ones8=sb("ones8", [BATCH, MEM]),
                half=sb("half", [BATCH, 1]),
            ), alloc

        A, alloc = chunk_buffers()
        alloc.close()
        g = type("Buffers", (), A)
        NCH = SEQ // STEPS
        mp, ma, mv, mq = sem("mp"), sem("ma"), sem("mv"), sem("mq")
        x1_in, memw_in, x2_out, xo_in = sem("x1_in"), sem("memw_in"), sem("x2_out"), sem("xo_in")
        end_dve = sem("end_dve")
        prep_in, rows_full, gram_full, y_full, gp_full, hp_full, cf_full, n_full = (
            sem("prep_in"), sem("rows_full"), sem("gram_full"), sem("y_full"), sem("gp_full"), sem("hp_full"),
            sem("cf_full"), sem("n_full"))
        rows_done, gram_done, gp_done, root_done = sem("rows_done"), sem("gram_done"), sem("gp_done"), sem("root_done")
        coef_step, coef_done, gram_in = sem("coef_step"), sem("coef_done"), sem("gram_in")
        start_full, by_step_done = sem("start_full"), sem("by_step_done")
        dve_step, want_root, yt_done, ysq_done, cf_done, scaled_done2, m_done = (
            sem("dve_step"), sem("want_root"), sem("yt_done"), sem("ysq_done"), sem("cf_done"), sem("scaled2"), sem("m_done"))
        fin_pe, fin_act, fin_dve = sem("fin_pe"), sem("fin_act"), sem("fin_dve")
        ROOTS = 2 * STEPS
        GP0 = BATCH * STEPS
        SUMS0 = GP0 + STEPS * STEPS1
        ALL_X = BATCH * (layers + 1)

        class Chunk:

            def __init__(self, it, p):
                self.it, self.p = it, p

            def __call__(self, per, k, ahead=0):
                return self.it * (2 * per) + (per * (self.p + ahead + 2) + k + 1)

        def mid_sp(sp):
            sp.wait_ge(x_ready, ALL_X)
            for c in range(4):
                sp.dma_start(g.x1[:, 512 * c:512 * c + 512], xT[:, 512 * c:512 * c + 512]).then_inc(x1_in, 16)
            sp.wait_ge(mq, 1)

            def gram(done):
                sp.wait_ge(gram_done, done(1, 0))
                for b in range(BATCH):
                    sp.dma_start(g.gram_b[b:b + 1, done.p, :, :], g.gram_s[:, GRAM * b:GRAM * b + GRAM]).then_inc(gram_in, 16)

            gram(Chunk(0, 0))
            with sp.Fori(0, NCH // 2) as it:
                for p in range(2):
                    d = Chunk(it, p)
                    sp.wait_ge(gram_done, d(1, 0, 1))
                    for b in range(BATCH):
                        sp.dma_start(g.gram_b[b:b + 1, 1 - p, :, :], g.gram_s[:, GRAM * b:GRAM * b + GRAM]).then_inc(gram_in, 16)
            sp.wait_ge(fin_dve, 8)
            sp.dma_start(x2, x[:, :]).then_inc(x2_out, 16)
            sp.wait_ge(x2_out, 16)

        def mid_pe(pe):
            for s, per in ((rows_full, 2), (gram_full, 1), (y_full, 1), (gp_full, 1), (hp_full, 1), (start_full, 1), (cf_full, 1), (n_full, 1)):
                pe.sem_inc(s, 2 * per)
            pe.wait_ge(memw_in, 16)
            for c in range(4):
                cols = slice(512 * c, 512 * c + 512)
                pe.wait_ge(mv, 8 * c + 1)
                pe.matmul(bank_c[:, :], mean_w, g.x1[:, cols], start=True, stop=True).then_inc(mp, 1)
                for k_ in (1, 4):
                    pe.wait_ge(ma, 9 * c + k_)
                    pe.matmul(bank_c[:, :], mean_w, g.msq[:, :], start=True, stop=True).then_inc(mp, 1)
                pe.wait_ge(mv, 8 * c + 4)
                pe.matmul(bank_r[0:64, :], wk_T, g.yn[:, cols], start=True, stop=True).then_inc(mp, 1)
                pe.matmul(bank_t[0:64, :], wq_T, g.yn[:, cols], start=True, stop=True).then_inc(mp, 1)
                pe.matmul(bank_m[:, :], wv_T, g.yn[:, cols], start=True, stop=True).then_inc(mp, 1)

            def prep(done, ahead):
                p = (done.p + ahead) % 2
                pe.wait_ge(prep_in, done(3, 2, ahead))
                pe.wait_ge(rows_done, done(2, 1, ahead - 1))
                for b in range(BATCH):
                    last = pe.transpose(bank_o[0:STEPS, DIM * b:DIM * b + DIM], g.vc[:, p, b, 0:STEPS], ident)
                last.then_inc(rows_full, 1)
                for b in range(BATCH):
                    last = pe.transpose(bank_t[0:STEPS, MEM * b:MEM * b + MEM], g.ke[:, p, b, STEPS:2 * STEPS], ident[0:64, 0:64])
                last.then_inc(rows_full, 1)
                pe.wait_ge(gram_done, done(1, 0, ahead - 1))
                for b in range(BATCH):
                    pe.matmul(bank_m[0:STEPS1, GRAM * b + 2 * STEPS + 1:GRAM * b + GRAM], g.vc[:, p, b, :], g.vc[:, p, b, :],
                              start=True, stop=True)
                    last = pe.matmul(bank_m[0:STEPS1, GRAM * b:GRAM * b + 2 * STEPS + 1], g.ke[:, p, b, STEPS:], g.ke[:, p, b, :],
                                     start=True, stop=True)
                last.then_inc(gram_full, 1)

            pe.wait_ge(mv, 32 + 16)
            prep(Chunk(0, 0), 0)
            with pe.Fori(0, NCH // 2) as it:
                for p in range(2):
                    done = Chunk(it, p)
                    pe.wait_ge(m_done, done(1, 0, -1))
                    for b in range(BATCH):
                        last = pe.matmul(bank_c[:, 2 * STEPS * b:2 * STEPS * (b + 1)], g.m[:, b, :], g.ke[:, p, b, 0:2 * STEPS],
                                         start=True, stop=True)
                    last.then_inc(y_full, 1)
                    pe.wait_ge(yt_done, done(1, 0))
                    for b in range(BATCH):
                        last = pe.matmul(bank_r[0:STEPS1, STEPS * b:STEPS * (b + 1)], g.vc[:, p, b, :], g.yt[:, b, 0:STEPS],
                                         start=True, stop=True)
                    last.then_inc(gp_full, 1)
                    pe.wait_ge(ysq_done, done(2, 1))
                    pe.wait_ge(rows_done, done(2, 1))
                    for r in range(2):
                        last = pe.matmul(bank_t[:, r:r + 1], g.ysq[:, r, :, :].rearrange("p b j -> p (b j)"), ones_col,
                                         start=True, stop=True)
                    last.then_inc(hp_full, 1)
                    pe.wait_ge(by_step_done, done(1, 0))
                    pe.wait_ge(gp_done, done(1, 0))
                    pe.matmul(bank_r[0:BATCH, SUMS0:SUMS0 + 2 * STEPS], sequence_mask, g.by_step[:, :, :].rearrange("p r j -> p (r j)"),
                              start=True, stop=True)
                    gp = g.gp_s[:, :].rearrange("l (b j) -> l j b", b=BATCH)
                    for j in range(STEPS):
                        last = pe.transpose(bank_r[0:BATCH, GP0 + STEPS1 * j:GP0 + STEPS1 * (j + 1)], gp[:, j, :],
                                            ident[0:STEPS1, 0:STEPS1])
                    last.then_inc(start_full, 1)
                    prep(done, 1)
                    pe.wait_ge(cf_done, done(2, 1))
                    pe.matmul(bank_c[0:64, 272:272 + BATCH], g.ones8[:, :], g.diag[:, :], start=True, stop=True)
                    pe.transpose(bank_c[0:STEPS1, 256:256 + BATCH], g.cf[:, :], ident[0:BATCH, 0:BATCH]).then_inc(cf_full, 1)
                    pe.wait_ge(scaled_done2, done(1, 0))
                    pe.wait_ge(rows_done, done(2, 1))
                    for b in range(BATCH):
                        last = pe.matmul(bank_s[0:64, DIM * b:DIM * (b + 1)], g.scaled[:, b, :], g.v_rows[:, p, b, :],
                                         start=True, stop=True)
                    last.then_inc(n_full, 1)
            done = Chunk(NCH // 2, 0)
            pe.wait_ge(m_done, done(1, 0, -1))
            for c in range(4):
                if c:
                    pe.wait_ge(fin_act, c)
                for b in range(2):
                    last = pe.matmul(bank_c[:, SEQ * b:SEQ * (b + 1)], g.m[:, 2 * c + b, :], g.qT[:, 2 * c + b, :],
                                     start=True, stop=True)
                last.then_inc(fin_pe, 1)
                pe.wait_ge(fin_act, c + 1)
                if c:
                    pe.wait_ge(fin_dve, 2 * c)
                pe.matmul(bank_r[:, :], wout_T, g.mem_T[:, :], start=True, stop=True).then_inc(fin_pe, 1)

        def mid_act(act):
            for s, per in ((rows_done, 2), (gram_done, 1), (gp_done, 1), (root_done, ROOTS)):
                act.sem_inc(s, 2 * per)
            act.preload_act_table_set("natural_log_exp_and_others")
            for c in range(4):
                cols = slice(512 * c, 512 * c + 512)
                for r in range(2):
                    act.wait_ge(mv, 8 * c + 2 + r)
                    act.activation(g.msq[:, :], x[:, cols], ACT.Square).then_inc(ma, 1)
                    act.wait_ge(mp, 6 * c + 2 + r)
                    act.activation(g.mlog[:, :], bank_c[:, :], ACT.Ln, bias=(eps, eps_rms)[r]).then_inc(ma, 1)
                    act.wait_ge(ma, 9 * c + 3 * r + 2)
                    if r:
                        act.wait_ge(mv, 8 * c + 3)
                    act.activation(g.mrs[:, :], g.mlog[:, :], ACT.Exp, scale=-0.5).then_inc(ma, 1)
                for r in range(2):
                    act.wait_ge(mv, 8 * c + 5 + r)
                    act.activation(g.neg[:, r, :], g.neg[:, r, :], ACT.Exp).then_inc(ma, 1)
                act.wait_ge(mp, 6 * c + 6)
                act.activation(g.vT[:, 2 * c:2 * c + 2, 0:SEQ], bank_m[:, :].rearrange("p (b t) -> p b t", b=2), ACT.Copy)\
                    .then_inc(ma, 1)
            act.preload_act_table_set("sqrt_and_others")

            def prep_out(done, ahead, part, first=False):
                p = (done.p + ahead) % 2
                if part < 2:
                    act.wait_ge(rows_full, done(2, 0, ahead))
                    four = slice(4 * part, 4 * part + 4)
                    last = act.activation(g.v_rows[0:STEPS, p, four, :],
                                          bank_o[0:STEPS, 512 * part:512 * part + 512].rearrange("p (b f) -> p b f", b=4), ACT.Copy)
                    if part == 1:
                        last.then_inc(rows_done, 1)
                elif part == 2:
                    act.wait_ge(rows_full, done(2, 1, ahead))
                    act.activation(g.ek_rows[0:STEPS, p, :, :], bank_t[0:STEPS, :].rearrange("p (b f) -> p b f", b=BATCH), ACT.Copy)\
                        .then_inc(rows_done, 1)
                else:
                    act.wait_ge(gram_full, done(1, 0, ahead))
                    if not first:
                        act.wait_ge(gram_in, 16 * BATCH + done.it * (2 * 16 * BATCH) + (16 * BATCH * (done.p + ahead - 1)))
                    act.activation(g.gram_s[:, :], bank_m[0:STEPS1, 0:BATCH * GRAM], ACT.Copy).then_inc(gram_done, 1)

            act.wait_ge(mv, 32 + 16)
            for part in range(4):
                prep_out(Chunk(0, 0), 0, part, True)

            with act.Fori(0, NCH // 2) as it:
                for p in range(2):
                    done = Chunk(it, p)
                    act.wait_ge(gp_full, done(1, 0))
                    act.activation(g.gp_s[:, :], bank_r[0:STEPS1, 0:BATCH * STEPS], ACT.Copy).then_inc(gp_done, 1)
                    for i in range(STEPS):
                        act.wait_ge(want_root, done(ROOTS, 2 * i))
                        act.activation(g.w[:, i:i + 1], g.cross[:, :], ACT.Sqrt, bias=g.s2[:, :], scale=-1.0).then_inc(root_done, 1)
                        if 1 <= i <= 4:
                            prep_out(done, 1, i - 1)
                        act.wait_ge(want_root, done(ROOTS, 2 * i + 1))
                        act.activation(g.rt2[:, :], g.tau[:, :], ACT.Sqrt, scale=4.0).then_inc(root_done, 1)
            for c in range(4):
                act.wait_ge(fin_pe, 2 * c + 1)
                if c:
                    act.wait_ge(fin_pe, 2 * c)
                act.activation(g.mem_T[:, :], bank_c[:, :], ACT.Copy).then_inc(fin_act, 1)

        def mid_pool(pool):
            for s, per in ((prep_in, 3), (coef_done, 1)):
                pool.sem_inc(s, 2 * per)
            pool.wait_ge(mv, 32 + 16)
            pool.sem_inc(mq, 1)

            PER = 12

            def prep(done, ahead, at, base):
                p = (done.p + ahead) % 2
                n = [0]

                def step(ins):
                    ins.then_inc(coef_step, 1)
                    n[0] += 1
                    pool.wait_ge(coef_step, base + n[0])

                pool.wait_ge(m_done, done(1, 0, ahead - 2))
                kc = g.kT[:, :, bass.ds(at, STEPS)]
                pool.tensor_copy(g.ke[:, p, :, 0:STEPS], kc).then_inc(prep_in, 1)
                pool.tensor_tensor(g.ke[:, p, :, STEPS:2 * STEPS], kc, g.eta[:, 0:1].unsqueeze(2).to_broadcast([MEM, BATCH, STEPS]),
                                   ALU.mult).then_inc(prep_in, 1)
                pool.wait_ge(prep_in, done(3, 1, ahead))
                pool.tensor_copy(g.vc[:, p, :, 0:STEPS], g.vT[:, :, bass.ds(at, STEPS)]).then_inc(prep_in, 1)
                pool.wait_ge(prep_in, done(3, 2, ahead))
                pool.wait_ge(gram_in, 16 * BATCH + done.it * (2 * 16 * BATCH) + 16 * BATCH * (done.p + ahead))
                gb = g.gram_b[:, p, :, :]
                kk, ee, vv = gb[:, 0:STEPS, 0:STEPS], gb[:, 0:STEPS, STEPS:2 * STEPS + 1], gb[:, 0:STEPS, 2 * STEPS + 1:]
                vdiag = gb.rearrange("b i m -> b (i m)")[:, 2 * STEPS + 1:2 * STEPS + 1 + (STEPS - 1) * (GRAM + 1) + 1:GRAM + 1]
                co = g.coef[:, p, :, :, :]
                full = [BATCH, STEPS, STEPS1, STEPS]
                step(pool.tensor_tensor(co[:, :, :, 0:STEPS], kk.unsqueeze(2).to_broadcast(full),
                                        vv.unsqueeze(3).to_broadcast(full), ALU.mult))
                step(pool.tensor_tensor(g.ab[:, :, :], ee, vv, ALU.mult))
                step(pool.tensor_tensor(co[:, :, :, STEPS], g.ab[:, :, :], g.cvec[:, :].unsqueeze(1).to_broadcast([BATCH, STEPS, STEPS1]),
                                        ALU.mult))
                step(pool.tensor_tensor(g.lin[:, p, :, 0:STEPS], kk, kk, ALU.add))
                step(pool.tensor_tensor(g.sqr[:, p, :, 0:STEPS], kk, kk, ALU.mult))
                step(pool.tensor_tensor(g.sqr[:, p, :, 0:STEPS], g.sqr[:, p, :, 0:STEPS],
                                        vdiag.unsqueeze(2).to_broadcast([BATCH, STEPS, STEPS]), ALU.mult))
                abdiag = g.ab[:, :, :].rearrange("b i l -> b (i l)")[:, 0:(STEPS - 1) * (STEPS1 + 1) + 1:STEPS1 + 1]
                step(pool.tensor_tensor(g.sqr[:, p, :, STEPS], abdiag, g.cvec[:, STEPS:].to_broadcast([BATCH, STEPS]), ALU.mult))
                step(pool.tensor_tensor(g.kap2[:, p, :], gb[:, STEPS, 0:STEPS], gb[:, STEPS, 0:STEPS], ALU.add))
                pool.tensor_tensor(g.sigh[:, p, :], gb[:, 0:STEPS, GRAM - 1], g.half[:, :].to_broadcast([BATCH, STEPS]), ALU.mult).then_inc(coef_done, 1)
                pool.wait_ge(coef_done, done(1, 0, ahead))
                return n[0]

            per = prep(Chunk(0, 0), 0, 0, 0)
            with pool.Fori(0, NCH // 2) as it:
                for p in range(2):
                    prep(Chunk(it, p), 1, it * (2 * STEPS) + STEPS * (p + 1), it * (2 * per) + per * (p + 1))

        def mid_dve(dve):
            for s, per in ((want_root, ROOTS), (yt_done, 1), (ysq_done, 2), (by_step_done, 1), (cf_done, 2), (scaled_done2, 1), (m_done, 1)):
                dve.sem_inc(s, 2 * per)
            for c in range(4):
                cols = slice(512 * c, 512 * c + 512)
                dve.wait_ge(x_ready, ALL_X)
                dve.wait_ge(x1_in, 64)
                dve.scalar_tensor_tensor(out=g.x1[:, cols], in0=x[:, cols], scalar=0.5, in1=g.x1[:, cols], op0=ALU.mult, op1=ALU.add)\
                    .then_inc(mv, 1)
                dve.wait_ge(mp, 6 * c + 1)
                dve.wait_ge(mv, 8 * c + 1)
                dve.tensor_tensor(x[:, cols], g.x1[:, cols], bank_c[:, :], ALU.subtract).then_inc(mv, 1)
                dve.wait_ge(ma, 9 * c + 3)
                dve.wait_ge(mv, 8 * c + 2)
                dve.tensor_tensor(x[:, cols], x[:, cols], g.mrs[:, :], ALU.mult).then_inc(mv, 1)
                dve.wait_ge(ma, 9 * c + 6)
                dve.wait_ge(mv, 8 * c + 3)
                dve.scalar_tensor_tensor(out=g.yn[:, cols], in0=x[:, cols], scalar=norm_w, in1=g.mrs[:, :], op0=ALU.mult, op1=ALU.mult)\
                    .then_inc(mv, 1)
                for r, bank in ((0, bank_r), (1, bank_t)):
                    dve.wait_ge(mp, 6 * c + 4 + r)
                    dve.tensor_scalar(g.neg[:, r, :], bank[0:64, :], 0.0, None, ALU.min).then_inc(mv, 1)
                for r, (bank, dst) in enumerate(((bank_r, g.kT), (bank_t, g.qT))):
                    dve.wait_ge(ma, 9 * c + 7 + r)
                    dve.scalar_tensor_tensor(out=dst[:, 2 * c:2 * c + 2, 0:SEQ], in0=bank[0:64, :].rearrange("p (b t) -> p b t", b=2),
                                             scalar=0.0, in1=g.neg[:, r, :].rearrange("p (b t) -> p b t", b=2),
                                             op0=ALU.max, op1=ALU.add).then_inc(mv, 1)
            dve.wait_ge(ma, 36)
            dve.scalar_tensor_tensor(out=g.eta[:, :], in0=eta_in, scalar=-1.0, in1=eta_in, op0=ALU.mult, op1=ALU.max).then_inc(mv, 1)
            dve.wait_ge(mv, 32 + 1)
            dve.tensor_scalar(g.eta[:, :], g.eta[:, :], ETA_MIN, None, ALU.max).then_inc(mv, 1)
            dve.memset(g.kT[:, :, SEQ:], 0.0).then_inc(mv, 1)
            dve.memset(g.vT[:, :, SEQ:], 0.0).then_inc(mv, 1)
            dve.memset(g.ke[:, :, :, 2 * STEPS:], 1.0).then_inc(mv, 1)
            dve.memset(g.vc[:, :, :, STEPS:], 1.0).then_inc(mv, 1)
            dve.memset(g.ek_rows[:, :, :, :], 1.0).then_inc(mv, 1)
            dve.memset(g.v_rows[:, :, :, :], 1.0).then_inc(mv, 1)
            dve.memset(g.lin[:, :, :, STEPS:], 1.0).then_inc(mv, 1)
            dve.memset(g.cvec[:, 0:STEPS], 2.0 / MEM_SIZE).then_inc(mv, 1)
            dve.memset(g.cvec[:, STEPS:], 1.0 / MEM_SIZE).then_inc(mv, 1)
            dve.memset(g.m[:, :, :], 0.0).then_inc(mv, 1)
            dve.memset(g.itau[:, :], 0.0).then_inc(mv, 1)
            dve.memset(g.nd[:, :], 0.0).then_inc(mv, 1)
            dve.memset(g.ones8[:, :], 1.0).then_inc(mv, 1)
            dve.memset(g.half[:, :], -0.5).then_inc(mv, 1)
            dve.wait_ge(mv, 32 + 16)

            def chunk(done, base):
                p, n = done.p, [0]

                def step(ins):
                    ins.then_inc(dve_step, 1)
                    n[0] += 1
                    return n[0]

                def need(k):
                    dve.wait_ge(dve_step, base + k)

                def stt(out, in0, scalar, in1, op0, op1):
                    return dve.scalar_tensor_tensor(out=out, in0=in0, scalar=scalar, in1=in1, op0=op0, op1=op1)

                dve.wait_ge(y_full, done(1, 0))
                dve.tensor_copy(g.yt[:, :, :], bank_c[:, 0:2 * STEPS * BATCH].rearrange("p (b j) -> p b j", b=BATCH)).then_inc(yt_done, 1)
                dve.wait_ge(yt_done, done(1, 0))
                dve.tensor_tensor(g.ysq[:, 0, :, :], g.yt[:, :, 0:STEPS], g.yt[:, :, 0:STEPS], ALU.mult).then_inc(ysq_done, 1)
                dve.tensor_tensor(g.ysq[:, 1, :, :], g.yt[:, :, STEPS:], g.vc[:, p, :, 0:STEPS], ALU.mult).then_inc(ysq_done, 1)
                step(stt(g.quad[:, STEPS:], g.nd[:, :], -1.0, g.itau[:, :], ALU.mult, ALU.mult))
                step(dve.memset(g.gram_m[:, STEPS, STEPS:], 0.0))
                step(dve.memset(g.tau[:, :], 1.0))
                step(dve.memset(g.rt2[:, :], 2.0))
                dve.wait_ge(hp_full, done(1, 0))
                dve.tensor_tensor(g.by_step[:, :, :], step_mask.unsqueeze(1).to_broadcast([128, 2, STEPS]),
                                  bank_t[:, 0:2].unsqueeze(2).to_broadcast([128, 2, STEPS]), ALU.mult).then_inc(by_step_done, 1)
                dve.wait_ge(start_full, done(1, 0))
                step(dve.tensor_copy(g.gram_m[:, :, 0:STEPS],
                                     bank_r[0:BATCH, GP0:SUMS0].rearrange("b (j l) -> b l j", l=STEPS1)))
                step(dve.tensor_copy(g.quad[:, 0:STEPS], bank_r[0:BATCH, SUMS0:SUMS0 + STEPS]))
                ready = step(dve.tensor_scalar(g.gram_m[:, 0:STEPS, STEPS], bank_r[0:BATCH, SUMS0 + STEPS:SUMS0 + 2 * STEPS],
                                               2.0 / MEM_SIZE, None, ALU.mult))
                dve.wait_ge(coef_done, done(1, 0))
                mean = g.gram_m[:, STEPS, STEPS:]
                need(ready)
                for i in range(STEPS + 1):
                    now = slice(i, i + 1)
                    if i < STEPS:
                        u = step(dve.tensor_tensor(g.u2[:, :], mean, g.kap2[:, p, now], ALU.mult))
                    if i:
                        nd = step(stt(g.nd[:, :], mean, mean, g.quad[:, STEPS:], ALU.mult, ALU.subtract))
                    if i < STEPS:
                        need(u)
                        step(stt(g.s1[:, :], g.u2[:, :], float(DIM // 4), g.gram_m[:, STEPS, now], ALU.mult, ALU.subtract))
                    if i:
                        need(nd)
                        stt(g.tau[:, :], g.tau[:, :], EPS, g.nd[:, :], ALU.mult, ALU.subtract).then_inc(want_root, 1)
                    if i == STEPS:
                        break
                    step(stt(g.pn[:, :], g.sigh[:, p, now], g.u2[:, :], g.gram_m[:, i, now], ALU.mult, ALU.add))
                    dve.wait_ge(want_root, done(ROOTS, 2 * i - 1))
                    vii = g.gram_b[:, p, i, 2 * STEPS + 1 + i:2 * STEPS + 2 + i]
                    need(step(stt(g.s3[:, :], g.tau[:, :], vii, g.quad[:, now], ALU.mult, ALU.add)))
                    need(step(stt(g.s2[:, :], g.s1[:, :], g.u2[:, :], g.s3[:, :], ALU.mult, ALU.add)))
                    dve.wait_ge(root_done, done(ROOTS, 2 * i - 1))
                    stt(g.cross[:, :], g.pn[:, :], g.rt2[:, :], g.s2[:, :], ALU.mult, ALU.min).then_inc(want_root, 1)
                    lv = step(dve.tensor_tensor(g.lv[:, :], g.lin[:, p, i, :], g.gram_m[:, i, :], ALU.mult))
                    if 1 <= i < STEPS - 1:
                        rest = slice(i + 1, STEPS)
                        lv = step(stt(g.gram_m[:, rest, :], g.coef[:, p, i - 1, rest, :], g.w[:, i - 1:i], g.gram_m[:, rest, :],
                                      ALU.mult, ALU.add))
                    dve.wait_ge(root_done, done(ROOTS, 2 * i))
                    need(lv)
                    w = g.w[:, now]
                    lw = step(stt(g.lw[:, :], g.sqr[:, p, i, :], w, g.lv[:, :], ALU.mult, ALU.add))
                    rows = slice(i + 1, STEPS1, max(1, STEPS - 1 - i))
                    step(stt(g.gram_m[:, rows, :], g.coef[:, p, i, rows, :], w, g.gram_m[:, rows, :], ALU.mult, ALU.add))
                    need(lw)
                    need(step(stt(g.quad[:, :], g.lw[:, :], w, g.quad[:, :], ALU.mult, ALU.add)))
                dve.wait_ge(want_root, done(ROOTS, ROOTS - 1))
                dve.wait_ge(root_done, done(ROOTS, ROOTS - 1))
                need(step(dve.reciprocal(g.rho[:, :], g.rt2[:, :])))
                step(dve.reciprocal(g.itau[:, :], g.tau[:, :]))
                need(step(dve.tensor_scalar(g.nrho[:, :], g.rho[:, :], 2.0, None, ALU.mult)))
                dve.tensor_scalar(g.cf[:, 0:STEPS], g.w[:, :], g.nrho[:, :], None, ALU.mult).then_inc(cf_done, 1)
                need(step(stt(g.cf[:, STEPS:], mean, -1.0, g.nrho[:, :], ALU.mult, ALU.mult)))
                dve.tensor_scalar(g.diag[:, :], ident[0:BATCH, 0:BATCH], g.nrho[:, :], None, ALU.mult).then_inc(cf_done, 1)
                dve.wait_ge(cf_full, done(1, 0))
                need(step(dve.tensor_copy(g.cf_s[:, :], bank_c[0:STEPS1, 256:256 + BATCH])))
                dve.wait_ge(rows_done, done(2, 1))
                dve.tensor_tensor(g.scaled[:, :, :], g.ek_rows[:, p, :, :], g.cf_s[:, :].unsqueeze(2).to_broadcast([STEPS1, BATCH, MEM]),
                                  ALU.mult).then_inc(scaled_done2, 1)
                need(step(dve.tensor_tensor(g.m[:, :, :], g.m[:, :, :], bank_c[0:64, 272:272 + BATCH].unsqueeze(2).to_broadcast([64, BATCH, DIM]),
                                            ALU.mult)))
                dve.wait_ge(n_full, done(1, 0))
                dve.tensor_tensor(g.m[:, :, :], g.m[:, :, :], bank_s[0:64, :].rearrange("p (b d) -> p b d", b=BATCH), ALU.add)\
                    .then_inc(m_done, 1)
                return n[0]

            per = 7 + 10 * STEPS + STEPS - 2 + 6
            with dve.Fori(0, NCH // 2) as it:
                for p in range(2):
                    used = chunk(Chunk(it, p), it * (2 * per) + per * p)
                    assert used == per, used
            for c in range(4):
                cols = slice(512 * c, 512 * c + 512)
                dve.wait_ge(fin_pe, 2 * c + 2)
                dve.tensor_tensor(x[:, cols], x[:, cols], bank_r[:, :], ALU.add).then_inc(fin_dve, 1)
                dve.wait_ge(fin_dve, 2 * c + 1)
                dve.tensor_tensor(x[:, cols], x[:, cols], g.x1[:, cols], ALU.add).then_inc(fin_dve, 1)

        block = ctx.enter_context(nc.Block())

        def layer_of(layer, stack):
            return layer + LAYERS * stack

        def roles(b, last):
            nxt = b + 1 if b + 1 < BATCH or not last else None
            return nxt, b >= 0 and (b < BATCH or not last), b - 1 if b >= 1 else None

        @block.sync
        def _(sp):
            sp.dma_start(x[:, :], xT).then_inc(x_in, 16)
            sp.dma_start(memw[:, :], mem_w).then_inc(memw_in, 16)
            sp.dma_start(const[:, :], consts).then_inc(const_in, 16)
            sp.dma_start(maskf[:, :], maskc).then_inc(const_in, 16)
            for stack in range(stacks):
                if stack:
                    mid_sp(sp)
                def project_weights(layer, n):
                    for c in range(UNITS):
                        if not isinstance(n, int) or n + c:
                            sp.wait_ge(wl_done, n * UNITS + c)
                        sp.dma_start(raw[:, c % 2, :], w_qk[layer, :, c * INNER:(c + 1) * INNER]).then_inc(raw_in[c % 2], 16)
                        if c == 1:
                            if not isinstance(n, int) or n:
                                sp.wait_ge(wv_done, n)
                            sp.dma_start(wv_next[:, :], w_v[layer]).then_inc(wv_in, 16)
                            if not isinstance(n, int) or n:
                                sp.wait_ge(rots_done, n * 4)
                            sp.dma_start(qk_scales[:, :], smalls[layer, :, 0:4]).then_inc(scales_in, 16)

                def ffn_weights(layer):
                    done = Count(layer, stack)
                    sp.wait_ge(f_full, done(7, -1, 0))
                    sp.dma_start(wo[:, :, :], w_o[layer].rearrange("(c p) n -> p c n", p=128)).then_inc(wo_in, 16)
                    sp.wait_ge(f_full, done(7, -1, 5))
                    sp.dma_start(w1[:, :], w_1[layer]).then_inc(w1_in, 16)
                    sp.wait_ge(f_full, done(7, -1, 6))
                    sp.dma_start(w2[:, 0:2, :], w_2[layer, 0:256, :].rearrange("(c p) n -> p c n", p=128)).then_inc(w2_in, 16)
                    sp.dma_start(w2[0:FFN - 256, 2, :], w_2[layer, 256:FFN, :]).then_inc(w2_in, 16)
                    sp.wait_ge(x_ready, done.x(7))
                    sp.dma_start(small[:, :], smalls[layer, :, 4:]).then_inc(small_in, 16)

                sp.wait_ge(setup, 5 + 3 * stack)
                project_weights(0, LAYERS * stack)
                if layers > 1:
                    with sp.Fori(0, layers - 1) as layer:
                        ffn_weights(layer)
                        project_weights(layer + 1, layer_of(layer, stack) + 1)
                ffn_weights(layers - 1)
            for c in range(4):
                cols = slice(512 * c, 512 * c + 512)
                if c:
                    sp.wait_ge(end_dve, c)
                sp.dma_start(xo[:, :], (x2 if stacks > 1 else xT)[:, cols]).then_inc(xo_in, 16)
            for c in range(4):
                cols = slice(512 * c, 512 * c + 512)
                sp.wait_ge(end_dve, c + 1)
                sp.dma_start(out[:, cols], x[:, cols]).then_inc(out_done, 16)
            sp.wait_ge(out_done, 64)

        @block.tensor
        def _(pe):
            for s, per in ((c_full, 8), (r_full, 8), (nsum_full, 4), (rqt_full, 4), (spread_full, 4), (v_full, 8),
                           (f_full, 7), (s_full, 4), (pt_full, 4), (o_full, 4), (ot_full, 4)):
                pe.sem_inc(s, 2 * per)
            pe.wait_ge(const_in, 32)
            pe.wait_ge(setup, 5)

            def project(done, b, u, kind, which, bank, full):
                p = b % 2
                n = 2 * u + kind
                if kind == 0:
                    if which == 0:
                        pe.wait_ge(rq_done, done(4, b, u - 1))
                    else:
                        pe.wait_ge(kn_done, done(4, b, u - 1))
                else:
                    pe.wait_ge(prod_done, done(16, b, 4 * u + which))
                    if which == 0:
                        pe.wait_ge(sq_done, done(8, b, 2 * u))
                for a in range(2):
                    at = u * INNER + ((2 * kind + which) * 2 + a) * 128
                    w = slice(at, at + 128)
                    dst = bank[:, a * SEQ:(a + 1) * SEQ]
                    pe.matmul(dst, wh[:, w], xh[:, p, :], start=True, stop=False)
                    pe.matmul(dst, wl[:, w], xh[:, p, :], start=False, stop=False)
                    last = pe.matmul(dst, wh[:, w], xl[:, p, :], start=False, stop=True)
                last.then_inc(full, 1)

            def values(done, b, w, before):
                p = b % 2
                before()
                for e in range(2):
                    last = pe.matmul(bank_m[64 * e:64 * e + 64, :], xs[:, p, w * WINDOW:w * WINDOW + 64],
                                     wv[:, :].rearrange("p (c e d) -> p e c d", e=2, d=HEAD_DIM)[:, e, :, :],
                                     start=True, stop=True)
                last.then_inc(v_full, 1)

            def norms(done, b, u):
                pe.wait_ge(sq_done, done(8, b, 2 * u + 1))
                pe.wait_ge(prod_done, done(16, b, 4 * u + 2))
                for a in range(2):
                    for kind in range(2):
                        last = pe.matmul(bank_c[32 * kind:32 * kind + 32, 0:SEQ], head_sum[:, a, :], sq[:, kind, a, :],
                                         start=(a == 0), stop=(a == 1))
                last.then_inc(nsum_full, 1)

            def spread_norms(done, b, u):
                pe.wait_ge(rnorm_done, done(4, b, u))
                pe.wait_ge(prod_done, done(16, b, 4 * u + 3))
                for a in range(2):
                    last = pe.matmul(bank_r[:, a * SEQ:(a + 1) * SEQ], spread[32:64, a, :], rnorm[32:64, :],
                                     start=True, stop=True)
                last.then_inc(spread_full, 1)
                for j in range(2):
                    last = pe.transpose(bank_c[:, SEQ + 32 * j:SEQ + 32 * j + 32], rnorm[0:32, 128 * j:128 * j + 128],
                                        ident[0:32, 0:32])
                last.then_inc(rqt_full, 1)

            def scores(done, b, i):
                p, j, oct_ = b % 2, i // 2, i % 2
                half = 256 * (i % 2)
                pe.wait_ge(kn_done, done(4, b, 2 * oct_ + 1))
                pe.wait_ge(qadd_done, done(4, b, 2 * oct_ + 1))
                pe.wait_ge(diff_done, done(4, b, i - 2))
                for e in range(2):
                    pe.matmul(bank_s[:, 512 * e + half:512 * e + half + 256], identb[:, :], mask[:, j, :],
                              start=True, stop=False, skip_group_check=True)
                for c in range(4):
                    for g in range(4):
                        t = 128 * j + WINDOW * g
                        lo = 0 if t == 0 else WINDOW
                        n = WINDOW + lo
                        for e in range(2):
                            rows = slice(64 * e, 64 * e + 64)
                            s0 = 512 * e + half + 64 * c + WINDOW - lo
                            last = pe.matmul(bank_s[32 * g:32 * g + 32, s0:s0 + n],
                                             q[rows, p, 4 * oct_ + c, t:t + WINDOW], k[rows, p, 4 * oct_ + c, t - lo:t + WINDOW],
                                             start=False, stop=True, skip_group_check=True)
                last.then_inc(s_full, 1)

            def probs_T(done, b, i):
                pe.wait_ge(prob_done, done(4, b, i))
                pe.wait_ge(ot_done, done(4, b, i - 1))
                for c in range(4):
                    last = pe.transpose(bank_t[:, 128 * c:128 * c + 128], prob[:, i % 2, 128 * c:128 * c + 128], ident)
                last.then_inc(pt_full, 1)

            def attend(done, b, i):
                p, j, oct_ = b % 2, i // 2, i % 2
                pe.wait_ge(pt_done, done(4, b, i))
                pe.wait_ge(v_done, done(8, b, 4 * j + 3))
                pe.wait_ge(o_done, done(4, b, i - 1))
                pe.sem_inc(attend_on, 1)
                for c in range(4):
                    for g in range(4):
                        for e in range(2):
                            rows = slice(64 * e, 64 * e + 64)
                            last = pe.matmul(bank_o[32 * g:32 * g + 32, 512 * e + VW * c:512 * e + VW * c + VW],
                                             probT[rows, i % 2, 128 * c + 32 * g:128 * c + 32 * g + 32],
                                             v[rows, p, 4 * j + g, 4 * oct_ + c, :], start=True, stop=True)
                last.then_inc(o_full, 1)

            def out_T(done, b, i):
                pe.wait_ge(o_done, done(4, b, i))
                pe.wait_ge(pt_done, done(4, b, i))
                for c in range(4):
                    last = pe.transpose(bank_t[:, 128 * c:128 * c + 128], o[:, i % 2, 128 * c:128 * c + 128], ident)
                last.then_inc(ot_full, 1)

            def ffn(done, b, step, before):
                before()
                if step == 0:
                    pe.wait_ge(ot_done, done(4, b, 3))
                    for c in range(PAIRS):
                        last = pe.matmul(bank_m[:, 0:SEQ], wo[:, c, :], oT[:, c, :], start=(c == 0), stop=(c == PAIRS - 1))
                elif step in (1, 2):
                    if step == 1:
                        pe.wait_ge(fs_done, done(2, b, 1))
                    else:
                        pe.wait_ge(fq_done, done(1, b, 0))
                    last = pe.matmul(bank_m[:, 0:SEQ], mean_w, (fs if step == 1 else fq)[:, :], start=True, stop=True)
                elif step < 6:
                    c0, n = CHUNKS[step - 3]
                    if step == 3:
                        pe.wait_ge(fn_done, done(1, b, 0))
                    pe.matmul(bank_m[0:n, 0:SEQ], w1[:, c0:c0 + n], fn[:, :], start=True, stop=True)
                    last = pe.matmul(bank_m[0:n, SEQ:2 * SEQ], w1[:, FFN + c0:FFN + c0 + n], fn[:, :], start=True, stop=True)
                else:
                    pe.wait_ge(hid_done, done(3, b, 2))
                    for c, (_, n) in enumerate(CHUNKS):
                        last = pe.matmul(bank_m[:, 0:SEQ], w2[0:n, c, :], hid[0:n, c, :], start=(c == 0), stop=(c == 2))
                last.then_inc(f_full, 1)

            for stack in range(stacks):
                if stack:
                    mid_pe(pe)
                for c in range(TOKENS // 512):
                    for h in range(2):
                        if h == 0:
                            if c:
                                pe.wait_ge(pro_dve, (stack * 4 + c) * 2)
                            elif stack:
                                pe.wait_ge(fin_dve, 8)
                            else:
                                pe.wait_ge(x_in, 16)
                            src = x[:, c * 512:c * 512 + 512]
                        else:
                            pe.wait_ge(pro_act, (stack * 4 + c) * 3 + 1)
                            src = sq[:, 0, :, :].rearrange("p a t -> p (a t)")
                        pe.matmul(bank_c[:, :], mean_w, src, start=True, stop=True).then_inc(pro_pe, 1)
                pe.wait_ge(pro_dve, (stack * 4 + 4) * 2)
                pe.wait_ge(setup, 5 + 3 * stack)
                def slots(layer, streams, last):
                    done = Count(layer, stack)
                    nth = layer_of(layer, stack)
                    used = {"m": None}

                    def m_free():
                        if used["m"] is None:
                            pe.wait_ge(x_ready, done.x(7))
                            if streams[0] == 1:
                                pe.wait_ge(v_done, done(8, 1, 7))
                        else:
                            pe.wait_ge(*used["m"])

                    def V(b, w):
                        values(done, b, w, m_free)
                        used["m"] = (v_done, done(8, b, w))

                    def F(b, step):
                        ffn(done, b, step, m_free)
                        used["m"] = [(x1_done, done(1, b, 0)), (fc_done, done(1, b, 0)), (fl_done, done(1, b, 0)),
                                     (hid_done, done(3, b, 0)), (hid_done, done(3, b, 1)), (hid_done, done(3, b, 2)),
                                     (x_ready, done.x(b + BATCH))][step]

                    for b in streams:
                        nxt, att, prev = roles(b, last)
                        for i in range(4):
                            if att:
                                scores(done, b, i)
                            if prev is not None and i > 0:
                                if prev == 0 and i == 2:
                                    pe.wait_ge(w1_in, nth * 16 + 16)
                                F(prev, [None, 1, 3, 5][i])
                            if nxt is not None:
                                if i == 0:
                                    pe.wait_ge(xl_done, done(1, nxt, 0))
                                if nxt % BATCH == 0:
                                    pe.wait_ge(wl_done, (nth + nxt // BATCH) * UNITS + i + 2)
                                project(done, nxt, i, 0, 0, bank_c, c_full)
                                project(done, nxt, i, 0, 1, bank_r, r_full)
                            if att and i:
                                out_T(done, b, i - 1)
                            elif i == 0 and prev is not None:
                                out_T(done, prev, 3)
                            if nxt is not None:
                                if nxt % BATCH == 0 and i == 0:
                                    pe.wait_ge(wv_done, nth + nxt // BATCH + 1)
                                V(nxt, 2 * i)
                                project(done, nxt, i, 1, 0, bank_c, c_full)
                                project(done, nxt, i, 1, 1, bank_r, r_full)
                                V(nxt, 2 * i + 1)
                            if att:
                                probs_T(done, b, i)
                            if nxt is not None:
                                norms(done, nxt, i)
                            if prev is not None:
                                if prev == 0 and i == 0:
                                    pe.wait_ge(wo_in, nth * 16 + 16)
                                if prev == 0 and i == 3:
                                    pe.wait_ge(w2_in, nth * 32 + 32)
                                F(prev, [0, 2, 4, 6][i])
                            if att:
                                attend(done, b, i)
                            if nxt is not None:
                                spread_norms(done, nxt, i)

                slots(0, range(-1, 1), False)
                if layers > 1:
                    with pe.Fori(0, layers - 1) as layer:
                        slots(layer, range(1, BATCH + 1), False)
                slots(layers - 1, range(1, BATCH + 1), True)

        @block.scalar
        def _(act):
            for s, per in ((sq_done, 8), (log_done, 4), (rnorm_done, 4), (v_done, 8), (prob_done, 4), (pt_done, 4),
                           (ot_done, 4), (xh_done, 1), (fq_done, 1), (fl_done, 1), (fr_done, 1), (gelu_done, 3)):
                act.sem_inc(s, 2 * per)
            act.wait_ge(const_in, 32)
            act.preload_act_table_set("natural_log_exp_and_others")
            for stack in range(stacks):
                if stack:
                    mid_act(act)
                for c in range(TOKENS // 512):
                    at = stack * 4 + c
                    flat = sq[:, 0, :, :].rearrange("p a t -> p (a t)")
                    act.wait_ge(pro_dve, at * 2 + 1)
                    act.activation(flat, x[:, c * 512:c * 512 + 512], ACT.Square).then_inc(pro_act, 1)
                    act.wait_ge(pro_pe, at * 2 + 2)
                    act.activation(diff[:, 0, :], bank_c[:, :], ACT.Ln, bias=eps).then_inc(pro_act, 1)
                    act.wait_ge(pro_act, at * 3 + 2)
                    act.activation(diff[:, 1, :], diff[:, 0, :], ACT.Exp, scale=-0.5).then_inc(pro_act, 1)

                def slots(layer, streams, last):
                    done = Count(layer, stack)
                    nth = layer_of(layer, stack)

                    def to_xh(b):
                        act.wait_ge(xs_done, done(2, b, 1))
                        act.wait_ge(r_full, done(8, b - 2, 7))
                        act.activation(xh[:, b % 2, :], xs[:, b % 2, PAD:], ACT.Copy).then_inc(xh_done, 1)

                    def square(b, u, kind):
                        act.wait_ge(c_full, done(8, b, 2 * u + kind))
                        if kind == 0:
                            act.wait_ge(nsum_full, done(4, b, u - 1))
                        act.activation(sq[:, kind, :, :], bank_c[:, :].rearrange("p (a t) -> p a t", a=2), ACT.Square)\
                            .then_inc(sq_done, 1)

                    def values_out(b, w):
                        act.wait_ge(v_full, done(8, b, w))
                        act.wait_ge(o_full, done(4, b - 2, 3))
                        act.activation(v[:, b % 2, w, :, 0:HEAD_DIM], bank_m[:, :].rearrange("p (c d) -> p c d", d=HEAD_DIM),
                                       ACT.Copy).then_inc(v_done, 1)

                    def rnorms(b, u):
                        act.wait_ge(clamp_done, done(4, b, u))
                        act.activation(nlog[:, :], nsum[:, :], ACT.Ln).then_inc(log_done, 1)
                        act.wait_ge(log_done, done(4, b, u))
                        act.wait_ge(rqt_full, done(4, b, u - 1))
                        act.activation(rnorm[:, :], nlog[:, :], ACT.Exp, bias=norm_bias, scale=-0.5).then_inc(rnorm_done, 1)

                    def exps(b, i):
                        act.wait_ge(scaled_done, done(4, b, i))
                        act.wait_ge(pt_full, done(4, b, i - 2))
                        act.activation(prob[:, i % 2, :], diff[:, i % 2, :], ACT.Exp).then_inc(prob_done, 1)

                    def probs_out(b, i):
                        act.wait_ge(pt_full, done(4, b, i))
                        act.wait_ge(o_full, done(4, b, i - 2))
                        act.activation(probT[:, i % 2, :], bank_t[:, :], ACT.Copy).then_inc(pt_done, 1)

                    def out_out(b, i):
                        act.wait_ge(ot_full, done(4, b, i))
                        act.wait_ge(f_full, done(7, b - 1, 0))
                        j, oct_ = i // 2, i % 2
                        act.activation(oT[:, 4 * oct_:4 * oct_ + 4, 128 * j:128 * j + 128],
                                       bank_t[:, :].rearrange("p (c t) -> p c t", c=4), ACT.Copy).then_inc(ot_done, 1)

                    def gelu(b, c):
                        n = CHUNKS[c][1]
                        act.wait_ge(f_full, done(7, b, 3 + c))
                        act.wait_ge(hid_done, done(3, b, c - 1))
                        act.activation(gl[0:n, :], bank_m[0:n, SEQ:2 * SEQ], ACT.Gelu, bias=small[0:n, 6 + c:7 + c])\
                            .then_inc(gelu_done, 1)

                    def fvar(b):
                        act.wait_ge(f_full, done(7, b, 2))
                        act.activation(fl[:, :], bank_m[:, 0:SEQ], ACT.Ln, bias=eps).then_inc(fl_done, 1)
                        act.wait_ge(fl_done, done(1, b, 0))
                        act.wait_ge(fm_done, done(1, b - 1, 0))
                        act.activation(fr[:, :], fl[:, :], ACT.Exp, scale=-0.5).then_inc(fr_done, 1)

                    def split(n, u, stream, i):
                        act.wait_ge(raw_in[u % 2], n * 32 + 16 * (u // 2 + 1))
                        act.wait_ge(r_full, done(8, stream, 2 * i + 1))
                        act.activation(wh[:, u * INNER:(u + 1) * INNER], raw[:, u % 2, :], ACT.Copy).then_inc(wh_done, 1)

                    def next_wv(n, stream):
                        act.wait_ge(wv_in, n * 16 + 16)
                        act.wait_ge(v_full, done(8, stream, 7))
                        act.activation(wv[:, :], wv_next[:, :], ACT.Copy).then_inc(wv_done, 1)

                    if streams[0] < 0:
                        to_xh(0)
                        for u in range(UNITS):
                            split(nth, u, -1, 3)
                            if u == 0:
                                next_wv(nth, -1)
                    for b in streams:
                        nxt, att, prev = roles(b, last)
                        for i in range(4):
                            if prev is not None and i == 2:
                                gelu(prev, 0)
                                act.preload_act_table_set("natural_log_exp_and_others")
                            if nxt is not None:
                                square(nxt, i, 0)
                            if prev is not None and i == 1:
                                act.wait_ge(fc_done, done(1, prev, 0))
                                act.wait_ge(f_full, done(7, prev - 1, 2))
                                act.activation(fq[:, :], fc[:, :], ACT.Square).then_inc(fq_done, 1)
                            if att and i:
                                out_out(b, i - 1)
                            elif i == 0 and prev is not None:
                                out_out(prev, 3)
                            if nxt is not None:
                                values_out(nxt, 2 * i)
                            if att:
                                exps(b, i)
                            if nxt is not None:
                                square(nxt, i, 1)
                                values_out(nxt, 2 * i + 1)
                            if att:
                                probs_out(b, i)
                            if nxt is not None:
                                rnorms(nxt, i)
                            if prev is not None:
                                if i == 1:
                                    fvar(prev)
                                if i == 2:
                                    gelu(prev, 1)
                                    gelu(prev, 2)
                                    act.preload_act_table_set("natural_log_exp_and_others")
                            if i == 1 and (b + 2 < BATCH or not last):
                                to_xh(b + 2)
                            if nxt == BATCH - 1 and not last:
                                split(nth + 1, i, nxt, i)
                                if i == 3:
                                    next_wv(nth + 1, nxt)

                slots(0, range(-1, 1), False)
                if layers > 1:
                    with act.Fori(0, layers - 1) as layer:
                        slots(layer, range(1, BATCH + 1), False)
                slots(layers - 1, range(1, BATCH + 1), True)

        @block.vector
        def _(dve):
            for s, per in ((prod_done, 16), (clamp_done, 4), (rq_done, 4), (kn_done, 4), (max_done, 4), (diff_done, 4),
                           (rsum_done, 4), (o_done, 4), (xl_done, 1), (x1_done, 1), (fs_done, 2), (fc_done, 1),
                           (fm_done, 1), (fn_done, 1), (hid_done, 3), (xs_done, 2)):
                dve.sem_inc(s, 2 * per)
            dve.sem_inc(wl_done, 1)
            dve.wait_ge(const_in, 32)
            dve.tensor_copy(identb[:, :], ident).then_inc(setup, 1)
            dve.tensor_copy(mask[:, :, :], maskf[:, :].rearrange("p (f n) -> p f n", f=2)).then_inc(setup, 1)
            dve.wait_ge(setup, 2)
            for stack in range(stacks):
                if stack:
                    mid_dve(dve)
                    dve.wait_ge(coef_done, NCH + 3)
                    dve.wait_ge(rows_done, 2 * (NCH + 3))
                    dve.wait_ge(gram_done, NCH + 3)
                    dve.wait_ge(gram_in, 16 * BATCH * (NCH + 1))
                    dve.wait_ge(fin_act, 4)
                dve.memset(xs[:, :, 0:PAD + 1], 0.0).then_inc(setup, 1)
                dve.memset(fs[:, 0:1], 0.0).then_inc(setup, 1)
                dve.memset(v[:, :, :, :, HEAD_DIM:VW], 1.0).then_inc(setup, 1)
                dve.wait_ge(setup, 5 + 3 * stack)
                for c in range(TOKENS // 512):
                    at = stack * 4 + c
                    xc = x[:, c * 512:c * 512 + 512]
                    dve.wait_ge(pro_pe, at * 2 + 1)
                    if c == 0:
                        dve.wait_ge(*((x2_out, 16) if stack else (x_in, 16)))
                    dve.tensor_tensor(xc, xc, bank_c[:, :], ALU.subtract).then_inc(pro_dve, 1)
                    dve.wait_ge(pro_act, at * 3 + 3)
                    dve.wait_ge(pro_dve, at * 2 + 1)
                    dve.tensor_tensor(xc, xc, diff[:, 1, :], ALU.mult).then_inc(pro_dve, 1)
                dve.wait_ge(pro_dve, (stack * 4 + 4) * 2)
                dve.sem_inc(x_ready, BATCH)

                def slots(layer, streams, last):
                    done = Count(layer, stack)
                    nth = layer_of(layer, stack)

                    def shift_tokens(b):
                        dve.wait_ge(x_ready, done.x(b))
                        dve.wait_ge(v_full, done(8, b - 2, 7))
                        dve.wait_ge(xl_done, done(1, b - 2, 0))
                        p, at = b % 2, SEQ * (b % BATCH)
                        dve.tensor_copy(xs[0:64, p, PAD:], x[0:64, at:at + SEQ]).then_inc(xs_done, 1)
                        dve.tensor_copy(xs[64:128, p, PAD + 1:], x[64:128, at:at + SEQ - 1]).then_inc(xs_done, 1)

                    def to_xl(b):
                        dve.wait_ge(xh_done, done(1, b, 0))
                        dve.tensor_tensor(xl[:, b % 2, :], xs[:, b % 2, PAD:], xh[:, b % 2, :].bitcast(F32), ALU.subtract)\
                            .then_inc(xl_done, 1)

                    def product(b, u, kind, which):
                        bank, full = ((bank_c, c_full), (bank_r, r_full))[which]
                        dve.wait_ge(full, done(8, b, 2 * u + kind))
                        if which == 0:
                            dve.wait_ge(sq_done, done(8, b, 2 * u + kind))
                            dve.wait_ge((qadd_done, kadd_done)[kind], done(4, b, u - 1))
                        table = rots[:, 2 * kind + which, :].unsqueeze(1).to_broadcast([128, 2, SEQ])
                        dve.tensor_tensor(prod[:, 2 * kind + which, :, :], bank[:, :].rearrange("p (a t) -> p a t", a=2),
                                          table, ALU.mult).then_inc(prod_done, 1)

                    def clamp(b, u):
                        dve.wait_ge(nsum_full, done(4, b, u))
                        dve.wait_ge(log_done, done(4, b, u - 1))
                        dve.tensor_scalar(nsum[:, :], bank_c[0:64, 0:SEQ], NORM_FLOOR, LN_SHIFT, ALU.max, ALU.mult)\
                            .then_inc(clamp_done, 1)

                    def norms_out(b, u):
                        dve.wait_ge(spread_full, done(4, b, u))
                        dve.wait_ge(kadd_done, done(4, b, u))
                        ku = k[:, b % 2, 2 * u:2 * u + 2, :]
                        dve.tensor_tensor(ku, ku, bank_r[:, :].rearrange("p (a t) -> p a t", a=2), ALU.mult)\
                            .then_inc(kn_done, 1)
                        dve.wait_ge(rqt_full, done(4, b, u))
                        if u == 0:
                            dve.wait_ge(scaled_done, done(4, b - 2, 3))
                        dve.tensor_copy(rq[:, b % 2, :, 4 * u:4 * u + 4],
                                        bank_c[:, SEQ:SEQ + 64].rearrange("p (j h) -> p j h", j=2)[:, :, 0:4])\
                            .then_inc(rq_done, 1)

                    def shift_scores(b, i):
                        half = 256 * (i % 2)
                        s4 = bank_s[:, :].rearrange("p (e n) -> p e n", e=2)[:, :, half:half + 256]\
                            .rearrange("p e (c k) -> p e c k", c=4)
                        m = smax[:, i % 2, :].rearrange("p (e c) -> p e c", e=2)
                        dve.wait_ge(s_full, done(4, b, i))
                        dve.tensor_reduce(m, s4, AX.X, ALU.max).then_inc(max_done, 1)
                        dve.wait_ge(max_done, done(4, b, i))
                        dve.wait_ge(prob_done, done(4, b, i - 2))
                        d = diff[:, i % 2, :].rearrange("p (c e k) -> p e c k", c=4, e=2)
                        for e in range(2):
                            last = dve.tensor_tensor(d[:, e, :, :], s4[:, e, :, :],
                                                     m[:, e, :].unsqueeze(2).to_broadcast([128, 4, 64]), ALU.subtract)
                        last.then_inc(diff_done, 1)

                    def out_norm(b, i):
                        dve.wait_ge(o_full, done(4, b, i))
                        o4 = bank_o[:, :].rearrange("p (e n) -> p e n", e=2)[:, :, 0:4 * VW]\
                            .rearrange("p e (c d) -> p e c d", c=4)
                        r = rsum[:, :].rearrange("p (e c) -> p e c", e=2)
                        dve.wait_ge(o_done, done(4, b, i - 1))
                        dve.reciprocal(r, o4[:, :, :, HEAD_DIM]).then_inc(rsum_done, 1)
                        dve.wait_ge(rsum_done, done(4, b, i))
                        dve.wait_ge(ot_full, done(4, b, i - 2))
                        dst = o[:, i % 2, :].rearrange("p (c e d) -> p e c d", c=4, e=2)
                        for e in range(2):
                            last = dve.tensor_tensor(dst[:, e, :, :], o4[:, e, :, 0:HEAD_DIM],
                                                     r[:, e, :].unsqueeze(2).to_broadcast([128, 4, HEAD_DIM]), ALU.mult)
                        last.then_inc(o_done, 1)

                    def ffn(b, step):
                        xb = x[:, SEQ * b:SEQ * b + SEQ]
                        dve.wait_ge(f_full, done(7, b, step))
                        if step == 0:
                            dve.tensor_tensor(xb, xb, bank_m[:, 0:SEQ], ALU.add).then_inc(x1_done, 1)
                            dve.wait_ge(x1_done, done(1, b, 0))
                            dve.tensor_copy(fs[0:64, :], xb[0:64, :]).then_inc(fs_done, 1)
                            dve.tensor_copy(fs[64:128, 1:], xb[64:128, 0:SEQ - 1]).then_inc(fs_done, 1)
                        elif step == 1:
                            dve.wait_ge(fs_done, done(2, b, 1))
                            dve.tensor_tensor(fc[:, :], fs[:, :], bank_m[:, 0:SEQ], ALU.subtract).then_inc(fc_done, 1)
                        elif step == 2:
                            dve.wait_ge(fr_done, done(1, b, 0))
                            dve.tensor_tensor(fc[:, :], fc[:, :], fr[:, :], ALU.mult).then_inc(fm_done, 1)
                            dve.wait_ge(fm_done, done(1, b, 0))
                            if b == 0:
                                dve.wait_ge(small_in, nth * 16 + 16)
                            dve.tensor_scalar(fn[:, :], fc[:, :], small[:, 0:1], small[:, 1:2], ALU.mult, ALU.add)\
                                .then_inc(fn_done, 1)
                        elif step < 6:
                            c, n = step - 3, CHUNKS[step - 3][1]
                            dve.wait_ge(gelu_done, done(3, b, c))
                            dve.scalar_tensor_tensor(out=hid[0:n, c, :], in0=bank_m[0:n, 0:SEQ], scalar=small[0:n, 3 + c:4 + c],
                                                     in1=gl[0:n, :], op0=ALU.add, op1=ALU.mult).then_inc(hid_done, 1)
                        else:
                            dve.scalar_tensor_tensor(out=xb, in0=bank_m[:, 0:SEQ], scalar=small[:, 2:3], in1=xb,
                                                     op0=ALU.add, op1=ALU.add).then_inc(x_ready, 1)

                    def split(n, u):
                        dve.wait_ge(wh_done, n * UNITS + u + 1)
                        sec = slice(u * INNER, (u + 1) * INNER)
                        dve.tensor_tensor(wl[:, sec], raw[:, u % 2, :], wh[:, sec].bitcast(F32), ALU.subtract)\
                            .then_inc(wl_done, 1)

                    def rotary(n):
                        dve.wait_ge(scales_in, n * 16 + 16)
                        for t in range(4):
                            dve.tensor_scalar(rots[:, t, :], rot[:, t, :], qk_scales[:, t:t + 1], None, ALU.mult)\
                                .then_inc(rots_done, 1)
                        dve.wait_ge(rots_done, n * 4 + 4)

                    if streams[0] < 0:
                        shift_tokens(0)
                        to_xl(0)
                        split(nth, 0)
                        rotary(nth)
                        for u in range(1, UNITS):
                            split(nth, u)
                    for b in streams:
                        nxt, att, prev = roles(b, last)
                        for i in range(4):
                            if i == 0 and (b + 2 < BATCH or not last):
                                shift_tokens(b + 2)
                            if att:
                                shift_scores(b, i)
                            if prev is not None and i > 0:
                                ffn(prev, [None, 1, 3, 5][i])
                            if nxt is not None:
                                for kind in range(2):
                                    for which in range(2):
                                        product(nxt, i, kind, which)
                                clamp(nxt, i)
                            if prev is not None:
                                ffn(prev, [0, 2, 4, 6][i])
                            if att:
                                out_norm(b, i)
                            if nxt is not None:
                                norms_out(nxt, i)
                            if i == 1 and (b + 2 < BATCH or not last):
                                to_xl(b + 2)
                            if nxt == BATCH - 1 and not last:
                                split(nth + 1, i)
                                if i == 3:
                                    rotary(nth + 1)

                slots(0, range(-1, 1), False)
                if layers > 1:
                    with dve.Fori(0, layers - 1) as layer:
                        slots(layer, range(1, BATCH + 1), False)
                slots(layers - 1, range(1, BATCH + 1), True)

            dve.wait_ge(x_ready, BATCH * (LAYERS + 1) * (stacks - 1) + BATCH * (layers + 1))
            for c in range(4):
                cols = slice(512 * c, 512 * c + 512)
                dve.wait_ge(xo_in, 16 * c + 16)
                dve.scalar_tensor_tensor(out=x[:, cols], in0=x[:, cols], scalar=0.5, in1=xo[:, :], op0=ALU.mult, op1=ALU.add)\
                    .then_inc(end_dve, 1)

        @block.gpsimd
        def _(pool):
            for s, per in ((scaled_done, 4), (qadd_done, 4), (kadd_done, 4)):
                pool.sem_inc(s, 2 * per)
            pool.wait_ge(setup, 5)
            for stack in range(stacks):
                if stack:
                    mid_pool(pool)
                def slots(layer, streams, last):
                    done = Count(layer, stack)

                    def scale_scores(b, i):
                        pool.wait_ge(diff_done, done(4, b, i))
                        if i < 2:
                            pool.wait_ge(rq_done, done(4, b, 3))
                        d = diff[:, i % 2, :].rearrange("p (h k) -> p h k", k=64)
                        r = rq[:, b % 2, i // 2, 8 * (i % 2):8 * (i % 2) + 8].unsqueeze(2).to_broadcast([128, 8, 64])
                        pool.tensor_tensor(d, d, r, ALU.mult).then_inc(scaled_done, 1)

                    def rotate(b, u, kind):
                        pool.wait_ge(prod_done, done(16, b, 4 * u + 2 * kind + 1))
                        pool.wait_ge(s_full, done(4, b - 2, 3))
                        dst = (q, k)[kind][:, b % 2, 2 * u:2 * u + 2, :]
                        pool.tensor_tensor(dst, prod[:, 2 * kind, :, :], prod[:, 2 * kind + 1, :, :], ALU.add)\
                            .then_inc((qadd_done, kadd_done)[kind], 1)

                    for b in streams:
                        nxt, att, _ = roles(b, last)
                        for i in range(4):
                            if att:
                                scale_scores(b, i)
                            if nxt is not None:
                                rotate(nxt, i, 0)
                                rotate(nxt, i, 1)

                slots(0, range(-1, 1), False)
                if layers > 1:
                    with pool.Fori(0, layers - 1) as layer:
                        slots(layer, range(1, BATCH + 1), False)
                slots(layers - 1, range(1, BATCH + 1), True)
    return nc


def layout(inputs):
    a = {n: np.asarray(v) for n, v in inputs.items()}
    half = HEAD_DIM // 2
    wqkv = a["L0_ffn_Wqkv"]

    def swapped(w, axis):
        parts = np.split(w, w.shape[axis] // half, axis)
        return np.concatenate([parts[i ^ 1] for i in range(len(parts))], axis)

    wq, wk, wv = np.split(wqkv, 3, -1)
    w_qk = np.stack([w.reshape(LAYERS, DIM, UNITS, -1) for w in (wq, swapped(wq, 2), wk, swapped(wk, 2))], 3)
    w_qk = w_qk.reshape(LAYERS, DIM, 4 * INNER)
    qs, ks = a["L0_ffn_q_scale"], a["L0_ffn_k_scale"]
    cols = [np.concatenate([c, c], 1) for c in (qs, swapped(qs, 1), ks, swapped(ks, 1))]
    cols += [a["L0_ffn_ln_g"], a["L0_ffn_ln_b"], a["L0_ffn_b2"]]
    b1 = a["L0_ffn_b1"]
    for base in (0, FFN):
        for c0, n in CHUNKS:
            part = np.zeros((LAYERS, 128), np.float32)
            part[:, :n] = b1[:, base + c0:base + c0 + n]
            cols.append(part)
    smalls = np.stack(cols, -1)
    consts, mask = tables()
    return {
        "xT": a["L0_attn_x"].transpose(2, 0, 1).reshape(DIM, TOKENS), "w_qk": w_qk, "w_v": wv,
        "w_o": a["L0_ffn_Wo"], "w_1": a["L0_ffn_W1"], "w_2": a["L0_ffn_W2"], "smalls": smalls,
        "mem_w": np.concatenate([a["L0_attn_Wk"].T, a["L0_attn_Wq"].T, a["L0_attn_Wv"].T, a["L0_attn_Wout"].T,
                                 a["L0_attn_norm_weight"][:, None], np.pad(a["L0_attn_eta"], (0, DIM - MEM))[:, None]], 1),
        "consts": consts, "maskc": mask,
    }


def kernel(**inputs):
    import concourse.bacc as bacc
    from concourse.bass_utils import run_bass_kernel_spmd

    nc = bacc.Bacc("TRN2", target_bir_lowering=False, num_devices=1)
    arrays, args = {}, []
    for name, a in layout(inputs).items():
        a = np.ascontiguousarray(a)
        arrays[f"in_{name}"] = a
        args.append(nc.dram_tensor(f"in_{name}", a.shape, mybir.dt.from_np(a.dtype), kind="ExternalInput").ap())
    args.append(nc.dram_tensor("out", (DIM, TOKENS), F32, kind="ExternalOutput").ap())
    build(nc, *args)
    r = run_bass_kernel_spmd(nc, [arrays], core_ids=[0])
    return r.results[0]["out"].reshape(DIM, BATCH, SEQ).transpose(1, 2, 0)
```

```python
from contextlib import ExitStack

import numpy as np

import concourse.bass as bass
from concourse import mybir
from concourse.alu_op_type import AluOpType as ALU

ACT = mybir.ActivationFunctionType
AX = mybir.AxisListType
F32 = mybir.dt.float32
F32R = mybir.dt.float32r
BF16 = mybir.dt.bfloat16

BATCH, SEQ, DIM = 8, 256, 128
LAYERS, HEADS, HEAD_DIM, WINDOW = 6, 16, 64, 32
INNER = HEADS * HEAD_DIM
PAIRS = HEADS // 2
UNITS = PAIRS // 2
FFN = int(DIM * 4 * 2 / 3)
CHUNKS = [(0, 128), (128, 128), (256, FFN - 256)]
TOKENS = BATCH * SEQ
WINDOWS = SEQ // WINDOW
MASKED = -1e30
NORM_FLOOR = 1e-24
LN_SHIFT = 2.0 ** 20
SMALLS = 13
EPS = 1e-5


def tables():
    half = np.arange(0, HEAD_DIM, 2, dtype=np.float32)
    inv_freq = (1.0 / 10000.0 ** (half / HEAD_DIM)).astype(np.float32)
    t = np.arange(SEQ, dtype=np.float32)
    freqs = t[:, None] * inv_freq[None, :]
    freqs = np.concatenate([freqs, freqs], -1)
    base = (half + 0.4 * HEAD_DIM) / (1.4 * HEAD_DIM)
    power = (t - SEQ // 2) / (WINDOW // 2)
    scale = base[None, :] ** power[:, None]
    scale = np.concatenate([scale, scale], -1)
    sign = np.where(np.arange(HEAD_DIM) < HEAD_DIM // 2, -1.0, 1.0)
    cos, sin = np.cos(freqs), np.sin(freqs) * sign
    rot = np.stack([cos * scale, sin * scale, cos / scale, sin / scale], 0)
    rot = np.concatenate([rot, rot], 2).transpose(2, 0, 1)
    mask = np.zeros((2, 128, 2 * WINDOW), np.float32)
    for first in range(2):
        for q in range(128):
            g, i = divmod(q, WINDOW)
            for j in range(WINDOW):
                if j < i or (first == 0 and g == 0):
                    mask[first, q, j] = MASKED
                if j > i:
                    mask[first, q, WINDOW + j] = MASKED
    mask = np.tile(mask.transpose(1, 0, 2)[:, :, None, :], (1, 1, 4, 1))
    ident = np.eye(128, dtype=np.float32)
    heads = np.zeros((128, 2, 32), np.float32)
    for a in range(2):
        for e in range(2):
            heads[64 * e:64 * e + 64, a, 2 * a + e] = 1.0
    spread = np.zeros((128, 2, 128), np.float32)
    for a in range(2):
        for e in range(2):
            spread[32 + 2 * a + e, a, 64 * e:64 * e + 64] = 1.0
    bias = np.zeros((128, 4), np.float32)
    bias[0:32, 0] = np.log(8.0 * LN_SHIFT ** 0.5)
    bias[32:64, 0] = np.log(LN_SHIFT ** 0.5)
    bias[:, 1] = EPS
    bias[:, 2] = EPS_RMS
    bias[:, 3] = 1.0
    mean = np.full((128, 128), 1.0 / DIM, np.float32)
    at = np.arange(128)
    picks = np.concatenate([at[:, None] % STEPS == np.arange(STEPS), at[:, None] // STEPS == np.arange(BATCH)], 1)
    f = np.concatenate([rot.reshape(128, -1), ident, heads.reshape(128, -1), spread.reshape(128, -1), bias, mean, picks.astype(np.float32)], 1)
    return np.ascontiguousarray(f.astype(np.float32)), np.ascontiguousarray(mask.reshape(128, -1))


MEM = 64
STEPS = 16
STEPS1 = STEPS + 1
MEM_SIZE = MEM * DIM
EPS_RMS, ETA_MIN = 1e-6, 1e-6
MEM_COLS = 2 * MEM + 2 * DIM + 2
GRAM = 2 * STEPS1 + STEPS

ROT0, IDENT0 = 0, 4 * SEQ
HEADS0 = IDENT0 + 128
SPREAD0 = HEADS0 + 64
BIAS0 = SPREAD0 + 256
MEAN0 = BIAS0 + 4
STEP0 = MEAN0 + 128
SEQUENCE0 = STEP0 + STEPS
CONST_COLS = SEQUENCE0 + BATCH


class Count:

    def __init__(self, layer, stack):
        self.layer, self.stack = layer, stack

    def __call__(self, per, b, k):
        return self.layer * (per * BATCH) + (per * (BATCH * LAYERS * self.stack + b + 2) + k + 1)

    def x(self, b):
        return self.layer * BATCH + (BATCH * (LAYERS + 1) * self.stack + b + 1)


def build(nc, xT, w_qk, w_v, w_o, w_1, w_2, smalls, mem_w, consts, maskc, out, stacks=2, layers=LAYERS):
    x2 = nc.dram_tensor("x2", (DIM, TOKENS), F32, kind="Internal").ap()
    ctx = ExitStack()
    with ctx:
        def sb(name, shape, dt=F32):
            return ctx.enter_context(nc.sbuf_tensor(name, shape, dt))

        def ps(name, cols):
            return ctx.enter_context(nc.psum_tensor(name, [128, cols], F32))

        def sem(name):
            return ctx.enter_context(nc.semaphore(name))

        const = sb("const", [128, CONST_COLS])
        mask = sb("mask", [128, 2, 256], BF16)
        identb = sb("identb", [128, 128], BF16)
        rot = const[:, ROT0:IDENT0].rearrange("p (k t) -> p k t", k=4)
        ident = const[:, IDENT0:HEADS0]
        head_sum = const[:, HEADS0:SPREAD0].rearrange("p (a m) -> p a m", a=2)
        spread_r = sb("spread_r", [64, 2 * 128], F32R)
        spread = spread_r[:, :].rearrange("p (a m) -> p a m", a=2)
        norm_bias = const[0:64, BIAS0:BIAS0 + 1]
        eps = const[:, BIAS0 + 1:BIAS0 + 2]
        eps_rms = const[:, BIAS0 + 2:BIAS0 + 3]
        ones_col = const[:, BIAS0 + 3:BIAS0 + 4]
        mean_w = const[:, MEAN0:STEP0]
        step_mask = const[:, STEP0:SEQUENCE0]
        sequence_mask = const[:, SEQUENCE0:CONST_COLS]

        x = sb("x", [128, TOKENS])
        xo = sb("xo", [128, 512])
        memw = sb("memw", [128, MEM_COLS])
        wk_T, wq_T = memw[:, 0:MEM], memw[:, MEM:2 * MEM]
        wv_T, wout_T = memw[:, 2 * MEM:2 * MEM + DIM], memw[:, 2 * MEM + DIM:2 * MEM + 2 * DIM]
        norm_w, eta_in = memw[:, MEM_COLS - 2:MEM_COLS - 1], memw[0:MEM, MEM_COLS - 1:MEM_COLS]
        ctx2 = ExitStack()

        def sb(name, shape, dt=F32):
            return ctx2.enter_context(nc.sbuf_tensor(name, shape, dt))

        xs = sb("xs", [128, 2, SEQ])
        xh = sb("xh", [128, 2, SEQ], F32R)
        xl = sb("xl", [128, 2, SEQ], F32R)
        raw = sb("raw", [128, 2, INNER])
        wh = sb("wh", [128, 4 * INNER], F32R)
        wl = sb("wl", [128, 4 * INNER], F32R)
        wv_next = sb("wv_next", [128, INNER])
        wvh = sb("wvh", [128, INNER], F32R)
        wvl = sb("wvl", [128, INNER], F32R)
        wo = sb("wo", [128, PAIRS, DIM])
        w1 = sb("w1", [128, 2 * FFN])
        w2 = sb("w2", [128, 3, DIM])
        small = sb("small", [128, SMALLS - 4])
        qk_scales = sb("qk_scales", [128, 4])
        rots = sb("rots", [128, 4, SEQ])
        q = sb("q", [128, 2, PAIRS, SEQ])
        k = sb("k", [128, 2, PAIRS, SEQ])
        v_rows_s = sb("v_rows_s", [128, 2, PAIRS * HEAD_DIM])
        v = sb("v", [128, 2, WINDOWS, PAIRS, HEAD_DIM])
        prod = sb("prod", [128, 4, 2, SEQ])
        sq = sb("sq", [128, 2, 2, SEQ])
        nsum = sb("nsum", [64, SEQ])
        nlog = nsum
        rnorm = sb("rnorm", [64, SEQ])
        rnormh = sb("rnormh", [64, SEQ], F32R)
        rnorml = sb("rnorml", [64, SEQ], F32R)
        rq = sb("rq", [128, 2, 2, HEADS])
        smax = sb("smax", [128, 2, PAIRS])
        diff = sb("diff", [128, 2, 512])
        prob = sb("prob", [128, 2, 512])
        probT = sb("probT", [128, 2, 512])
        psum = sb("psum", [128, 2, 8])
        rsum = sb("rsum", [128, 8])
        o = sb("o", [128, 2, 512])
        oT = sb("oT", [128, PAIRS, SEQ])
        fs = sb("fs", [128, SEQ])
        fc = sb("fc", [128, SEQ])
        fl = sb("fl", [128, SEQ])
        fr = fl
        fn = sb("fn", [128, SEQ])
        gl = sb("gl", [128, SEQ])
        fq = gl
        hid = sb("hid", [128, 3, SEQ])

        bank_c = ps("bank_c", 512)
        bank_r = ps("bank_r", 512)
        bank_m = ps("bank_m", 512)
        bank_t = ps("bank_t", 512)
        bank_s = ps("bank_s", 1024)
        bank_o = ps("bank_o", 1024)

        c_full, r_full = sem("c_full"), sem("r_full")
        nsum_full = sem("nsum_full")
        rqt_full, spread_full = sem("rqt_full"), sem("spread_full")
        v_full, f_full = sem("v_full"), sem("f_full")
        s_full, pt_full, o_full, ot_full = sem("s_full"), sem("pt_full"), sem("o_full"), sem("ot_full")
        sq_done = sem("sq_done")
        log_done, rnorm_done = sem("log_done"), sem("rnorm_done")
        v_done, prob_done, pt_done, ot_done = sem("v_done"), sem("prob_done"), sem("pt_done"), sem("ot_done")
        xh_done = sem("xh_done")
        fq_done, fl_done, fr_done, gelu_done = sem("fq_done"), sem("fl_done"), sem("fr_done"), sem("gelu_done")
        wh_done, wvh_done = sem("wh_done"), sem("wvh_done")
        wvl_done, sum_done = sem("wvl_done"), sem("sum_done")
        v_in = [sem("v_in0"), sem("v_in1"), sem("v_in2"), sem("v_in3")]
        attend_on, place_on = sem("attend_on"), sem("place_on")
        xs_done = sem("xs_done")
        prod_done = sem("prod_done")
        clamp_done, rnorml_done, rq_done, kn_done = sem("clamp_done"), sem("rnorml_done"), sem("rq_done"), sem("kn_done")
        max_done, diff_done, rsum_done, o_done = sem("max_done"), sem("diff_done"), sem("rsum_done"), sem("o_done")
        xl_done = sem("xl_done")
        x1_done, fs_done, fc_done, fm_done, fn_done, hid_done = (
            sem("x1_done"), sem("fs_done"), sem("fc_done"), sem("fm_done"), sem("fn_done"), sem("hid_done"))
        x_ready = sem("x_ready")
        wl_done, rots_done = sem("wl_done"), sem("rots_done")
        scaled_done, qadd_done, kadd_done = sem("scaled_done"), sem("qadd_done"), sem("kadd_done")
        raw_in = [sem("raw_in0"), sem("raw_in1")]
        wv_in, wo_in, w1_in, w2_in = sem("wv_in"), sem("wo_in"), sem("w1_in"), sem("w2_in")
        small_in, scales_in = sem("small_in"), sem("scales_in")
        const_in, x_in, setup, out_done = sem("const_in"), sem("x_in"), sem("setup"), sem("out_done")
        pro_pe, pro_act, pro_dve = sem("pro_pe"), sem("pro_act"), sem("pro_dve")

        ctx2.close()

        def chunk_buffers():
            alloc = ExitStack()

            def sb(name, shape):
                return alloc.enter_context(nc.sbuf_tensor(name, shape, F32))

            return dict(
                x1=sb("x1", [128, TOKENS]), yn=sb("yn", [128, TOKENS]), msq=sb("msq", [128, 512]), mlog=sb("mlog", [128, 512]),
                mrs=sb("mrs", [128, 512]), neg=sb("neg", [64, 2, 512]),
                kT=sb("kT", [64, BATCH, SEQ + STEPS]), qT=sb("qT", [64, BATCH, SEQ]), vT=sb("vT", [128, BATCH, SEQ + STEPS]),
                eta=sb("eta", [64, 1]), ke=sb("ke", [64, 2, BATCH, 2 * STEPS + 1]), vc=sb("vc", [128, 2, BATCH, STEPS1]),
                ek_rows=sb("ek_rows", [STEPS1, 2, BATCH, MEM]), v_rows=sb("v_rows", [STEPS1, 2, BATCH, DIM]),
                gram_s=sb("gram_s", [STEPS1, BATCH * GRAM]), gram_b=sb("gram_b", [BATCH, 2, STEPS1, GRAM]),
                coef=sb("coef", [BATCH, 2, STEPS, STEPS1, STEPS1]), ab=sb("ab", [BATCH, STEPS, STEPS1]),
                lin=sb("lin", [BATCH, 2, STEPS, STEPS1]), sqr=sb("sqr", [BATCH, 2, STEPS, STEPS1]),
                kap2=sb("kap2", [BATCH, 2, STEPS]), sigh=sb("sigh", [BATCH, 2, STEPS]), cvec=sb("cvec", [BATCH, STEPS1]),
                m=sb("m", [64, BATCH, DIM]), yt=sb("yt", [128, BATCH, 2 * STEPS]), ysq=sb("ysq", [128, 2, BATCH, STEPS]),
                gp_s=sb("gp_s", [STEPS1, BATCH * STEPS]), by_step=sb("by_step", [128, 2, STEPS]),
                gram_m=sb("gram_m", [BATCH, STEPS1, STEPS1]), quad=sb("quad", [BATCH, STEPS1]), 
                u2=sb("u2", [BATCH, 1]), pn=sb("pn", [BATCH, 1]), s1=sb("s1", [BATCH, 1]), s2=sb("s2", [BATCH, 1]),
                s3=sb("s3", [BATCH, 1]), cross=sb("cross", [BATCH, 1]), nd=sb("nd", [BATCH, 1]),
                tau=sb("tau", [BATCH, 1]), rt2=sb("rt2", [BATCH, 1]), lv=sb("lv", [BATCH, STEPS1]), lw=sb("lw", [BATCH, STEPS1]),
                w=sb("w", [BATCH, STEPS]), rho=sb("rho", [BATCH, 1]), itau=sb("itau", [BATCH, 1]), nrho=sb("nrho", [BATCH, 1]),
                cf=sb("cf", [BATCH, STEPS1]), diag=sb("diag", [BATCH, BATCH]), cf_s=sb("cf_s", [STEPS1, BATCH]),
                scaled=sb("scaled", [STEPS1, BATCH, MEM]), mem_T=sb("mem_T", [128, 512]), ones8=sb("ones8", [BATCH, MEM]),
                minus_half=sb("minus_half", [BATCH, 1]),
            ), alloc

        buffers, alloc = chunk_buffers()
        alloc.close()
        g = type("Buffers", (), buffers)
        NCH = SEQ // STEPS
        pe_did, act_did, dve_did, pool_did = sem("pe_did"), sem("act_did"), sem("dve_did"), sem("pool_did")
        x1_in, memw_in, x2_out, xo_in = sem("x1_in"), sem("memw_in"), sem("x2_out"), sem("xo_in")
        end_dve = sem("end_dve")
        prep_in, rows_full, gram_full, y_full, gp_full, hp_full, cf_full, n_full = (
            sem("prep_in"), sem("rows_full"), sem("gram_full"), sem("y_full"), sem("gp_full"), sem("hp_full"),
            sem("cf_full"), sem("n_full"))
        rows_done, gram_done, gp_done, root_done = sem("rows_done"), sem("gram_done"), sem("gp_done"), sem("root_done")
        coef_step, coef_done, gram_in = sem("coef_step"), sem("coef_done"), sem("gram_in")
        start_full, by_step_done = sem("start_full"), sem("by_step_done")
        dve_step, want_root, yt_done, ysq_done, cf_done, scaled_rows_done, m_done = (
            sem("dve_step"), sem("want_root"), sem("yt_done"), sem("ysq_done"), sem("cf_done"), sem("scaled_rows_done"), sem("m_done"))
        fin_pe, fin_act, fin_dve = sem("fin_pe"), sem("fin_act"), sem("fin_dve")
        ROOTS = 2 * STEPS
        GP0 = BATCH * STEPS
        SUMS0 = GP0 + STEPS * STEPS1
        ALL_X = BATCH * (layers + 1)

        class Chunk:

            def __init__(self, it, p):
                self.it, self.p = it, p

            def __call__(self, per, k, ahead=0):
                return self.it * (2 * per) + (per * (self.p + ahead + 2) + k + 1)

        def mid_sp(sp):
            sp.wait_ge(x_ready, ALL_X)
            for c in range(4):
                sp.dma_start(g.x1[:, 512 * c:512 * c + 512], xT[:, 512 * c:512 * c + 512]).then_inc(x1_in, 16)
            sp.wait_ge(pool_did, 1)

            def gram(done):
                sp.wait_ge(gram_done, done(1, 0))
                for b in range(BATCH):
                    sp.dma_start(g.gram_b[b:b + 1, done.p, :, :], g.gram_s[:, GRAM * b:GRAM * b + GRAM]).then_inc(gram_in, 16)

            gram(Chunk(0, 0))
            with sp.Fori(0, NCH // 2) as it:
                for p in range(2):
                    d = Chunk(it, p)
                    sp.wait_ge(gram_done, d(1, 0, 1))
                    for b in range(BATCH):
                        sp.dma_start(g.gram_b[b:b + 1, 1 - p, :, :], g.gram_s[:, GRAM * b:GRAM * b + GRAM]).then_inc(gram_in, 16)
            sp.wait_ge(fin_dve, 8)
            sp.dma_start(x2, x[:, :]).then_inc(x2_out, 16)
            sp.wait_ge(x2_out, 16)

        def mid_pe(pe):
            for s, per in ((rows_full, 2), (gram_full, 1), (y_full, 1), (gp_full, 1), (hp_full, 1), (start_full, 1), (cf_full, 1), (n_full, 2)):
                pe.sem_inc(s, 2 * per)
            pe.wait_ge(memw_in, 16)
            for c in range(4):
                cols = slice(512 * c, 512 * c + 512)
                pe.wait_ge(dve_did, 8 * c + 1)
                pe.matmul(bank_c[:, :], mean_w, g.x1[:, cols], start=True, stop=True).then_inc(pe_did, 1)
                for k_ in (1, 4):
                    pe.wait_ge(act_did, 9 * c + k_)
                    pe.matmul(bank_c[:, :], mean_w, g.msq[:, :], start=True, stop=True).then_inc(pe_did, 1)
                pe.wait_ge(dve_did, 8 * c + 4)
                pe.matmul(bank_r[0:64, :], wk_T, g.yn[:, cols], start=True, stop=True).then_inc(pe_did, 1)
                pe.matmul(bank_t[0:64, :], wq_T, g.yn[:, cols], start=True, stop=True).then_inc(pe_did, 1)
                pe.matmul(bank_m[:, :], wv_T, g.yn[:, cols], start=True, stop=True).then_inc(pe_did, 1)

            def prep(done, ahead):
                p = (done.p + ahead) % 2
                pe.wait_ge(prep_in, done(3, 2, ahead))
                pe.wait_ge(rows_done, done(2, 1, ahead - 1))
                for b in range(BATCH):
                    last = pe.transpose(bank_o[0:STEPS, DIM * b:DIM * b + DIM], g.vc[:, p, b, 0:STEPS], ident)
                last.then_inc(rows_full, 1)
                for b in range(BATCH):
                    last = pe.transpose(bank_t[0:STEPS, MEM * b:MEM * b + MEM], g.ke[:, p, b, STEPS:2 * STEPS], ident[0:64, 0:64])
                last.then_inc(rows_full, 1)
                pe.wait_ge(gram_done, done(1, 0, ahead - 1))
                for b in range(BATCH):
                    pe.matmul(bank_m[0:STEPS1, GRAM * b + 2 * STEPS + 1:GRAM * b + GRAM], g.vc[:, p, b, :], g.vc[:, p, b, :],
                              start=True, stop=True)
                    last = pe.matmul(bank_m[0:STEPS1, GRAM * b:GRAM * b + 2 * STEPS + 1], g.ke[:, p, b, STEPS:], g.ke[:, p, b, :],
                                     start=True, stop=True)
                last.then_inc(gram_full, 1)

            pe.wait_ge(dve_did, 32 + 16)
            prep(Chunk(0, 0), 0)
            with pe.Fori(0, NCH // 2) as it:
                for p in range(2):
                    done = Chunk(it, p)
                    for b in range(BATCH):
                        if b % 4 == 0:
                            pe.wait_ge(m_done, done(2, b // 4, -1))
                        last = pe.matmul(bank_c[:, 2 * STEPS * b:2 * STEPS * (b + 1)], g.m[:, b, :], g.ke[:, p, b, 0:2 * STEPS],
                                         start=True, stop=True)
                    last.then_inc(y_full, 1)
                    pe.wait_ge(yt_done, done(1, 0))
                    for b in range(BATCH):
                        last = pe.matmul(bank_r[0:STEPS1, STEPS * b:STEPS * (b + 1)], g.vc[:, p, b, :], g.yt[:, b, 0:STEPS],
                                         start=True, stop=True)
                    last.then_inc(gp_full, 1)
                    pe.wait_ge(ysq_done, done(2, 1))
                    pe.wait_ge(rows_done, done(2, 1))
                    for r in range(2):
                        last = pe.matmul(bank_t[:, r:r + 1], g.ysq[:, r, :, :].rearrange("p b j -> p (b j)"), ones_col,
                                         start=True, stop=True)
                    last.then_inc(hp_full, 1)
                    pe.wait_ge(by_step_done, done(1, 0))
                    pe.wait_ge(gp_done, done(1, 0))
                    pe.matmul(bank_r[0:BATCH, SUMS0:SUMS0 + 2 * STEPS], sequence_mask, g.by_step[:, :, :].rearrange("p r j -> p (r j)"),
                              start=True, stop=True)
                    gp = g.gp_s[:, :].rearrange("l (b j) -> l j b", b=BATCH)
                    for j in range(STEPS):
                        last = pe.transpose(bank_r[0:BATCH, GP0 + STEPS1 * j:GP0 + STEPS1 * (j + 1)], gp[:, j, :],
                                            ident[0:STEPS1, 0:STEPS1])
                    last.then_inc(start_full, 1)
                    prep(done, 1)
                    pe.wait_ge(cf_done, done(2, 1))
                    pe.matmul(bank_c[0:64, 272:272 + BATCH], g.ones8[:, :], g.diag[:, :], start=True, stop=True)
                    pe.transpose(bank_c[0:STEPS1, 256:256 + BATCH], g.cf[:, :], ident[0:BATCH, 0:BATCH]).then_inc(cf_full, 1)
                    pe.wait_ge(scaled_rows_done, done(1, 0))
                    pe.wait_ge(rows_done, done(2, 1))
                    for b in range(BATCH):
                        last = pe.matmul(bank_s[0:64, DIM * b:DIM * (b + 1)], g.scaled[:, b, :], g.v_rows[:, p, b, :],
                                         start=True, stop=True)
                        if b % 4 == 3:
                            last.then_inc(n_full, 1)
            done = Chunk(NCH // 2, 0)
            pe.wait_ge(m_done, done(2, 1, -1))
            for c in range(4):
                if c:
                    pe.wait_ge(fin_act, c)
                for b in range(2):
                    last = pe.matmul(bank_c[:, SEQ * b:SEQ * (b + 1)], g.m[:, 2 * c + b, :], g.qT[:, 2 * c + b, :],
                                     start=True, stop=True)
                last.then_inc(fin_pe, 1)
                pe.wait_ge(fin_act, c + 1)
                if c:
                    pe.wait_ge(fin_dve, 2 * c)
                pe.matmul(bank_r[:, :], wout_T, g.mem_T[:, :], start=True, stop=True).then_inc(fin_pe, 1)

        def mid_act(act):
            for s, per in ((rows_done, 2), (gram_done, 1), (gp_done, 1), (root_done, ROOTS)):
                act.sem_inc(s, 2 * per)
            act.preload_act_table_set("natural_log_exp_and_others")
            for c in range(4):
                cols = slice(512 * c, 512 * c + 512)
                for r in range(2):
                    act.wait_ge(dve_did, 8 * c + 2 + r)
                    act.activation(g.msq[:, :], x[:, cols], ACT.Square).then_inc(act_did, 1)
                    act.wait_ge(pe_did, 6 * c + 2 + r)
                    act.activation(g.mlog[:, :], bank_c[:, :], ACT.Ln, bias=(eps, eps_rms)[r]).then_inc(act_did, 1)
                    act.wait_ge(act_did, 9 * c + 3 * r + 2)
                    if r:
                        act.wait_ge(dve_did, 8 * c + 3)
                    act.activation(g.mrs[:, :], g.mlog[:, :], ACT.Exp, scale=-0.5).then_inc(act_did, 1)
                for r in range(2):
                    act.wait_ge(dve_did, 8 * c + 5 + r)
                    act.activation(g.neg[:, r, :], g.neg[:, r, :], ACT.Exp).then_inc(act_did, 1)
                act.wait_ge(pe_did, 6 * c + 6)
                act.activation(g.vT[:, 2 * c:2 * c + 2, 0:SEQ], bank_m[:, :].rearrange("p (b t) -> p b t", b=2), ACT.Copy)\
                    .then_inc(act_did, 1)
            act.preload_act_table_set("sqrt_and_others")

            def prep_out(done, ahead, part, first=False):
                p = (done.p + ahead) % 2
                if part < 2:
                    act.wait_ge(rows_full, done(2, 0, ahead))
                    four = slice(4 * part, 4 * part + 4)
                    last = act.activation(g.v_rows[0:STEPS, p, four, :],
                                          bank_o[0:STEPS, 512 * part:512 * part + 512].rearrange("p (b f) -> p b f", b=4), ACT.Copy)
                    if part == 1:
                        last.then_inc(rows_done, 1)
                elif part == 2:
                    act.wait_ge(rows_full, done(2, 1, ahead))
                    act.activation(g.ek_rows[0:STEPS, p, :, :], bank_t[0:STEPS, :].rearrange("p (b f) -> p b f", b=BATCH), ACT.Copy)\
                        .then_inc(rows_done, 1)
                else:
                    act.wait_ge(gram_full, done(1, 0, ahead))
                    if not first:
                        act.wait_ge(gram_in, 16 * BATCH + done.it * (2 * 16 * BATCH) + (16 * BATCH * (done.p + ahead - 1)))
                    act.activation(g.gram_s[:, :], bank_m[0:STEPS1, 0:BATCH * GRAM], ACT.Copy).then_inc(gram_done, 1)

            act.wait_ge(dve_did, 32 + 16)
            for part in range(4):
                prep_out(Chunk(0, 0), 0, part, True)

            with act.Fori(0, NCH // 2) as it:
                for p in range(2):
                    done = Chunk(it, p)
                    act.wait_ge(gp_full, done(1, 0))
                    act.activation(g.gp_s[:, :], bank_r[0:STEPS1, 0:BATCH * STEPS], ACT.Copy).then_inc(gp_done, 1)
                    for i in range(STEPS):
                        act.wait_ge(want_root, done(ROOTS, 2 * i))
                        act.activation(g.w[:, i:i + 1], g.cross[:, :], ACT.Sqrt, bias=g.s2[:, :], scale=-1.0).then_inc(root_done, 1)
                        if 1 <= i <= 4:
                            prep_out(done, 1, i - 1)
                        act.wait_ge(want_root, done(ROOTS, 2 * i + 1))
                        act.activation(g.rt2[:, :], g.tau[:, :], ACT.Sqrt, scale=4.0).then_inc(root_done, 1)
            for c in range(4):
                act.wait_ge(fin_pe, 2 * c + 1)
                if c:
                    act.wait_ge(fin_pe, 2 * c)
                act.activation(g.mem_T[:, :], bank_c[:, :], ACT.Copy).then_inc(fin_act, 1)

        def mid_pool(pool):
            for s, per in ((prep_in, 3), (coef_done, 1)):
                pool.sem_inc(s, 2 * per)
            pool.wait_ge(dve_did, 32 + 16)
            pool.sem_inc(pool_did, 1)

            PER = 12

            def prep(done, ahead, at, base):
                p = (done.p + ahead) % 2
                n = [0]

                def step(ins):
                    ins.then_inc(coef_step, 1)
                    n[0] += 1
                    pool.wait_ge(coef_step, base + n[0])

                pool.wait_ge(m_done, done(2, 1, ahead - 2))
                kc = g.kT[:, :, bass.ds(at, STEPS)]
                pool.tensor_copy(g.ke[:, p, :, 0:STEPS], kc).then_inc(prep_in, 1)
                pool.tensor_tensor(g.ke[:, p, :, STEPS:2 * STEPS], kc, g.eta[:, 0:1].unsqueeze(2).to_broadcast([MEM, BATCH, STEPS]),
                                   ALU.mult).then_inc(prep_in, 1)
                pool.wait_ge(prep_in, done(3, 1, ahead))
                pool.tensor_copy(g.vc[:, p, :, 0:STEPS], g.vT[:, :, bass.ds(at, STEPS)]).then_inc(prep_in, 1)
                pool.wait_ge(prep_in, done(3, 2, ahead))
                pool.wait_ge(gram_in, 16 * BATCH + done.it * (2 * 16 * BATCH) + 16 * BATCH * (done.p + ahead))
                gb = g.gram_b[:, p, :, :]
                kk, ee, vv = gb[:, 0:STEPS, 0:STEPS], gb[:, 0:STEPS, STEPS:2 * STEPS + 1], gb[:, 0:STEPS, 2 * STEPS + 1:]
                vdiag = gb.rearrange("b i m -> b (i m)")[:, 2 * STEPS + 1:2 * STEPS + 1 + (STEPS - 1) * (GRAM + 1) + 1:GRAM + 1]
                co = g.coef[:, p, :, :, :]
                full = [BATCH, STEPS, STEPS1, STEPS]
                step(pool.tensor_tensor(co[:, :, :, 0:STEPS], kk.unsqueeze(2).to_broadcast(full),
                                        vv.unsqueeze(3).to_broadcast(full), ALU.mult))
                step(pool.tensor_tensor(g.ab[:, :, :], ee, vv, ALU.mult))
                step(pool.tensor_tensor(co[:, :, :, STEPS], g.ab[:, :, :], g.cvec[:, :].unsqueeze(1).to_broadcast([BATCH, STEPS, STEPS1]),
                                        ALU.mult))
                step(pool.tensor_tensor(g.lin[:, p, :, 0:STEPS], kk, kk, ALU.add))
                step(pool.tensor_tensor(g.sqr[:, p, :, 0:STEPS], kk, kk, ALU.mult))
                step(pool.tensor_tensor(g.sqr[:, p, :, 0:STEPS], g.sqr[:, p, :, 0:STEPS],
                                        vdiag.unsqueeze(2).to_broadcast([BATCH, STEPS, STEPS]), ALU.mult))
                abdiag = g.ab[:, :, :].rearrange("b i l -> b (i l)")[:, 0:(STEPS - 1) * (STEPS1 + 1) + 1:STEPS1 + 1]
                step(pool.tensor_tensor(g.sqr[:, p, :, STEPS], abdiag, g.cvec[:, STEPS:].to_broadcast([BATCH, STEPS]), ALU.mult))
                step(pool.tensor_tensor(g.kap2[:, p, :], gb[:, STEPS, 0:STEPS], gb[:, STEPS, 0:STEPS], ALU.add))
                pool.tensor_tensor(g.sigh[:, p, :], gb[:, 0:STEPS, GRAM - 1], g.minus_half[:, :].to_broadcast([BATCH, STEPS]), ALU.mult).then_inc(coef_done, 1)
                pool.wait_ge(coef_done, done(1, 0, ahead))
                return n[0]

            per = prep(Chunk(0, 0), 0, 0, 0)
            with pool.Fori(0, NCH // 2) as it:
                for p in range(2):
                    prep(Chunk(it, p), 1, it * (2 * STEPS) + STEPS * (p + 1), it * (2 * per) + per * (p + 1))

        def mid_dve(dve):
            for s, per in ((want_root, ROOTS), (yt_done, 1), (ysq_done, 2), (by_step_done, 1), (cf_done, 2), (scaled_rows_done, 1), (m_done, 2)):
                dve.sem_inc(s, 2 * per)
            for c in range(4):
                cols = slice(512 * c, 512 * c + 512)
                dve.wait_ge(x_ready, ALL_X)
                dve.wait_ge(x1_in, 64)
                dve.scalar_tensor_tensor(out=g.x1[:, cols], in0=x[:, cols], scalar=0.5, in1=g.x1[:, cols], op0=ALU.mult, op1=ALU.add)\
                    .then_inc(dve_did, 1)
                dve.wait_ge(pe_did, 6 * c + 1)
                dve.wait_ge(dve_did, 8 * c + 1)
                dve.tensor_tensor(x[:, cols], g.x1[:, cols], bank_c[:, :], ALU.subtract).then_inc(dve_did, 1)
                dve.wait_ge(act_did, 9 * c + 3)
                dve.wait_ge(dve_did, 8 * c + 2)
                dve.tensor_tensor(x[:, cols], x[:, cols], g.mrs[:, :], ALU.mult).then_inc(dve_did, 1)
                dve.wait_ge(act_did, 9 * c + 6)
                dve.wait_ge(dve_did, 8 * c + 3)
                dve.scalar_tensor_tensor(out=g.yn[:, cols], in0=x[:, cols], scalar=norm_w, in1=g.mrs[:, :], op0=ALU.mult, op1=ALU.mult)\
                    .then_inc(dve_did, 1)
                for r, bank in ((0, bank_r), (1, bank_t)):
                    dve.wait_ge(pe_did, 6 * c + 4 + r)
                    dve.tensor_scalar(g.neg[:, r, :], bank[0:64, :], 0.0, None, ALU.min).then_inc(dve_did, 1)
                for r, (bank, dst) in enumerate(((bank_r, g.kT), (bank_t, g.qT))):
                    dve.wait_ge(act_did, 9 * c + 7 + r)
                    dve.scalar_tensor_tensor(out=dst[:, 2 * c:2 * c + 2, 0:SEQ], in0=bank[0:64, :].rearrange("p (b t) -> p b t", b=2),
                                             scalar=0.0, in1=g.neg[:, r, :].rearrange("p (b t) -> p b t", b=2),
                                             op0=ALU.max, op1=ALU.add).then_inc(dve_did, 1)
            dve.wait_ge(act_did, 36)
            dve.scalar_tensor_tensor(out=g.eta[:, :], in0=eta_in, scalar=-1.0, in1=eta_in, op0=ALU.mult, op1=ALU.max).then_inc(dve_did, 1)
            dve.wait_ge(dve_did, 32 + 1)
            dve.tensor_scalar(g.eta[:, :], g.eta[:, :], ETA_MIN, None, ALU.max).then_inc(dve_did, 1)
            dve.memset(g.kT[:, :, SEQ:], 0.0).then_inc(dve_did, 1)
            dve.memset(g.vT[:, :, SEQ:], 0.0).then_inc(dve_did, 1)
            dve.memset(g.ke[:, :, :, 2 * STEPS:], 1.0).then_inc(dve_did, 1)
            dve.memset(g.vc[:, :, :, STEPS:], 1.0).then_inc(dve_did, 1)
            dve.memset(g.ek_rows[:, :, :, :], 1.0).then_inc(dve_did, 1)
            dve.memset(g.v_rows[:, :, :, :], 1.0).then_inc(dve_did, 1)
            dve.memset(g.lin[:, :, :, STEPS:], 1.0).then_inc(dve_did, 1)
            dve.memset(g.cvec[:, 0:STEPS], 2.0 / MEM_SIZE).then_inc(dve_did, 1)
            dve.memset(g.cvec[:, STEPS:], 1.0 / MEM_SIZE).then_inc(dve_did, 1)
            dve.memset(g.m[:, :, :], 0.0).then_inc(dve_did, 1)
            dve.memset(g.itau[:, :], 0.0).then_inc(dve_did, 1)
            dve.memset(g.nd[:, :], 0.0).then_inc(dve_did, 1)
            dve.memset(g.ones8[:, :], 1.0).then_inc(dve_did, 1)
            dve.memset(g.minus_half[:, :], -0.5).then_inc(dve_did, 1)
            dve.wait_ge(dve_did, 32 + 16)

            def chunk(done, base):
                p, n = done.p, [0]

                def step(ins):
                    ins.then_inc(dve_step, 1)
                    n[0] += 1
                    return n[0]

                def need(k):
                    dve.wait_ge(dve_step, base + k)

                def stt(out, in0, scalar, in1, op0, op1):
                    return dve.scalar_tensor_tensor(out=out, in0=in0, scalar=scalar, in1=in1, op0=op0, op1=op1)

                dve.wait_ge(y_full, done(1, 0))
                dve.tensor_copy(g.yt[:, :, :], bank_c[:, 0:2 * STEPS * BATCH].rearrange("p (b j) -> p b j", b=BATCH)).then_inc(yt_done, 1)
                dve.wait_ge(yt_done, done(1, 0))
                dve.tensor_tensor(g.ysq[:, 0, :, :], g.yt[:, :, 0:STEPS], g.yt[:, :, 0:STEPS], ALU.mult).then_inc(ysq_done, 1)
                dve.tensor_tensor(g.ysq[:, 1, :, :], g.yt[:, :, STEPS:], g.vc[:, p, :, 0:STEPS], ALU.mult).then_inc(ysq_done, 1)
                step(stt(g.quad[:, STEPS:], g.nd[:, :], -1.0, g.itau[:, :], ALU.mult, ALU.mult))
                step(dve.memset(g.gram_m[:, STEPS, STEPS:], 0.0))
                step(dve.memset(g.tau[:, :], 1.0))
                step(dve.memset(g.rt2[:, :], 2.0))
                dve.wait_ge(hp_full, done(1, 0))
                dve.tensor_tensor(g.by_step[:, :, :], step_mask.unsqueeze(1).to_broadcast([128, 2, STEPS]),
                                  bank_t[:, 0:2].unsqueeze(2).to_broadcast([128, 2, STEPS]), ALU.mult).then_inc(by_step_done, 1)
                dve.wait_ge(start_full, done(1, 0))
                step(dve.tensor_copy(g.gram_m[:, :, 0:STEPS],
                                     bank_r[0:BATCH, GP0:SUMS0].rearrange("b (j l) -> b l j", l=STEPS1)))
                step(dve.tensor_copy(g.quad[:, 0:STEPS], bank_r[0:BATCH, SUMS0:SUMS0 + STEPS]))
                ready = step(dve.tensor_scalar(g.gram_m[:, 0:STEPS, STEPS], bank_r[0:BATCH, SUMS0 + STEPS:SUMS0 + 2 * STEPS],
                                               2.0 / MEM_SIZE, None, ALU.mult))
                dve.wait_ge(coef_done, done(1, 0))
                mean = g.gram_m[:, STEPS, STEPS:]
                need(ready)
                for i in range(STEPS + 1):
                    now = slice(i, i + 1)
                    if i < STEPS:
                        u = step(dve.tensor_tensor(g.u2[:, :], mean, g.kap2[:, p, now], ALU.mult))
                    if i:
                        nd = step(stt(g.nd[:, :], mean, mean, g.quad[:, STEPS:], ALU.mult, ALU.subtract))
                    if i < STEPS:
                        need(u)
                        step(stt(g.s1[:, :], g.u2[:, :], float(DIM // 4), g.gram_m[:, STEPS, now], ALU.mult, ALU.subtract))
                    if i:
                        need(nd)
                        stt(g.tau[:, :], g.tau[:, :], EPS, g.nd[:, :], ALU.mult, ALU.subtract).then_inc(want_root, 1)
                    if i == STEPS:
                        break
                    step(stt(g.pn[:, :], g.sigh[:, p, now], g.u2[:, :], g.gram_m[:, i, now], ALU.mult, ALU.add))
                    dve.wait_ge(want_root, done(ROOTS, 2 * i - 1))
                    vii = g.gram_b[:, p, i, 2 * STEPS + 1 + i:2 * STEPS + 2 + i]
                    need(step(stt(g.s3[:, :], g.tau[:, :], vii, g.quad[:, now], ALU.mult, ALU.add)))
                    need(step(stt(g.s2[:, :], g.s1[:, :], g.u2[:, :], g.s3[:, :], ALU.mult, ALU.add)))
                    dve.wait_ge(root_done, done(ROOTS, 2 * i - 1))
                    stt(g.cross[:, :], g.pn[:, :], g.rt2[:, :], g.s2[:, :], ALU.mult, ALU.min).then_inc(want_root, 1)
                    lv = step(dve.tensor_tensor(g.lv[:, :], g.lin[:, p, i, :], g.gram_m[:, i, :], ALU.mult))
                    if 1 <= i < STEPS - 1:
                        rest = slice(i + 1, STEPS)
                        lv = step(stt(g.gram_m[:, rest, :], g.coef[:, p, i - 1, rest, :], g.w[:, i - 1:i], g.gram_m[:, rest, :],
                                      ALU.mult, ALU.add))
                    dve.wait_ge(root_done, done(ROOTS, 2 * i))
                    need(lv)
                    w = g.w[:, now]
                    lw = step(stt(g.lw[:, :], g.sqr[:, p, i, :], w, g.lv[:, :], ALU.mult, ALU.add))
                    rows = slice(i + 1, STEPS1, max(1, STEPS - 1 - i))
                    step(stt(g.gram_m[:, rows, :], g.coef[:, p, i, rows, :], w, g.gram_m[:, rows, :], ALU.mult, ALU.add))
                    need(lw)
                    need(step(stt(g.quad[:, :], g.lw[:, :], w, g.quad[:, :], ALU.mult, ALU.add)))
                dve.wait_ge(want_root, done(ROOTS, ROOTS - 1))
                dve.wait_ge(root_done, done(ROOTS, ROOTS - 1))
                need(step(dve.reciprocal(g.rho[:, :], g.rt2[:, :])))
                step(dve.reciprocal(g.itau[:, :], g.tau[:, :]))
                need(step(dve.tensor_scalar(g.nrho[:, :], g.rho[:, :], 2.0, None, ALU.mult)))
                dve.tensor_scalar(g.cf[:, 0:STEPS], g.w[:, :], g.nrho[:, :], None, ALU.mult).then_inc(cf_done, 1)
                need(step(stt(g.cf[:, STEPS:], mean, -1.0, g.nrho[:, :], ALU.mult, ALU.mult)))
                dve.tensor_scalar(g.diag[:, :], ident[0:BATCH, 0:BATCH], g.nrho[:, :], None, ALU.mult).then_inc(cf_done, 1)
                dve.wait_ge(cf_full, done(1, 0))
                need(step(dve.tensor_copy(g.cf_s[:, :], bank_c[0:STEPS1, 256:256 + BATCH])))
                dve.wait_ge(rows_done, done(2, 1))
                dve.tensor_tensor(g.scaled[:, :, :], g.ek_rows[:, p, :, :], g.cf_s[:, :].unsqueeze(2).to_broadcast([STEPS1, BATCH, MEM]),
                                  ALU.mult).then_inc(scaled_rows_done, 1)
                need(step(dve.tensor_tensor(g.m[:, :, :], g.m[:, :, :], bank_c[0:64, 272:272 + BATCH].unsqueeze(2).to_broadcast([64, BATCH, DIM]),
                                            ALU.mult)))
                for h in range(2):
                    dve.wait_ge(n_full, done(2, h))
                    four = g.m[:, 4 * h:4 * h + 4, :]
                    dve.tensor_tensor(four, four, bank_s[0:64, 512 * h:512 * h + 512].rearrange("p (b d) -> p b d", b=4), ALU.add)\
                        .then_inc(m_done, 1)
                return n[0]

            per = 7 + 10 * STEPS + STEPS - 2 + 6
            with dve.Fori(0, NCH // 2) as it:
                for p in range(2):
                    used = chunk(Chunk(it, p), it * (2 * per) + per * p)
                    assert used == per, used
            for c in range(4):
                cols = slice(512 * c, 512 * c + 512)
                dve.wait_ge(fin_pe, 2 * c + 2)
                dve.tensor_tensor(x[:, cols], x[:, cols], bank_r[:, :], ALU.add).then_inc(fin_dve, 1)
                dve.wait_ge(fin_dve, 2 * c + 1)
                dve.tensor_tensor(x[:, cols], x[:, cols], g.x1[:, cols], ALU.add).then_inc(fin_dve, 1)

        block = ctx.enter_context(nc.Block())

        def layer_of(layer, stack):
            return layer + LAYERS * stack

        VALUE_COPIES = (8, 8, 7, 7)

        def roles(b, last):
            nxt = b + 1 if b + 1 < BATCH or not last else None
            return nxt, b >= 0 and (b < BATCH or not last), b - 1 if b >= 1 else None

        @block.sync
        def _(sp):
            for m in range(4):
                sp.sem_inc(v_in[m], 2 * 16 * VALUE_COPIES[m])
            sp.dma_start(x[:, :], xT).then_inc(x_in, 16)
            sp.dma_start(memw[:, :], mem_w).then_inc(memw_in, 16)
            sp.dma_start(const[:, :], consts).then_inc(const_in, 16)
            sp.dma_start(xo[:, :], maskc).then_inc(const_in, 16)
            for stack in range(stacks):
                if stack:
                    mid_sp(sp)
                def project_weights(layer, n, c):
                    if not isinstance(n, int) or n + c:
                        sp.wait_ge(wl_done, n * UNITS + c)
                    sp.dma_start(raw[:, c % 2, :], w_qk[layer, :, c * INNER:(c + 1) * INNER]).then_inc(raw_in[c % 2], 16)
                    if c == 1:
                        if not isinstance(n, int) or n:
                            sp.wait_ge(wvl_done, n)
                        sp.dma_start(wv_next[:, :], w_v[layer]).then_inc(wv_in, 16)
                        if not isinstance(n, int) or n:
                            sp.wait_ge(rots_done, n * 4)
                        sp.dma_start(qk_scales[:, :], smalls[layer, :, 0:4]).then_inc(scales_in, 16)

                def ffn_weights(layer, done):
                    sp.wait_ge(f_full, done(7, -1, 0))
                    sp.dma_start(wo[:, :, :], w_o[layer].rearrange("(c p) n -> p c n", p=128)).then_inc(wo_in, 16)
                    sp.wait_ge(f_full, done(7, -1, 5))
                    sp.dma_start(w1[:, :], w_1[layer]).then_inc(w1_in, 16)
                    sp.wait_ge(f_full, done(7, -1, 6))
                    sp.dma_start(w2[:, 0:2, :], w_2[layer, 0:256, :].rearrange("(c p) n -> p c n", p=128)).then_inc(w2_in, 16)
                    sp.dma_start(w2[0:FFN - 256, 2, :], w_2[layer, 256:FFN, :]).then_inc(w2_in, 16)
                    sp.wait_ge(x_ready, done.x(7))
                    sp.dma_start(small[:, :], smalls[layer, :, 4:]).then_inc(small_in, 16)

                def place_values(b, m, done):
                    j, e = divmod(m, 2)
                    if m == 0:
                        sp.wait_ge(o_full, done(4, b - 2, 3))
                        sp.sem_inc(place_on, 1)
                    sp.wait_ge(v_done, done(4, b, m))
                    for g in range(4):
                        for own in range(2):
                            w = 4 * j + g + 1 - own
                            if w < WINDOWS:
                                rows = slice(64 * e + 32 * own, 64 * e + 32 * own + 32)
                                sp.dma_start(v[rows, b % 2, w, :, :].rearrange("p c d -> p (c d)"),
                                             v_rows_s[32 * g:32 * g + 32, m % 2, :]).then_inc(v_in[m], 16)

                def slots(layer, streams, last):
                    done = Count(layer, stack)
                    nth = layer_of(layer, stack)
                    for b in streams:
                        nxt, _, _ = roles(b, last)
                        for i in range(4):
                            if b == 1 and i == 0:
                                ffn_weights(layer, done)
                            if not last and (b, i) in NEXT_WEIGHTS:
                                project_weights(layer + 1, nth + 1, NEXT_WEIGHTS[b, i])
                            if nxt is not None:
                                place_values(nxt, i, done)

                NEXT_WEIGHTS = {(2, 0): 0, (2, 1): 1, (6, 1): 2, (6, 2): 3}
                sp.wait_ge(setup, 6 + 3 * stack)
                for c in range(UNITS):
                    project_weights(0, LAYERS * stack, c)
                slots(0, range(-1, 1), False)
                if layers > 1:
                    with sp.Fori(0, layers - 1) as layer:
                        slots(layer, range(1, BATCH + 1), False)
                slots(layers - 1, range(1, BATCH + 1), True)
            for c in range(4):
                cols = slice(512 * c, 512 * c + 512)
                if c:
                    sp.wait_ge(end_dve, c)
                sp.dma_start(xo[:, :], (x2 if stacks > 1 else xT)[:, cols]).then_inc(xo_in, 16)
            for c in range(4):
                cols = slice(512 * c, 512 * c + 512)
                sp.wait_ge(end_dve, c + 1)
                sp.dma_start(out[:, cols], x[:, cols]).then_inc(out_done, 16)
            sp.wait_ge(out_done, 64)

        @block.tensor
        def _(pe):
            for s, per in ((c_full, 8), (r_full, 8), (nsum_full, 4), (rqt_full, 4), (spread_full, 4), (v_full, 4),
                           (f_full, 7), (s_full, 4), (pt_full, 4), (o_full, 4), (ot_full, 4)):
                pe.sem_inc(s, 2 * per)
            pe.wait_ge(const_in, 32)
            pe.wait_ge(setup, 6)

            def project(done, b, u, kind, which, bank, full):
                p = b % 2
                n = 2 * u + kind
                if kind == 0:
                    if which == 0:
                        pe.wait_ge(rq_done, done(4, b, u - 1))
                    else:
                        pe.wait_ge(kn_done, done(4, b, u - 1))
                else:
                    pe.wait_ge(prod_done, done(16, b, 4 * u + which))
                    if which == 0:
                        pe.wait_ge(sq_done, done(8, b, 2 * u))
                for a in range(2):
                    at = u * INNER + ((2 * kind + which) * 2 + a) * 128
                    w = slice(at, at + 128)
                    dst = bank[:, a * SEQ:(a + 1) * SEQ]
                    pe.matmul(dst, wh[:, w], xh[:, p, :], start=True, stop=False)
                    pe.matmul(dst, wl[:, w], xh[:, p, :], start=False, stop=False)
                    last = pe.matmul(dst, wh[:, w], xl[:, p, :], start=False, stop=True)
                last.then_inc(full, 1)

            def values(done, b, m, before):
                p, (j, e) = b % 2, divmod(m, 2)
                before()
                t, w = slice(128 * j, 128 * j + 128), slice(512 * e, 512 * e + 512)
                pe.matmul(bank_m[:, :], xh[:, p, t], wvh[:, w], start=True, stop=False)
                pe.matmul(bank_m[:, :], xh[:, p, t], wvl[:, w], start=False, stop=False)
                pe.matmul(bank_m[:, :], xl[:, p, t], wvh[:, w], start=False, stop=True).then_inc(v_full, 1)

            def norms(done, b, u):
                pe.wait_ge(sq_done, done(8, b, 2 * u + 1))
                pe.wait_ge(o_done, done(4, b - 1, u - 1))
                for a in range(2):
                    for kind in range(2):
                        last = pe.matmul(bank_o[32 * kind:32 * kind + 32, SEQ:2 * SEQ], head_sum[:, a, :], sq[:, kind, a, :],
                                         start=(a == 0), stop=(a == 1))
                last.then_inc(nsum_full, 1)

            def spread_norms(done, b, u):
                pe.wait_ge(rnorml_done, done(4, b, u))
                pe.wait_ge(prod_done, done(16, b, 4 * u + 3))
                for a in range(2):
                    pe.matmul(bank_r[:, a * SEQ:(a + 1) * SEQ], spread[32:64, a, :], rnormh[32:64, :], start=True, stop=False)
                    last = pe.matmul(bank_r[:, a * SEQ:(a + 1) * SEQ], spread[32:64, a, :], rnorml[32:64, :],
                                     start=False, stop=True)
                last.then_inc(spread_full, 1)
                for j in range(2):
                    last = pe.transpose(bank_c[:, SEQ + 32 * j:SEQ + 32 * j + 32], rnorm[0:32, 128 * j:128 * j + 128],
                                        ident[0:32, 0:32])
                last.then_inc(rqt_full, 1)

            def scores(done, b, i):
                p, j, oct_ = b % 2, i // 2, i % 2
                half = 256 * (i % 2)
                pe.wait_ge(kn_done, done(4, b, 2 * oct_ + 1))
                pe.wait_ge(qadd_done, done(4, b, 2 * oct_ + 1))
                pe.wait_ge(diff_done, done(4, b, i - 2))
                for e in range(2):
                    pe.matmul(bank_s[:, 512 * e + half:512 * e + half + 256], identb[:, :], mask[:, j, :],
                              start=True, stop=False, skip_group_check=True)
                for c in range(4):
                    for g in range(4):
                        t = 128 * j + WINDOW * g
                        lo = 0 if t == 0 else WINDOW
                        n = WINDOW + lo
                        for e in range(2):
                            rows = slice(64 * e, 64 * e + 64)
                            s0 = 512 * e + half + 64 * c + WINDOW - lo
                            last = pe.matmul(bank_s[32 * g:32 * g + 32, s0:s0 + n],
                                             q[rows, p, 4 * oct_ + c, t:t + WINDOW], k[rows, p, 4 * oct_ + c, t - lo:t + WINDOW],
                                             start=False, stop=True, skip_group_check=True)
                last.then_inc(s_full, 1)

            def probs_T(done, b, i):
                pe.wait_ge(prob_done, done(4, b, i))
                pe.wait_ge(ot_done, done(4, b, i - 1))
                for c in range(4):
                    last = pe.transpose(bank_t[:, 128 * c:128 * c + 128], prob[:, i % 2, 128 * c:128 * c + 128], ident)
                last.then_inc(pt_full, 1)

            def attend(done, b, i, beside):
                p, j, oct_ = b % 2, i // 2, i % 2
                pe.wait_ge(pt_done, done(4, b, i))
                for m in (2 * j, 2 * j + 1):
                    pe.wait_ge(v_in[m], done(16 * VALUE_COPIES[m], b, 16 * VALUE_COPIES[m] - 1))
                pe.wait_ge(o_done, done(4, b, i - 1))
                if beside:
                    pe.wait_ge(clamp_done, done(4, b + 1, i))
                pe.sem_inc(attend_on, 1)
                for c in range(4):
                    for g in range(4):
                        for e in range(2):
                            rows = slice(64 * e, 64 * e + 64)
                            last = pe.matmul(bank_o[32 * g:32 * g + 32, 512 * e + 64 * c:512 * e + 64 * c + 64],
                                             probT[rows, i % 2, 128 * c + 32 * g:128 * c + 32 * g + 32],
                                             v[rows, p, 4 * j + g, 4 * oct_ + c, :], start=True, stop=True)
                last.then_inc(o_full, 1)

            def out_T(done, b, i):
                pe.wait_ge(o_done, done(4, b, i))
                pe.wait_ge(pt_done, done(4, b, i))
                for c in range(4):
                    last = pe.transpose(bank_t[:, 128 * c:128 * c + 128], o[:, i % 2, 128 * c:128 * c + 128], ident)
                last.then_inc(ot_full, 1)

            def ffn(done, b, step, before):
                before()
                if step == 0:
                    pe.wait_ge(ot_done, done(4, b, 3))
                    for c in range(PAIRS):
                        last = pe.matmul(bank_m[:, 0:SEQ], wo[:, c, :], oT[:, c, :], start=(c == 0), stop=(c == PAIRS - 1))
                elif step in (1, 2):
                    if step == 1:
                        pe.wait_ge(fs_done, done(2, b, 1))
                    else:
                        pe.wait_ge(fq_done, done(1, b, 0))
                    last = pe.matmul(bank_m[:, 0:SEQ], mean_w, (fs if step == 1 else fq)[:, :], start=True, stop=True)
                elif step < 6:
                    c0, n = CHUNKS[step - 3]
                    if step == 3:
                        pe.wait_ge(fn_done, done(1, b, 0))
                    pe.matmul(bank_m[0:n, 0:SEQ], w1[:, c0:c0 + n], fn[:, :], start=True, stop=True)
                    last = pe.matmul(bank_m[0:n, SEQ:2 * SEQ], w1[:, FFN + c0:FFN + c0 + n], fn[:, :], start=True, stop=True)
                else:
                    pe.wait_ge(hid_done, done(3, b, 2))
                    for c, (_, n) in enumerate(CHUNKS):
                        last = pe.matmul(bank_m[:, 0:SEQ], w2[0:n, c, :], hid[0:n, c, :], start=(c == 0), stop=(c == 2))
                last.then_inc(f_full, 1)

            for stack in range(stacks):
                if stack:
                    mid_pe(pe)
                for c in range(TOKENS // 512):
                    for h in range(2):
                        if h == 0:
                            if c:
                                pe.wait_ge(pro_dve, (stack * 4 + c) * 2)
                            elif stack:
                                pe.wait_ge(fin_dve, 8)
                            else:
                                pe.wait_ge(x_in, 16)
                            src = x[:, c * 512:c * 512 + 512]
                        else:
                            pe.wait_ge(pro_act, (stack * 4 + c) * 3 + 1)
                            src = sq[:, 0, :, :].rearrange("p a t -> p (a t)")
                        pe.matmul(bank_c[:, :], mean_w, src, start=True, stop=True).then_inc(pro_pe, 1)
                pe.wait_ge(pro_dve, (stack * 4 + 4) * 2)
                pe.wait_ge(setup, 6 + 3 * stack)
                def slots(layer, streams, last):
                    done = Count(layer, stack)
                    nth = layer_of(layer, stack)
                    used = {"m": None}

                    def m_free():
                        if used["m"] is None:
                            pe.wait_ge(x_ready, done.x(7))
                            if streams[0] == 1:
                                pe.wait_ge(v_done, done(4, 1, 3))
                        else:
                            pe.wait_ge(*used["m"])

                    def V(b, w):
                        values(done, b, w, m_free)
                        used["m"] = (v_done, done(4, b, w))

                    def F(b, step):
                        ffn(done, b, step, m_free)
                        used["m"] = [(x1_done, done(1, b, 0)), (fc_done, done(1, b, 0)), (fl_done, done(1, b, 0)),
                                     (hid_done, done(3, b, 0)), (hid_done, done(3, b, 1)), (hid_done, done(3, b, 2)),
                                     (x_ready, done.x(b + BATCH))][step]

                    for b in streams:
                        nxt, att, prev = roles(b, last)
                        for i in range(4):
                            if att:
                                scores(done, b, i)
                            if prev is not None and i > 0:
                                if prev == 0 and i == 2:
                                    pe.wait_ge(w1_in, nth * 16 + 16)
                                F(prev, [None, 1, 3, 5][i])
                            if nxt is not None:
                                if i == 0:
                                    pe.wait_ge(xl_done, done(1, nxt, 0))
                                if nxt % BATCH == 0:
                                    pe.wait_ge(wl_done, (nth + nxt // BATCH) * UNITS + i + 2)
                                project(done, nxt, i, 0, 0, bank_c, c_full)
                                project(done, nxt, i, 0, 1, bank_r, r_full)
                            if att and i:
                                out_T(done, b, i - 1)
                            elif i == 0 and prev is not None:
                                out_T(done, prev, 3)
                            if nxt is not None:
                                if nxt % BATCH == 0 and i == 0:
                                    pe.wait_ge(wvl_done, nth + nxt // BATCH + 1)
                                V(nxt, i)
                                project(done, nxt, i, 1, 0, bank_c, c_full)
                                project(done, nxt, i, 1, 1, bank_r, r_full)
                            if att:
                                probs_T(done, b, i)
                            if nxt is not None:
                                norms(done, nxt, i)
                            if prev is not None:
                                if prev == 0 and i == 0:
                                    pe.wait_ge(wo_in, nth * 16 + 16)
                                if prev == 0 and i == 3:
                                    pe.wait_ge(w2_in, nth * 32 + 32)
                                F(prev, [0, 2, 4, 6][i])
                            if att:
                                attend(done, b, i, nxt is not None)
                            if nxt is not None:
                                spread_norms(done, nxt, i)

                slots(0, range(-1, 1), False)
                if layers > 1:
                    with pe.Fori(0, layers - 1) as layer:
                        slots(layer, range(1, BATCH + 1), False)
                slots(layers - 1, range(1, BATCH + 1), True)

        @block.scalar
        def _(act):
            for s, per in ((sq_done, 8), (log_done, 4), (rnorm_done, 4), (v_done, 4), (prob_done, 4), (pt_done, 4),
                           (ot_done, 4), (xh_done, 1), (fq_done, 1), (fl_done, 1), (fr_done, 1), (gelu_done, 3)):
                act.sem_inc(s, 2 * per)
            act.wait_ge(const_in, 32)
            act.preload_act_table_set("natural_log_exp_and_others")
            for stack in range(stacks):
                if stack:
                    mid_act(act)
                for c in range(TOKENS // 512):
                    at = stack * 4 + c
                    flat = sq[:, 0, :, :].rearrange("p a t -> p (a t)")
                    act.wait_ge(pro_dve, at * 2 + 1)
                    act.activation(flat, x[:, c * 512:c * 512 + 512], ACT.Square).then_inc(pro_act, 1)
                    act.wait_ge(pro_pe, at * 2 + 2)
                    act.activation(diff[:, 0, :], bank_c[:, :], ACT.Ln, bias=eps).then_inc(pro_act, 1)
                    act.wait_ge(pro_act, at * 3 + 2)
                    act.activation(diff[:, 1, :], diff[:, 0, :], ACT.Exp, scale=-0.5).then_inc(pro_act, 1)

                def slots(layer, streams, last):
                    done = Count(layer, stack)
                    nth = layer_of(layer, stack)

                    def to_xh(b):
                        act.wait_ge(xs_done, done(2, b, 1))
                        act.wait_ge(r_full, done(8, b - 2, 7))
                        act.wait_ge(v_full, done(4, b - 2, 3))
                        act.activation(xh[:, b % 2, :], xs[:, b % 2, :], ACT.Copy).then_inc(xh_done, 1)

                    def square(b, u, kind):
                        act.wait_ge(c_full, done(8, b, 2 * u + kind))
                        if kind == 0:
                            act.wait_ge(nsum_full, done(4, b, u - 1))
                        act.activation(sq[:, kind, :, :], bank_c[:, :].rearrange("p (a t) -> p a t", a=2), ACT.Square)\
                            .then_inc(sq_done, 1)

                    def values_out(b, m):
                        act.wait_ge(v_full, done(4, b, m))
                        used, of = (m - 2, b) if m >= 2 else (m + 2, b - 1)
                        act.wait_ge(v_in[used], done(16 * VALUE_COPIES[used], of, 16 * VALUE_COPIES[used] - 1))
                        act.activation(v_rows_s[:, m % 2, :], bank_m[:, :], ACT.Copy).then_inc(v_done, 1)

                    def rnorms(b, u):
                        act.wait_ge(clamp_done, done(4, b, u))
                        act.activation(nlog[:, :], nsum[:, :], ACT.Ln).then_inc(log_done, 1)
                        act.wait_ge(log_done, done(4, b, u))
                        act.wait_ge(rqt_full, done(4, b, u - 1))
                        act.activation(rnormh[:, :], nlog[:, :], ACT.Exp, bias=norm_bias, scale=-0.5)
                        act.activation(rnorm[:, :], nlog[:, :], ACT.Exp, bias=norm_bias, scale=-0.5).then_inc(rnorm_done, 1)

                    def exps(b, i):
                        act.wait_ge(scaled_done, done(4, b, i))
                        act.wait_ge(pt_full, done(4, b, i - 2))
                        act.wait_ge(sum_done, done(4, b, i - 2))
                        act.activation(prob[:, i % 2, :], diff[:, i % 2, :], ACT.Exp).then_inc(prob_done, 1)

                    def probs_out(b, i):
                        act.wait_ge(pt_full, done(4, b, i))
                        act.wait_ge(o_full, done(4, b, i - 2))
                        act.activation(probT[:, i % 2, :], bank_t[:, :], ACT.Copy).then_inc(pt_done, 1)

                    def out_out(b, i):
                        act.wait_ge(ot_full, done(4, b, i))
                        act.wait_ge(f_full, done(7, b - 1, 0))
                        j, oct_ = i // 2, i % 2
                        act.activation(oT[:, 4 * oct_:4 * oct_ + 4, 128 * j:128 * j + 128],
                                       bank_t[:, :].rearrange("p (c t) -> p c t", c=4), ACT.Copy).then_inc(ot_done, 1)

                    def gelu(b, c):
                        n = CHUNKS[c][1]
                        act.wait_ge(f_full, done(7, b, 3 + c))
                        act.wait_ge(hid_done, done(3, b, c - 1))
                        act.activation(gl[0:n, :], bank_m[0:n, SEQ:2 * SEQ], ACT.Gelu, bias=small[0:n, 6 + c:7 + c])\
                            .then_inc(gelu_done, 1)

                    def fvar(b):
                        act.wait_ge(f_full, done(7, b, 2))
                        act.wait_ge(fm_done, done(1, b - 1, 0))
                        act.activation(fl[:, :], bank_m[:, 0:SEQ], ACT.Ln, bias=eps).then_inc(fl_done, 1)
                        act.wait_ge(fl_done, done(1, b, 0))
                        act.activation(fr[:, :], fl[:, :], ACT.Exp, scale=-0.5).then_inc(fr_done, 1)

                    def split(n, u, stream, i):
                        act.wait_ge(raw_in[u % 2], n * 32 + 16 * (u // 2 + 1))
                        act.wait_ge(r_full, done(8, stream, 2 * i + 1))
                        act.activation(wh[:, u * INNER:(u + 1) * INNER], raw[:, u % 2, :], ACT.Copy).then_inc(wh_done, 1)

                    def next_wv(n, stream):
                        act.wait_ge(wv_in, n * 16 + 16)
                        act.wait_ge(v_full, done(4, stream, 3))
                        act.activation(wvh[:, :], wv_next[:, :], ACT.Copy).then_inc(wvh_done, 1)

                    if streams[0] < 0:
                        to_xh(0)
                        for u in range(UNITS):
                            split(nth, u, -1, 3)
                            if u == 0:
                                next_wv(nth, -1)
                    for b in streams:
                        nxt, att, prev = roles(b, last)
                        for i in range(4):
                            if prev is not None and i == 2:
                                gelu(prev, 0)
                            if nxt is not None:
                                square(nxt, i, 0)
                            if prev is not None and i >= 2:
                                act.preload_act_table_set("natural_log_exp_and_others")
                            if prev is not None and i == 1:
                                act.wait_ge(fc_done, done(1, prev, 0))
                                act.wait_ge(f_full, done(7, prev - 1, 2))
                                act.activation(fq[:, :], fc[:, :], ACT.Square).then_inc(fq_done, 1)
                            if att and i:
                                out_out(b, i - 1)
                            elif i == 0 and prev is not None:
                                out_out(prev, 3)
                            if att:
                                exps(b, i)
                            if nxt is not None:
                                square(nxt, i, 1)
                                values_out(nxt, i)
                            if att:
                                probs_out(b, i)
                            if nxt is not None:
                                rnorms(nxt, i)
                            if prev is not None:
                                if i == 1:
                                    fvar(prev)
                                if i == 2:
                                    gelu(prev, 1)
                                    gelu(prev, 2)
                            if i == 1 and (b + 2 < BATCH or not last):
                                to_xh(b + 2)
                            if nxt == BATCH - 1 and not last:
                                split(nth + 1, i, nxt, i)
                                if i == 3:
                                    next_wv(nth + 1, nxt)

                slots(0, range(-1, 1), False)
                if layers > 1:
                    with act.Fori(0, layers - 1) as layer:
                        slots(layer, range(1, BATCH + 1), False)
                slots(layers - 1, range(1, BATCH + 1), True)

        @block.vector
        def _(dve):
            for s, per in ((prod_done, 16), (clamp_done, 4), (rnorml_done, 4), (rq_done, 4), (kn_done, 4), (max_done, 4), (diff_done, 4),
                           (sum_done, 4), (rsum_done, 4), (o_done, 4), (xl_done, 1), (x1_done, 1), (fs_done, 2), (fc_done, 1),
                           (fm_done, 1), (fn_done, 1), (hid_done, 3), (xs_done, 2)):
                dve.sem_inc(s, 2 * per)
            dve.sem_inc(wl_done, 1)
            dve.wait_ge(const_in, 32)
            dve.tensor_copy(identb[:, :], ident).then_inc(setup, 1)
            dve.tensor_copy(mask[:, :, :], xo[:, :].rearrange("p (f n) -> p f n", f=2)).then_inc(setup, 1)
            dve.tensor_copy(spread_r[:, :], const[0:64, SPREAD0:BIAS0]).then_inc(setup, 1)
            dve.wait_ge(setup, 3)
            for stack in range(stacks):
                if stack:
                    mid_dve(dve)
                    dve.wait_ge(coef_done, NCH + 3)
                    dve.wait_ge(rows_done, 2 * (NCH + 3))
                    dve.wait_ge(gram_done, NCH + 3)
                    dve.wait_ge(gram_in, 16 * BATCH * (NCH + 1))
                    dve.wait_ge(fin_act, 4)
                dve.memset(xs[:, :, 0:1], 0.0).then_inc(setup, 1)
                dve.memset(fs[:, 0:1], 0.0).then_inc(setup, 1)
                dve.memset(v[:, :, 0, :, :], 0.0).then_inc(setup, 1)
                dve.wait_ge(setup, 6 + 3 * stack)
                for c in range(TOKENS // 512):
                    at = stack * 4 + c
                    xc = x[:, c * 512:c * 512 + 512]
                    dve.wait_ge(pro_pe, at * 2 + 1)
                    if c == 0:
                        dve.wait_ge(*((x2_out, 16) if stack else (x_in, 16)))
                    dve.tensor_tensor(xc, xc, bank_c[:, :], ALU.subtract).then_inc(pro_dve, 1)
                    dve.wait_ge(pro_act, at * 3 + 3)
                    dve.wait_ge(pro_dve, at * 2 + 1)
                    dve.tensor_tensor(xc, xc, diff[:, 1, :], ALU.mult).then_inc(pro_dve, 1)
                dve.wait_ge(pro_dve, (stack * 4 + 4) * 2)
                dve.sem_inc(x_ready, BATCH)

                def slots(layer, streams, last):
                    done = Count(layer, stack)
                    nth = layer_of(layer, stack)

                    def shift_tokens(b):
                        dve.wait_ge(x_ready, done.x(b))
                        dve.wait_ge(xl_done, done(1, b - 2, 0))
                        p, at = b % 2, SEQ * (b % BATCH)
                        dve.tensor_copy(xs[0:64, p, :], x[0:64, at:at + SEQ]).then_inc(xs_done, 1)
                        dve.tensor_copy(xs[64:128, p, 1:], x[64:128, at:at + SEQ - 1]).then_inc(xs_done, 1)

                    def to_xl(b):
                        dve.wait_ge(xh_done, done(1, b, 0))
                        dve.tensor_tensor(xl[:, b % 2, :], xs[:, b % 2, :], xh[:, b % 2, :].bitcast(F32), ALU.subtract)\
                            .then_inc(xl_done, 1)

                    def product(b, u, kind, which):
                        bank, full = ((bank_c, c_full), (bank_r, r_full))[which]
                        dve.wait_ge(full, done(8, b, 2 * u + kind))
                        if which == 0:
                            dve.wait_ge(sq_done, done(8, b, 2 * u + kind))
                            dve.wait_ge((qadd_done, kadd_done)[kind], done(4, b, u - 1))
                        table = rots[:, 2 * kind + which, :].unsqueeze(1).to_broadcast([128, 2, SEQ])
                        dve.tensor_tensor(prod[:, 2 * kind + which, :, :], bank[:, :].rearrange("p (a t) -> p a t", a=2),
                                          table, ALU.mult).then_inc(prod_done, 1)

                    def clamp(b, u):
                        dve.wait_ge(nsum_full, done(4, b, u))
                        dve.wait_ge(rnorm_done, done(4, b, u - 1))
                        dve.tensor_scalar(nsum[:, :], bank_o[0:64, SEQ:2 * SEQ], NORM_FLOOR, LN_SHIFT, ALU.max, ALU.mult)\
                            .then_inc(clamp_done, 1)

                    def low_norms(b, u):
                        dve.wait_ge(rnorm_done, done(4, b, u))
                        dve.tensor_tensor(rnorml[:, :], rnorm[:, :], rnormh[:, :].bitcast(F32), ALU.subtract).then_inc(rnorml_done, 1)

                    def norms_out(b, u):
                        dve.wait_ge(rqt_full, done(4, b, u))
                        if u == 0:
                            dve.wait_ge(scaled_done, done(4, b - 2, 3))
                        dve.tensor_copy(rq[:, b % 2, :, 4 * u:4 * u + 4],
                                        bank_c[:, SEQ:SEQ + 64].rearrange("p (j h) -> p j h", j=2)[:, :, 0:4])\
                            .then_inc(rq_done, 1)
                        dve.wait_ge(spread_full, done(4, b, u))
                        dve.wait_ge(kadd_done, done(4, b, u))
                        ku = k[:, b % 2, 2 * u:2 * u + 2, :]
                        dve.tensor_tensor(ku, ku, bank_r[:, :].rearrange("p (a t) -> p a t", a=2), ALU.mult)\
                            .then_inc(kn_done, 1)

                    def shift_scores(b, i):
                        half = 256 * (i % 2)
                        s4 = bank_s[:, :].rearrange("p (e n) -> p e n", e=2)[:, :, half:half + 256]\
                            .rearrange("p e (c k) -> p e c k", c=4)
                        m = smax[:, i % 2, :].rearrange("p (e c) -> p e c", e=2)
                        dve.wait_ge(s_full, done(4, b, i))
                        dve.tensor_reduce(m, s4, AX.X, ALU.max).then_inc(max_done, 1)
                        dve.wait_ge(max_done, done(4, b, i))
                        dve.wait_ge(prob_done, done(4, b, i - 2))
                        d = diff[:, i % 2, :].rearrange("p (c e k) -> p e c k", c=4, e=2)
                        for e in range(2):
                            last = dve.tensor_tensor(d[:, e, :, :], s4[:, e, :, :],
                                                     m[:, e, :].unsqueeze(2).to_broadcast([128, 4, 64]), ALU.subtract)
                        last.then_inc(diff_done, 1)

                    def prob_sums(b, i):
                        dve.wait_ge(prob_done, done(4, b, i))
                        dve.tensor_reduce(psum[:, i % 2, :], prob[:, i % 2, :].rearrange("p (h k) -> p h k", k=64), AX.X, ALU.add)\
                            .then_inc(sum_done, 1)
                        dve.wait_ge(sum_done, done(4, b, i))
                        dve.wait_ge(o_done, done(4, b, i - 1))
                        dve.reciprocal(rsum[:, :], psum[:, i % 2, :]).then_inc(rsum_done, 1)

                    def out_norm(b, i):
                        dve.wait_ge(o_full, done(4, b, i))
                        o4 = bank_o[:, :].rearrange("p (e n) -> p e n", e=2)[:, :, 0:256].rearrange("p e (c d) -> p e c d", c=4)
                        r = rsum[:, :].rearrange("p (c e) -> p e c", e=2)
                        dve.wait_ge(rsum_done, done(4, b, i))
                        dve.wait_ge(ot_full, done(4, b, i - 2))
                        dst = o[:, i % 2, :].rearrange("p (c e d) -> p e c d", c=4, e=2)
                        for e in range(2):
                            last = dve.tensor_tensor(dst[:, e, :, :], o4[:, e, :, :],
                                                     r[:, e, :].unsqueeze(2).to_broadcast([128, 4, HEAD_DIM]), ALU.mult)
                        last.then_inc(o_done, 1)

                    def ffn(b, step):
                        xb = x[:, SEQ * b:SEQ * b + SEQ]
                        dve.wait_ge(f_full, done(7, b, step))
                        if step == 0:
                            dve.tensor_tensor(xb, xb, bank_m[:, 0:SEQ], ALU.add).then_inc(x1_done, 1)
                            dve.wait_ge(x1_done, done(1, b, 0))
                            dve.tensor_copy(fs[0:64, :], xb[0:64, :]).then_inc(fs_done, 1)
                            dve.tensor_copy(fs[64:128, 1:], xb[64:128, 0:SEQ - 1]).then_inc(fs_done, 1)
                        elif step == 1:
                            dve.wait_ge(fs_done, done(2, b, 1))
                            dve.tensor_tensor(fc[:, :], fs[:, :], bank_m[:, 0:SEQ], ALU.subtract).then_inc(fc_done, 1)
                        elif step == 2:
                            dve.wait_ge(fr_done, done(1, b, 0))
                            dve.tensor_tensor(fc[:, :], fc[:, :], fr[:, :], ALU.mult).then_inc(fm_done, 1)
                            dve.wait_ge(fm_done, done(1, b, 0))
                            if b == 0:
                                dve.wait_ge(small_in, nth * 16 + 16)
                            dve.tensor_scalar(fn[:, :], fc[:, :], small[:, 0:1], small[:, 1:2], ALU.mult, ALU.add)\
                                .then_inc(fn_done, 1)
                        elif step < 6:
                            c, n = step - 3, CHUNKS[step - 3][1]
                            dve.wait_ge(gelu_done, done(3, b, c))
                            dve.scalar_tensor_tensor(out=hid[0:n, c, :], in0=bank_m[0:n, 0:SEQ], scalar=small[0:n, 3 + c:4 + c],
                                                     in1=gl[0:n, :], op0=ALU.add, op1=ALU.mult).then_inc(hid_done, 1)
                        else:
                            dve.scalar_tensor_tensor(out=xb, in0=bank_m[:, 0:SEQ], scalar=small[:, 2:3], in1=xb,
                                                     op0=ALU.add, op1=ALU.add).then_inc(x_ready, 1)

                    def split(n, u):
                        dve.wait_ge(wh_done, n * UNITS + u + 1)
                        sec = slice(u * INNER, (u + 1) * INNER)
                        dve.tensor_tensor(wl[:, sec], raw[:, u % 2, :], wh[:, sec].bitcast(F32), ALU.subtract)\
                            .then_inc(wl_done, 1)

                    def split_wv(n):
                        dve.wait_ge(wvh_done, n + 1)
                        dve.tensor_tensor(wvl[:, :], wv_next[:, :], wvh[:, :].bitcast(F32), ALU.subtract).then_inc(wvl_done, 1)

                    def rotary(n):
                        dve.wait_ge(scales_in, n * 16 + 16)
                        for t in range(4):
                            dve.tensor_scalar(rots[:, t, :], rot[:, t, :], qk_scales[:, t:t + 1], None, ALU.mult)\
                                .then_inc(rots_done, 1)
                        dve.wait_ge(rots_done, n * 4 + 4)

                    if streams[0] < 0:
                        shift_tokens(0)
                        to_xl(0)
                        split(nth, 0)
                        split_wv(nth)
                        rotary(nth)
                        for u in range(1, UNITS):
                            split(nth, u)
                    for b in streams:
                        nxt, att, prev = roles(b, last)
                        for i in range(4):
                            if i == 0 and (b + 2 < BATCH or not last):
                                shift_tokens(b + 2)
                            if att:
                                shift_scores(b, i)
                            if prev is not None and i > 0:
                                ffn(prev, [None, 1, 3, 5][i])
                            if nxt is not None:
                                for kind in range(2):
                                    for which in range(2):
                                        product(nxt, i, kind, which)
                                clamp(nxt, i)
                            if att:
                                prob_sums(b, i)
                            if nxt is not None:
                                low_norms(nxt, i)
                            if prev is not None:
                                ffn(prev, [0, 2, 4, 6][i])
                            if att:
                                out_norm(b, i)
                            if nxt is not None:
                                norms_out(nxt, i)
                            if i == 1 and (b + 2 < BATCH or not last):
                                to_xl(b + 2)
                            if nxt == BATCH - 1 and not last:
                                split(nth + 1, i)
                                if i == 3:
                                    split_wv(nth + 1)
                                    rotary(nth + 1)

                slots(0, range(-1, 1), False)
                if layers > 1:
                    with dve.Fori(0, layers - 1) as layer:
                        slots(layer, range(1, BATCH + 1), False)
                slots(layers - 1, range(1, BATCH + 1), True)

            dve.wait_ge(x_ready, BATCH * (LAYERS + 1) * (stacks - 1) + BATCH * (layers + 1))
            for c in range(4):
                cols = slice(512 * c, 512 * c + 512)
                dve.wait_ge(xo_in, 16 * c + 16)
                dve.scalar_tensor_tensor(out=x[:, cols], in0=x[:, cols], scalar=0.5, in1=xo[:, :], op0=ALU.mult, op1=ALU.add)\
                    .then_inc(end_dve, 1)

        @block.gpsimd
        def _(pool):
            for s, per in ((scaled_done, 4), (qadd_done, 4), (kadd_done, 4)):
                pool.sem_inc(s, 2 * per)
            pool.wait_ge(setup, 6)
            for stack in range(stacks):
                if stack:
                    mid_pool(pool)
                def slots(layer, streams, last):
                    done = Count(layer, stack)

                    def scale_scores(b, i):
                        pool.wait_ge(diff_done, done(4, b, i))
                        if i < 2:
                            pool.wait_ge(rq_done, done(4, b, 3))
                        d = diff[:, i % 2, :].rearrange("p (h k) -> p h k", k=64)
                        r = rq[:, b % 2, i // 2, 8 * (i % 2):8 * (i % 2) + 8].unsqueeze(2).to_broadcast([128, 8, 64])
                        pool.tensor_tensor(d, d, r, ALU.mult).then_inc(scaled_done, 1)

                    def rotate(b, u, kind):
                        pool.wait_ge(prod_done, done(16, b, 4 * u + 2 * kind + 1))
                        pool.wait_ge(s_full, done(4, b - 2, 3))
                        dst = (q, k)[kind][:, b % 2, 2 * u:2 * u + 2, :]
                        pool.tensor_tensor(dst, prod[:, 2 * kind, :, :], prod[:, 2 * kind + 1, :, :], ALU.add)\
                            .then_inc((qadd_done, kadd_done)[kind], 1)

                    for b in streams:
                        nxt, att, _ = roles(b, last)
                        for i in range(4):
                            if att:
                                scale_scores(b, i)
                            if nxt is not None:
                                rotate(nxt, i, 0)
                                rotate(nxt, i, 1)

                slots(0, range(-1, 1), False)
                if layers > 1:
                    with pool.Fori(0, layers - 1) as layer:
                        slots(layer, range(1, BATCH + 1), False)
                slots(layers - 1, range(1, BATCH + 1), True)
    return nc


def layout(inputs):
    a = {n: np.asarray(v) for n, v in inputs.items()}
    half = HEAD_DIM // 2
    wqkv = a["L0_ffn_Wqkv"]

    def swapped(w, axis):
        parts = np.split(w, w.shape[axis] // half, axis)
        return np.concatenate([parts[i ^ 1] for i in range(len(parts))], axis)

    wq, wk, wv = np.split(wqkv, 3, -1)
    wv = wv.reshape(LAYERS, DIM, PAIRS, 2, HEAD_DIM).transpose(0, 1, 3, 2, 4).reshape(LAYERS, DIM, INNER)
    w_qk = np.stack([w.reshape(LAYERS, DIM, UNITS, -1) for w in (wq, swapped(wq, 2), wk, swapped(wk, 2))], 3)
    w_qk = w_qk.reshape(LAYERS, DIM, 4 * INNER)
    qs, ks = a["L0_ffn_q_scale"], a["L0_ffn_k_scale"]
    cols = [np.concatenate([c, c], 1) for c in (qs, swapped(qs, 1), ks, swapped(ks, 1))]
    cols += [a["L0_ffn_ln_g"], a["L0_ffn_ln_b"], a["L0_ffn_b2"]]
    b1 = a["L0_ffn_b1"]
    for base in (0, FFN):
        for c0, n in CHUNKS:
            part = np.zeros((LAYERS, 128), np.float32)
            part[:, :n] = b1[:, base + c0:base + c0 + n]
            cols.append(part)
    smalls = np.stack(cols, -1)
    consts, mask = tables()
    return {
        "xT": a["L0_attn_x"].transpose(2, 0, 1).reshape(DIM, TOKENS), "w_qk": w_qk, "w_v": wv,
        "w_o": a["L0_ffn_Wo"], "w_1": a["L0_ffn_W1"], "w_2": a["L0_ffn_W2"], "smalls": smalls,
        "mem_w": np.concatenate([a["L0_attn_Wk"].T, a["L0_attn_Wq"].T, a["L0_attn_Wv"].T, a["L0_attn_Wout"].T,
                                 a["L0_attn_norm_weight"][:, None], np.pad(a["L0_attn_eta"], (0, DIM - MEM))[:, None]], 1),
        "consts": consts, "maskc": mask,
    }


def kernel(**inputs):
    import concourse.bacc as bacc
    from concourse.bass_utils import run_bass_kernel_spmd

    nc = bacc.Bacc("TRN2", target_bir_lowering=False, num_devices=1)
    arrays, args = {}, []
    for name, a in layout(inputs).items():
        a = np.ascontiguousarray(a)
        arrays[f"in_{name}"] = a
        args.append(nc.dram_tensor(f"in_{name}", a.shape, mybir.dt.from_np(a.dtype), kind="ExternalInput").ap())
    args.append(nc.dram_tensor("out", (DIM, TOKENS), F32, kind="ExternalOutput").ap())
    build(nc, *args)
    r = run_bass_kernel_spmd(nc, [arrays], core_ids=[0])
    return r.results[0]["out"].reshape(DIM, BATCH, SEQ).transpose(1, 2, 0)
```
